# Optimizing a Trainium2 kernel written in Bass

```python
import numpy as np
import jax
import jax.numpy as jnp

def _softmax(x, axis=-1):
    return jax.nn.softmax(x, axis=axis)

def _gelu(x):
    return jax.nn.gelu(x, approximate=True)

def _silu(x):
    return jax.nn.silu(x)

def _sigmoid(x):
    return jax.nn.sigmoid(x)

def _layernorm(x, axis=-1, eps=1e-05):
    m = jnp.mean(x, axis=axis, keepdims=True)
    v = jnp.var(x, axis=axis, keepdims=True)
    return (x - m) / jnp.sqrt(v + eps)

def _scatter_add(tgt, idx, src, axis=0):
    return tgt.at[idx].add(src)

def _segment_sum(src, seg, n):
    return jax.ops.segment_sum(src, seg, n)
kernel_name = 'mk_prb_d1_jaxref_r8_46eddd'

def setup_inputs(seed: int=0):
    np.random.seed(seed)
    _w = jnp.asarray

    def _L0_attn_setup():
        import jax, jax.numpy as jnp
        import numpy as np
        NUM_HEADS = 16
        EMBED_DIM = 128

        def _linear_attention(x, Wq, bq, Wk, bk, Wv, bv, Wo, bo):
            B, S, D = x.shape
            H = NUM_HEADS
            hd = D // H
            v = (x @ Wv + bv).reshape(B, S, H, hd)
            q = (x @ Wq + bq).reshape(B, S, H, hd)
            k = (x @ Wk + bk).reshape(B, S, H, hd)
            q = jax.nn.elu(q) + 1.0
            k = jax.nn.elu(k) + 1.0
            qT = q.transpose(1, 0, 2, 3)
            kT = k.transpose(1, 0, 2, 3)
            vT = v.transpose(1, 0, 2, 3)
            s0 = jnp.zeros((B, H, hd, hd), dtype=x.dtype)
            z0 = jnp.zeros((B, H, hd), dtype=x.dtype)

            def step(carry, qkv):
                s, z = carry
                q_i, k_i, v_i = qkv
                s = s + jnp.einsum('bhd,bhm->bhdm', k_i, v_i)
                z = z + k_i
                qs = jnp.einsum('bhd,bhdm->bhm', q_i, s)
                qz = jnp.einsum('bhd,bhd->bh', q_i, z)[..., None]
                return ((s, z), qs / (qz + 1e-06))
            (_, _), values = jax.lax.scan(step, (s0, z0), (qT, kT, vT))
            values = values.transpose(1, 0, 2, 3).reshape(B, S, D)
            return values @ Wo + bo
        key = jax.random.key(seed)
        ks = jax.random.split(key, 6)
        B, S, D = (4, 256, EMBED_DIM)
        sc = 1.0 / np.sqrt(D)
        return {'x': jax.random.normal(ks[0], (B, S, D), dtype=jnp.float32), 'mask': jnp.ones((B, S), dtype=jnp.int32), 'Wq': jax.random.normal(ks[1], (D, D), dtype=jnp.float32) * sc, 'bq': jnp.zeros((D,), dtype=jnp.float32), 'Wk': jax.random.normal(ks[2], (D, D), dtype=jnp.float32) * sc, 'bk': jnp.zeros((D,), dtype=jnp.float32), 'Wv': jax.random.normal(ks[3], (D, D), dtype=jnp.float32) * sc, 'bv': jnp.zeros((D,), dtype=jnp.float32), 'Wo': jax.random.normal(ks[4], (D, D), dtype=jnp.float32) * sc, 'bo': jnp.zeros((D,), dtype=jnp.float32)}
    _L0_attn_in = _L0_attn_setup()

    def _L0_ffn_setup():
        import jax, jax.numpy as jnp
        import numpy as np
        HIDDEN = 128
        HEAD_DIM = 64
        N_EXPERTS = 16
        MIN_EXPERTS = 2
        B, T = (4, 256)

        def _normalize(x, axis):
            n = jnp.sqrt(jnp.sum(x * x, axis=axis, keepdims=True))
            return x / jnp.maximum(n, 1e-12)

        def _ste(x):
            hard = jax.lax.stop_gradient((x > 0).astype(x.dtype))
            return hard + x - jax.lax.stop_gradient(x)

        def _gating(hidden_states, sim_matrix, gates):
            b, t, c = hidden_states.shape
            flat = hidden_states.reshape(b * t, c)
            logits = _normalize(flat, -1) @ _normalize(sim_matrix, 0) - jax.nn.sigmoid(gates)
            gated = jax.nn.relu(logits)
            mask = _ste(gated)
            inactive = jnp.sum(mask, axis=1) == 0
            _, fb_idx = jax.lax.top_k(logits, MIN_EXPERTS)
            fb = jnp.zeros_like(mask).at[jnp.arange(b * t)[:, None], fb_idx].set(1.0)
            fb_applied = inactive[:, None] & (fb > 0)
            mask = jnp.where(fb_applied, 1.0, mask)
            masked_logits = jnp.where(mask > 0, gated, -jnp.inf)
            return jax.nn.softmax(masked_logits, axis=-1).reshape(b, t, -1)
        key = jax.random.key(seed)
        ks = jax.random.split(key, 6)
        xav_qkv = float(np.sqrt(6.0 / (HIDDEN + HEAD_DIM)))
        return {'hidden_states': jax.random.normal(ks[0], (B, T, HIDDEN), dtype=jnp.float32), 'sim_matrix': jax.random.normal(ks[1], (HIDDEN, N_EXPERTS), dtype=jnp.float32), 'gates': jnp.zeros((N_EXPERTS,), dtype=jnp.float32), 'q_proj': jax.random.uniform(ks[2], (N_EXPERTS, HIDDEN, HEAD_DIM), jnp.float32, -xav_qkv, xav_qkv), 'k_proj': jax.random.uniform(ks[3], (N_EXPERTS, HIDDEN, HEAD_DIM), jnp.float32, -xav_qkv, xav_qkv), 'v_proj': jax.random.uniform(ks[4], (N_EXPERTS, HIDDEN, HEAD_DIM), jnp.float32, -xav_qkv, xav_qkv), 'o_proj': jax.random.uniform(ks[5], (N_EXPERTS, HEAD_DIM, HIDDEN), jnp.float32, -xav_qkv, xav_qkv)}
    _L0_ffn_in = _L0_ffn_setup()
    _d = {'L0_attn_x': _L0_attn_in['x'], 'L0_attn_mask': _L0_attn_in['mask'], 'L0_attn_Wq': _L0_attn_in['Wq'], 'L0_attn_bq': _L0_attn_in['bq'], 'L0_attn_Wk': _L0_attn_in['Wk'], 'L0_attn_bk': _L0_attn_in['bk'], 'L0_attn_Wv': _L0_attn_in['Wv'], 'L0_attn_bv': _L0_attn_in['bv'], 'L0_attn_Wo': _L0_attn_in['Wo'], 'L0_attn_bo': _L0_attn_in['bo'], 'L0_ffn_sim_matrix': _L0_ffn_in['sim_matrix'], 'L0_ffn_gates': _L0_ffn_in['gates'], 'L0_ffn_q_proj': _L0_ffn_in['q_proj'], 'L0_ffn_k_proj': _L0_ffn_in['k_proj'], 'L0_ffn_v_proj': _L0_ffn_in['v_proj'], 'L0_ffn_o_proj': _L0_ffn_in['o_proj']}
    _x0 = _d['L0_attn_x']
    _d['L0_attn_x'] = jax.random.normal(jax.random.fold_in(jax.random.key(seed), 1), (8, 512, 128), dtype=_x0.dtype)
    del _x0
    return _d

def reference(L0_attn_x, L0_attn_mask, L0_attn_Wq, L0_attn_bq, L0_attn_Wk, L0_attn_bk, L0_attn_Wv, L0_attn_bv, L0_attn_Wo, L0_attn_bo, L0_ffn_sim_matrix, L0_ffn_gates, L0_ffn_q_proj, L0_ffn_k_proj, L0_ffn_v_proj, L0_ffn_o_proj):

    def _L0_attn_ref(x, mask, Wq, bq, Wk, bk, Wv, bv, Wo, bo):
        import jax, jax.numpy as jnp
        import numpy as np
        NUM_HEADS = 16
        EMBED_DIM = 128

        def _linear_attention(x, Wq, bq, Wk, bk, Wv, bv, Wo, bo):
            B, S, D = x.shape
            H = NUM_HEADS
            hd = D // H
            v = (x @ Wv + bv).reshape(B, S, H, hd)
            q = (x @ Wq + bq).reshape(B, S, H, hd)
            k = (x @ Wk + bk).reshape(B, S, H, hd)
            q = jax.nn.elu(q) + 1.0
            k = jax.nn.elu(k) + 1.0
            qT = q.transpose(1, 0, 2, 3)
            kT = k.transpose(1, 0, 2, 3)
            vT = v.transpose(1, 0, 2, 3)
            s0 = jnp.zeros((B, H, hd, hd), dtype=x.dtype)
            z0 = jnp.zeros((B, H, hd), dtype=x.dtype)

            def step(carry, qkv):
                s, z = carry
                q_i, k_i, v_i = qkv
                s = s + jnp.einsum('bhd,bhm->bhdm', k_i, v_i)
                z = z + k_i
                qs = jnp.einsum('bhd,bhdm->bhm', q_i, s)
                qz = jnp.einsum('bhd,bhd->bh', q_i, z)[..., None]
                return ((s, z), qs / (qz + 1e-06))
            (_, _), values = jax.lax.scan(step, (s0, z0), (qT, kT, vT))
            values = values.transpose(1, 0, 2, 3).reshape(B, S, D)
            return values @ Wo + bo
        return _linear_attention(x, Wq, bq, Wk, bk, Wv, bv, Wo, bo)

    def _L0_ffn_ref(hidden_states, sim_matrix, gates, q_proj, k_proj, v_proj, o_proj):
        import jax, jax.numpy as jnp
        import numpy as np
        HIDDEN = 128
        HEAD_DIM = 64
        N_EXPERTS = 16
        MIN_EXPERTS = 2
        B, T = (4, 256)

        def _normalize(x, axis):
            n = jnp.sqrt(jnp.sum(x * x, axis=axis, keepdims=True))
            return x / jnp.maximum(n, 1e-12)

        def _ste(x):
            hard = jax.lax.stop_gradient((x > 0).astype(x.dtype))
            return hard + x - jax.lax.stop_gradient(x)

        def _gating(hidden_states, sim_matrix, gates):
            b, t, c = hidden_states.shape
            flat = hidden_states.reshape(b * t, c)
            logits = _normalize(flat, -1) @ _normalize(sim_matrix, 0) - jax.nn.sigmoid(gates)
            gated = jax.nn.relu(logits)
            mask = _ste(gated)
            inactive = jnp.sum(mask, axis=1) == 0
            _, fb_idx = jax.lax.top_k(logits, MIN_EXPERTS)
            fb = jnp.zeros_like(mask).at[jnp.arange(b * t)[:, None], fb_idx].set(1.0)
            fb_applied = inactive[:, None] & (fb > 0)
            mask = jnp.where(fb_applied, 1.0, mask)
            masked_logits = jnp.where(mask > 0, gated, -jnp.inf)
            return jax.nn.softmax(masked_logits, axis=-1).reshape(b, t, -1)
        b, t, c = hidden_states.shape
        rw = _gating(hidden_states, sim_matrix, gates)
        q = jnp.einsum('bte,bted->btd', rw, jnp.einsum('btc,ecd->bted', hidden_states, q_proj))
        k = jnp.einsum('bte,bted->btd', rw, jnp.einsum('btc,ecd->bted', hidden_states, k_proj))
        v = jnp.einsum('bte,bted->btd', rw, jnp.einsum('btc,ecd->bted', hidden_states, v_proj))
        scale = 1.0 / jnp.sqrt(jnp.asarray(HEAD_DIM, dtype=q.dtype))
        scores = jnp.einsum('bqd,bkd->bqk', q, k) * scale
        causal = jnp.tril(jnp.ones((t, t), dtype=bool))
        scores = jnp.where(causal, scores, -jnp.inf)
        attn = jnp.einsum('bqk,bkd->bqd', jax.nn.softmax(scores, axis=-1), v)
        mixed = attn[:, :, None, :] * rw[..., None]
        return jnp.einsum('bted,edc->btc', mixed, o_proj)
    x = L0_attn_x
    xn = _layernorm(x, axis=-1)
    x = x + _L0_attn_ref(xn, L0_attn_mask, L0_attn_Wq, L0_attn_bq, L0_attn_Wk, L0_attn_bk, L0_attn_Wv, L0_attn_bv, L0_attn_Wo, L0_attn_bo) + _L0_ffn_ref(xn, L0_ffn_sim_matrix, L0_ffn_gates, L0_ffn_q_proj, L0_ffn_k_proj, L0_ffn_v_proj, L0_ffn_o_proj)
    return x

_drawn_inputs = setup_inputs


def setup_inputs(seed=0):
    import zlib

    import numpy as np

    out = dict(_drawn_inputs(seed))
    spreads = {'L0_attn_bq': (0.0, 0.8),
     'L0_attn_bk': (0.0, 0.8),
     'L0_attn_bv': (0.0, 0.1),
     'L0_attn_bo': (0.0, 0.1),
     'L0_ffn_gates': (0.0, 0.1)}
    factors = {'L0_attn_Wq': 2.892}
    for name, (base, spread) in spreads.items():
        noise = np.random.default_rng([zlib.crc32(name.encode()), seed]).standard_normal(out[name].shape)
        drawn = base * np.exp(spread * noise) if base else spread * noise
        out[name] = jnp.asarray(drawn.astype(out[name].dtype))
    for name, factor in factors.items():
        out[name] = (out[name] * factor).astype(out[name].dtype)
    return out
```

```python
from contextlib import ExitStack

import concourse.bass as bass
from concourse import mybir

F32 = mybir.dt.float32
F16 = mybir.dt.float16
BF16 = mybir.dt.bfloat16
ALU = mybir.AluOpType
ACT = mybir.ActivationFunctionType
AX = mybir.AxisListType

P = 128
BIG = 1.0e30
LN_EPS = 1e-5
NORM_EPS = 1e-12
DEN_EPS = 1e-6


def due(count):
    return not isinstance(count, int) or count > 0


class Chain:

    def __init__(self, engine, semaphore, per_pass, index):
        self.engine, self.semaphore, self.n = engine, semaphore, 0
        self.per_pass, self.index = per_pass, index

    def step(self, instruction):
        self.n += 1
        instruction.then_inc(self.semaphore, 1)
        self.engine.wait_ge(self.semaphore, self.index * self.per_pass + self.n)

    def end(self):
        assert self.n == self.per_pass, self.n


def build(nc, x_in, wq_in, bq_in, wk_in, bk_in, wv_in, bv_in, wo_in, bo_in,
          sim_in, gates_in, eq_in, ek_in, ev_in, eo_in, out):
    B, T, D = x_in.shape
    E, _, HD = eq_in.shape
    NT = T // P
    C = 32
    CT = P // C
    NC = T // C
    H, M = 16, 8
    G = 4
    S4 = H // G
    M1 = M + 1
    VW = H * M1
    W3 = 3 * HD
    PAIRS = E // 2
    YN = NT * PAIRS
    TMP = 4
    DB = 3
    ND = NC // DB
    SCALE = float(HD) ** -0.5
    assert D == P and H * M == D and NC == 16 and ND * DB == NC - 1

    ctx = ExitStack()
    with ctx:
        def sb(name, shape, dt=F32):
            return ctx.enter_context(nc.sbuf_tensor(name, shape, dt))

        def sem(name):
            return ctx.enter_context(nc.semaphore(name))

        ident = sb("ident", [P, P])
        ident_bf = sb("ident_bf", [P, P], BF16)
        ones = sb("ones", [P, P])
        future_bf = sb("future_bf", [P, P], BF16)
        past = sb("past", [P, C])
        place_mask = sb("place_mask", [P, S4])
        block_mask = sb("block_mask", [P, VW])
        pair_sel = sb("pair_sel", [P, PAIRS, 2, HD], BF16)
        rank = sb("rank", [P, E])
        half = sb("half", [P, NT])
        neg_half = sb("neg_half", [P, NT])
        half16 = sb("half16", [P, E])
        stage = sb("stage", [P, E, W3])
        w3_hi = sb("w3_hi", [P, E, W3], F16)
        w3_lo = sb("w3_lo", [P, E, W3], F16)
        lin_w = sb("lin_w", [P, 3, D])
        lin_hi = sb("lin_hi", [P, 3, D], F16)
        lin_lo = sb("lin_lo", [P, 3, D], F16)
        wv_raw = sb("wv_raw", [P, D])
        bv_raw = sb("bv_raw", [P, D])
        bv_row = sb("bv_row", [P, D])
        bo_row = sb("bo_row", [P, D])
        bqk = sb("bqk", [P, 2])
        wo = sb("wo", [P, D])
        eo = sb("eo", [P, PAIRS, D])
        sim = sb("sim", [P, E])
        sim_sq = sb("sim_sq", [P, E])
        sim_r = sb("sim_r", [P, 4, E])
        sim_hi = sb("sim_hi", [P, E], F16)
        sim_lo = sb("sim_lo", [P, E], F16)
        gates = sb("gates", [P, E])
        sig = sb("sig", [P, 3, E])
        sigmoid = sb("sigmoid", [P, E])

        x = sb("x", [P, NT, D])
        stats = sb("stats", [P, NT, 6])
        mv = sb("mv", [P, NT, 2])
        wait_pad = sb("wait_pad", [P, 1])
        var_eps = sb("var_eps", [P, NT])
        rstd = sb("rstd", [P, NT])
        nrm = sb("nrm", [P, 5, NT])
        xn = sb("xn", [P, NT, D])
        xt_hi = sb("xt_hi", [P, T], F16)
        xt_lo = sb("xt_lo", [P, T], F16)
        logit = sb("logit", [P, 2, NT, E])
        gmax = sb("gmax", [P, 8, NT])
        gate = sb("gate", [P, 12, NT, E])
        gexp = sb("gexp", [P, NT, E])
        rw = sb("rw", [P, NT, E])
        rw_prev = sb("rw_prev", [P, NT, E])

        acc_v = sb("acc_v", [P, NT, 2, W3])
        acc_s = sb("acc_s", [P, NT, 2, W3])
        y_tmp = sb("y_tmp", [P, TMP, 2, W3])
        y_sum = sb("y_sum", [P, NT, 2, W3])
        qk = sb("qk", [P, NT, 2 * HD])
        v_dup = sb("v_dup", [P, NT, 2, HD])

        elu_e = sb("elu_e", [P, 2, T])
        elu_r = sb("elu_r", [P, 2, T])
        q_t = sb("q_t", [P, T])
        k_t = sb("k_t", [P, T])
        q_groups = sb("q_groups", [P, NC, G, C])
        k_places = sb("k_places", [P, NC, S4, C])
        k_chunks = sb("k_chunks", [P, CT, NT, D])
        v_ones = sb("v_ones", [P, NT, S4, G, M1])
        v_blocks = sb("v_blocks", [P, NC, S4, G, M1])
        scores = sb("scores", [P, NT, CT * G * C])
        d_state = sb("d_state", [P, NC - 1, VW])
        state = sb("state", [P, NC, VW])
        den = sb("den", [P, 2, 2, 2 * H])
        val = sb("val", [P, NT, D])
        val_t = sb("val_t", [P, T])

        qk_t = sb("qk_t", [P, T])
        k_zero = sb("k_zero", [P, T])
        smax = sb("smax", [P, NT])
        neg_max = sb("neg_max", [P, NT])
        ssum = sb("ssum", [P, NT])
        srec = sb("srec", [P, NT])
        probs = sb("probs", [P, NT, T])
        probs_t = sb("probs_t", [P, NT, T])
        attn_t = sb("attn_t", [P, T])
        rwo = sb("rwo", [P, 2, NT, E])
        rwo_parts = sb("rwo_parts", [P, NT, P], BF16)
        rwo_t = sb("rwo_t", [P, T], BF16)
        mixed = sb("mixed", [P, 2, T])
        x_res = sb("x_res", [P, NT, D])
        res = sb("res", [P, NT, D])
        out_sb = sb("out_sb", [P, NT, D])

        y_ps = [ctx.enter_context(nc.psum_tensor(f"y_ps{n}", [P, 2, 256], F32)) for n in range(2)]
        out_ps = ctx.enter_context(nc.psum_tensor("out_ps", [P, NT, D], F32))
        g_ps = [ctx.enter_context(nc.psum_tensor(f"g_ps{n}", [P, 512], F32)) for n in range(5)]
        y_view = [t[:, :, :].rearrange("p a b -> p (a b)")[:, 0:2 * W3] for t in y_ps]

        w_loaded = sem("w_loaded")
        const_step = sem("const_step")
        const_ready = sem("const_ready")
        dve_const_step = sem("dve_const_step")
        dve_const_ready = sem("dve_const_ready")
        act_const_ready = sem("act_const_ready")
        sim_norm = sem("sim_norm")
        sim_norm_read = sem("sim_norm_read")
        sim_root = sem("sim_root")
        gates_exp = sem("gates_exp")

        x_loaded = sem("x_loaded")
        stats_step = sem("stats_step")
        var_ready = sem("var_ready")
        rstd_ready = sem("rstd_ready")
        norm_sq_ready = sem("norm_sq_ready")
        norm_ready = sem("norm_ready")
        xn_ready = sem("xn_ready")
        xt_ready = sem("xt_ready")
        xt_hi_ready = sem("xt_hi_ready")
        xt_lo_ready = sem("xt_lo_ready")
        logits_ready = sem("logits_ready")
        logits_read = sem("logits_read")
        gate_step = sem("gate_step")
        gate_arg_ready = sem("gate_arg_ready")
        gate_exp_ready = sem("gate_exp_ready")
        rw_ready = sem("rw_ready")

        y_ready = [sem("y_ready_v"), sem("y_ready_s")]
        y_added_v = sem("y_added_v")
        y_scaled_s = sem("y_scaled_s")
        y_added_s = sem("y_added_s")
        y_summed = sem("y_summed")
        qkv_ready = sem("qkv_ready")

        proj_ready = sem("proj_ready")
        elu_parts = sem("elu_parts")
        q_ready = sem("q_ready")
        k_ready = sem("k_ready")
        v_ready = sem("v_ready")
        v_spread = sem("v_spread")
        q_groups_ready = sem("q_groups_ready")
        k_places_ready = sem("k_places_ready")
        k_tok_ready = sem("k_tok_ready")
        k_chunks_ready = sem("k_chunks_ready")
        score_ready = sem("score_ready")
        score_masked = sem("score_masked")
        d_ready = sem("d_ready")
        d_masked = sem("d_masked")
        state_ready = sem("state_ready")
        la_ready = sem("la_ready")
        den_step = sem("den_step")
        val_ready = sem("val_ready")
        val_tr_ready = sem("val_tr_ready")
        val_t_ready = sem("val_t_ready")

        wo_added = sem("wo_added")
        qk_tr_ready = sem("qk_tr_ready")
        qk_t_ready = sem("qk_t_ready")
        k_zero_ready = sem("k_zero_ready")
        s_ready = sem("s_ready")
        max_ready = sem("max_ready")
        neg_max_ready = sem("neg_max_ready")
        probs_ready = sem("probs_ready")
        probs_tr_ready = sem("probs_tr_ready")
        probs_t_ready = sem("probs_t_ready")
        attn_ready = sem("attn_ready")
        attn_t_ready = sem("attn_t_ready")
        rwo_step = sem("rwo_step")
        rwo_ready = sem("rwo_ready")
        rwo_tr_ready = sem("rwo_tr_ready")
        rwo_t_ready = sem("rwo_t_ready")
        rwb_ready = sem("rwb_ready")
        mixed_ready = sem("mixed_ready")
        pair_added = sem("pair_added")
        xr_loaded = sem("xr_loaded")
        res_ready = sem("res_ready")
        out_ready = sem("out_ready")
        out_stored = sem("out_stored")

        WEIGHTS = 11 + 3

        def passes(body):
            def run(engine):
                body(0, False, True)
                body(1, True, True)
                with engine.Fori(2, B - 1) as b:
                    body(b, True, True)
                body(B - 1, True, False)
            return run

        def x_of(b):
            return x_in[b].rearrange("(i p) d -> p i d", p=P)

        def out_of(b):
            return out[b].rearrange("(i p) d -> p i d", p=P)

        block = ctx.enter_context(nc.Block())

        @block.sync
        def _(sp):
            sp.dma_start(x[:, :, :], x_of(0)).then_inc(x_loaded, 16)
            sp.dma_start(sim[:, :], sim_in).then_inc(w_loaded, 16)
            sp.dma_start(gates[:, :], gates_in.partition_broadcast(P)).then_inc(w_loaded, 16)
            sp.dma_start(lin_w[:, 0, :], wq_in).then_inc(w_loaded, 16)
            sp.dma_start(lin_w[:, 1, :], wk_in).then_inc(w_loaded, 16)
            sp.dma_start(wv_raw[:, :], wv_in).then_inc(w_loaded, 16)
            sp.dma_start(bqk[:, 0:1], bq_in.rearrange("(p a) -> p a", a=1)).then_inc(w_loaded, 16)
            sp.dma_start(bqk[:, 1:2], bk_in.rearrange("(p a) -> p a", a=1)).then_inc(w_loaded, 16)
            sp.dma_start(bv_raw[:, :], bv_in.partition_broadcast(P)).then_inc(w_loaded, 16)
            sp.dma_start(bo_row[:, :], bo_in.partition_broadcast(P)).then_inc(w_loaded, 16)
            sp.dma_start(wo[:, :], wo_in).then_inc(w_loaded, 16)
            for n, w in enumerate((eq_in, ek_in, ev_in)):
                sp.dma_start(stage[:, :, n * HD:(n + 1) * HD],
                             w.rearrange("e c d -> c e d")).then_inc(w_loaded, 16)
            sp.dma_start(eo[:, :, :], eo_in.rearrange("(p u) d c -> (u d) p c", u=2))\
              .then_inc(w_loaded, 16)

            def body(b, attn, norm):
                if norm:
                    sp.wait_ge(xn_ready, (b + 1) * NT)
                    sp.dma_start(x[:, :, :], x_of(b + 1)).then_inc(x_loaded, 16)
                if attn:
                    if due(b - 1):
                        sp.wait_ge(res_ready, b - 1)
                    sp.dma_start(x_res[:, :, :], x_of(b - 1)).then_inc(xr_loaded, 16)
                if due(b * NT):
                    sp.wait_ge(la_ready, b * NT)
                sp.wait_ge(v_ready, b + 1)
                for s in range(S4):
                    for j in range(CT):
                        sp.dma_start(v_blocks[C * s:C * s + C, j:NC:CT, s, :, :],
                                     v_ones[C * j:C * j + C, :, s, :, :]).then_inc(v_spread, 16)
                if attn:
                    if due(b):
                        sp.wait_ge(out_ready, b)
                    sp.dma_start(out_of(b - 1), out_sb[:, :, :]).then_inc(out_stored, 16)

            passes(body)(sp)
            sp.wait_ge(res_ready, B - 1)
            sp.dma_start(x_res[:, :, :], x_of(B - 1)).then_inc(xr_loaded, 16)
            sp.wait_ge(out_ready, B)
            sp.dma_start(out_of(B - 1), out_sb[:, :, :]).then_inc(out_stored, 16)
            sp.wait_ge(out_stored, 16 * B)

        @block.gpsimd
        def _(pool):
            g = nc.gpsimd
            consts = Chain(pool, const_step, 40, 0)
            for t in (ident, future_bf, pair_sel, q_groups, k_chunks, v_blocks, state,
                      k_zero, rwo_parts):
                consts.step(g.memset(t[tuple(slice(None) for _ in t.shape)], 0.0))
            for t in (ones, past, place_mask, block_mask, v_ones):
                consts.step(g.memset(t[tuple(slice(None) for _ in t.shape)], 1.0))
            consts.step(g.memset(half[:, :], 0.5))
            consts.step(g.memset(half16[:, :], 0.5))
            consts.step(g.memset(neg_half[:, :], -0.5))
            for e in range(E):
                last = g.memset(rank[:, e:e + 1], float(E - e))
            consts.step(last)
            consts.step(g.affine_select(out=ident[:, :], in_=ident[:, :], compare_op=ALU.not_equal,
                                        fill=1.0, base=0, pattern=[[-1, P]], channel_multiplier=1))
            consts.step(g.tensor_copy(ident_bf[:, :], ident[:, :]))
            consts.step(g.affine_select(out=future_bf[:, :], in_=future_bf[:, :], compare_op=ALU.is_ge,
                                        fill=-BIG, base=0, pattern=[[-1, P]], channel_multiplier=1))
            for s in range(S4):
                rows = slice(C * s, C * s + C)
                consts.step(g.affine_select(out=past[rows, :], in_=past[rows, :], compare_op=ALU.is_ge,
                                            fill=0.0, base=0, pattern=[[1, C]], channel_multiplier=-1))
                consts.step(g.affine_select(out=place_mask[rows, :], in_=place_mask[rows, :],
                                            compare_op=ALU.is_ge, fill=0.0, base=0,
                                            pattern=[[-M, S4]], channel_multiplier=1))
                consts.step(g.affine_select(out=place_mask[rows, :], in_=place_mask[rows, :],
                                            compare_op=ALU.is_ge, fill=0.0, base=M - 1,
                                            pattern=[[M, S4]], channel_multiplier=-1))
            view = block_mask[:, :].rearrange("p (s g m) -> p s g m", s=S4, g=G)
            consts.step(g.affine_select(out=view, in_=view, compare_op=ALU.is_ge, fill=0.0, base=0,
                                        pattern=[[-M, S4], [-M * S4, G], [0, M1]], channel_multiplier=1))
            consts.step(g.affine_select(out=view, in_=view, compare_op=ALU.is_ge, fill=0.0, base=M - 1,
                                        pattern=[[M, S4], [M * S4, G], [0, M1]], channel_multiplier=-1))
            for part in range(3):
                consts.step(g.affine_select(out=pair_sel[:, :, :, :], in_=pair_sel[:, :, :, :],
                                            compare_op=ALU.not_equal, fill=1.0, base=-E * part,
                                            pattern=[[-2, PAIRS], [-1, 2], [0, HD]], channel_multiplier=1))
            g.memset(y_sum[:, 0, 0, 0:1], 0.0).then_inc(const_ready, 1)
            pool.wait_ge(sim_norm_read, 1)
            g.tensor_tensor(sim_r[:, 1, :], sim_r[:, 0, :], half16[:, :], ALU.pow).then_inc(sim_root, 1)

            def norm_powers(n):
                pool.wait_ge(var_ready, n + 1)
                if due(n * NT):
                    pool.wait_ge(xn_ready, n * NT)
                g.tensor_tensor(rstd[:, :], var_eps[:, :], neg_half[:, :], ALU.pow).then_inc(rstd_ready, 1)
                pool.wait_ge(norm_sq_ready, n + 1)
                g.tensor_tensor(nrm[:, 2, :], nrm[:, 1, :], half[:, :], ALU.pow).then_inc(norm_ready, 1)

            def residual(a):
                pool.wait_ge(xr_loaded, (a + 1) * 16)
                if due(a):
                    pool.wait_ge(out_ready, a)
                pool.wait_ge(w_loaded, 16 * WEIGHTS)
                g.tensor_tensor(res[:, :, :], x_res[:, :, :],
                                bo_row[:, :].unsqueeze(1).broadcast_to([P, NT, D]), ALU.add)\
                 .then_inc(res_ready, 1)

            ADDS = 3

            def y_add(b, first, last):
                for n in range(first, last):
                    i, p = n // PAIRS, n % PAIRS
                    if p % 2 == 0 or p == 1:
                        continue
                    count = i * ADDS + (p - 3) // 2
                    pool.wait_ge(y_scaled_s, (b * NT * (PAIRS // 2) + i * (PAIRS // 2) + p // 2 + 1) * 2)
                    if due(b * NT * ADDS + count):
                        pool.wait_ge(y_added_s, b * NT * ADDS + count)
                    g.tensor_tensor(acc_s[:, i, :, :], acc_s[:, i, :, :],
                                    y_tmp[:, count % TMP, :, :], ALU.add).then_inc(y_added_s, 1)

            def y_finish(b, i):
                pool.wait_ge(y_added_s, b * NT * ADDS + (i + 1) * ADDS)
                pool.wait_ge(y_added_v, (b * NT + i + 1) * PAIRS)
                if due((b * NT) * 2):
                    pool.wait_ge(qkv_ready, (b * NT) * 2)
                g.tensor_tensor(y_sum[:, i, :, :], acc_v[:, i, :, :], acc_s[:, i, :, :], ALU.add)\
                 .then_inc(y_summed, 1)
                pool.wait_ge(y_summed, b * NT + i + 1)
                if due(b):
                    pool.wait_ge(attn_ready, b)
                if due(b):
                    pool.wait_ge(qk_tr_ready, b)
                g.tensor_tensor(qk[:, i, :], y_sum[:, i, 0, 0:2 * HD], y_sum[:, i, 1, 0:2 * HD], ALU.add)\
                 .then_inc(qkv_ready, 1)
                g.tensor_tensor(v_dup[:, i, :, :],
                                y_sum[:, i, 0, 2 * HD:W3].unsqueeze(1).broadcast_to([P, 2, HD]),
                                y_sum[:, i, 1, 2 * HD:W3].unsqueeze(1).broadcast_to([P, 2, HD]), ALU.add)\
                 .then_inc(qkv_ready, 1)

            def state_add(b, first, last):
                for c in range(first, last):
                    pool.wait_ge(d_masked, b * ND + c // DB + 1)
                    if c == 0:
                        if due(b * NT):
                            pool.wait_ge(la_ready, b * NT)
                    else:
                        if due(b * (NC - 1) + c):
                            pool.wait_ge(state_ready, b * (NC - 1) + c)
                    g.tensor_tensor(state[:, c + 1, :], state[:, c, :], d_state[:, c, :], ALU.add)\
                     .then_inc(state_ready, 1)

            norm_powers(0)

            def body(b, attn, norm):
                if attn:
                    residual(b - 1)
                y_add(b, 0, 12)
                state_add(b, 0, 6)
                y_add(b, 12, 14)
                state_add(b, 6, 12)
                y_add(b, 14, 18)
                state_add(b, 12, 15)
                if norm:
                    norm_powers(b + 1)
                y_add(b, 18, 24)
                y_finish(b, 0)
                y_add(b, 24, 26)
                y_finish(b, 1)
                y_add(b, 26, 28)
                y_finish(b, 2)
                y_add(b, 28, 32)
                y_finish(b, 3)

            passes(body)(pool)
            residual(B - 1)

        @block.scalar
        def _(act):
            a_ = nc.scalar
            act.wait_ge(w_loaded, 16 * WEIGHTS)
            a_.activation(sig[:, 0, :], gates[:, :], ACT.Exp, scale=-1.0).then_inc(gates_exp, 1)
            a_.activation(w3_hi[:, :, :], stage[:, :, :], ACT.Copy).then_inc(act_const_ready, 1)

            def xt_high(n):
                act.wait_ge(xt_ready, n + 1)
                if due(n * YN // 2):
                    act.wait_ge(y_ready[0], n * YN // 2)
                if due(n * YN // 2):
                    act.wait_ge(y_ready[1], n * YN // 2)
                if due(n):
                    act.wait_ge(logits_ready, n)
                a_.activation(xt_hi[:, :], g_ps[4][:, :], ACT.Copy).then_inc(xt_hi_ready, 1)

            def gate_exp(n):
                act.wait_ge(gate_arg_ready, n + 1)
                a_.activation(gexp[:, :, :], gate[:, 10, :, :], ACT.Exp).then_inc(gate_exp_ready, 1)

            def y_scale(b, first, last):
                for n in range(first, last):
                    i, p = n // PAIRS, n % PAIRS
                    if p % 2 == 0:
                        continue
                    act.wait_ge(rw_ready, b + 1)
                    act.wait_ge(y_ready[1], b * YN // 2 + n // 2 + 1)
                    count = i * 3 + (p - 3) // 2
                    if p == 1:
                        if due((b - 1) * NT + i + 1):
                            act.wait_ge(y_summed, (b - 1) * NT + i + 1)
                    else:
                        if due(b * NT * 3 + count - TMP + 1):
                            act.wait_ge(y_added_s, b * NT * 3 + count - TMP + 1)
                    for u in range(2):
                        dst = acc_s[:, i, u, :] if p == 1 else y_tmp[:, count % TMP, u, :]
                        a_.activation(dst, y_view[1][:, u * W3:(u + 1) * W3], ACT.Copy,
                                      scale=rw[:, i, 2 * p + u:2 * p + u + 1]).then_inc(y_scaled_s, 1)

            def elu_pieces(b):
                for n in range(2):
                    act.wait_ge(proj_ready, b * 3 + n + 1)
                    if due(b):
                        act.wait_ge((q_ready, k_ready)[n], b)
                    a_.activation(elu_e[:, n, :], g_ps[2 + n][:, :], ACT.Exp, bias=bqk[:, n:n + 1])\
                      .then_inc(elu_parts, 1)
                    a_.activation(elu_r[:, n, :], g_ps[2 + n][:, :], ACT.Relu, bias=bqk[:, n:n + 1])\
                      .then_inc(elu_parts, 1)

            def group_q(b):
                act.wait_ge(q_ready, b + 1)
                if due(b * NT):
                    act.wait_ge(score_ready, b * NT)
                act.wait_ge(const_ready, 1)
                for g in range(G):
                    rows = slice(C * g, C * g + C)
                    a_.activation(q_groups[rows, :, g, :],
                                  q_t[rows, :].rearrange("p (c t) -> p c t", t=C), ACT.Copy)\
                      .then_inc(q_groups_ready, 1)

            def chunk_k(b):
                act.wait_ge(k_tok_ready, b + 1)
                if due(b * ND):
                    act.wait_ge(d_ready, b * ND)
                for j in range(CT):
                    rows = slice(C * j, C * j + C)
                    a_.activation(k_chunks[rows, j, :, :],
                                  g_ps[2][rows, :].rearrange("p (i f) -> p i f", f=D), ACT.Copy)\
                      .then_inc(k_chunks_ready, 1)

            def soft_exp(a, i):
                act.wait_ge(neg_max_ready, a * NT + i + 1)
                if due(a * NT):
                    act.wait_ge(probs_tr_ready, a * NT)
                if due(a):
                    act.wait_ge(rwo_ready, a)
                n = (i + 1) * P
                a_.activation(probs[:, i, 0:n], g_ps[i % 2][:, 0:n], ACT.Exp, bias=neg_max[:, i:i + 1],
                              scale=SCALE, accum_out=ssum[:, i:i + 1]).then_inc(probs_ready, 1)

            def probs_out(a, i):
                act.wait_ge(probs_tr_ready, a * NT + i + 1)
                if due(a):
                    act.wait_ge(attn_ready, a)
                a_.activation(probs_t[:, 0:i + 1, i * P:(i + 1) * P],
                              g_ps[i % 2][:, 0:(i + 1) * P].rearrange("p (k q) -> p k q", q=P), ACT.Copy)\
                  .then_inc(probs_t_ready, 1)

            def qk_out(a):
                act.wait_ge(qk_tr_ready, a + 1)
                if due(a):
                    act.wait_ge(s_ready, a * NT)
                a_.activation(qk_t[:, :], g_ps[0][:, :], ACT.Copy).then_inc(qk_t_ready, 1)

            def attn_out(a):
                act.wait_ge(attn_ready, a + 1)
                if due(a):
                    act.wait_ge(mixed_ready, a * PAIRS)
                a_.activation(attn_t[:, :], g_ps[0][:, :], ACT.Copy).then_inc(attn_t_ready, 1)
                act.wait_ge(rwo_tr_ready, a + 1)
                if due(a):
                    act.wait_ge(rwb_ready, a * PAIRS)
                a_.activation(rwo_t[:, :], g_ps[1].bitcast(BF16)[:, 0:T], ACT.Copy)\
                  .then_inc(rwo_t_ready, 1)

            def val_out(b):
                act.wait_ge(val_tr_ready, b + 1)
                if due(b):
                    act.wait_ge(wo_added, b)
                a_.activation(val_t[:, :], g_ps[2][:, :], ACT.Copy).then_inc(val_t_ready, 1)

            xt_high(0)
            gate_exp(0)

            def body(b, attn, norm):
                if attn:
                    qk_out(b - 1)
                y_scale(b, 0, 2)
                elu_pieces(b)
                y_scale(b, 2, 4)
                group_q(b)
                y_scale(b, 4, 6)
                if attn:
                    soft_exp(b - 1, 0)
                    soft_exp(b - 1, 1)
                y_scale(b, 6, 8)
                chunk_k(b)
                if attn:
                    soft_exp(b - 1, 2)
                    soft_exp(b - 1, 3)
                y_scale(b, 8, 10)
                if attn:
                    probs_out(b - 1, 0)
                    probs_out(b - 1, 1)
                y_scale(b, 10, 12)
                if attn:
                    probs_out(b - 1, 2)
                    probs_out(b - 1, 3)
                y_scale(b, 12, 16)
                if attn:
                    attn_out(b - 1)
                y_scale(b, 16, 28)
                val_out(b)
                y_scale(b, 28, 32)
                if norm:
                    xt_high(b + 1)
                    gate_exp(b + 1)

            passes(body)(act)
            a = B - 1
            qk_out(a)
            for i in range(NT):
                soft_exp(a, i)
            for i in range(NT):
                probs_out(a, i)
            attn_out(a)

        @block.vector
        def _(dve):
            v = nc.vector
            dve.wait_ge(w_loaded, 16 * WEIGHTS)
            dve.wait_ge(const_ready, 1)
            consts = Chain(dve, dve_const_step, 17, 0)
            consts.step(v.tensor_tensor(sim_sq[:, :], sim[:, :], sim[:, :], ALU.mult))
            dve.wait_ge(sim_norm, 1)
            v.tensor_copy(sim_r[:, 0, :], g_ps[0][:, 0:E]).then_inc(sim_norm_read, 1)
            dve.wait_ge(sim_root, 1)
            consts.step(v.tensor_scalar(sim_r[:, 2, :], sim_r[:, 1, :], NORM_EPS, None, ALU.max))
            consts.step(v.reciprocal(sim_r[:, 3, :], sim_r[:, 2, :]))
            consts.step(v.tensor_tensor(sim_r[:, 0, :], sim[:, :], sim_r[:, 3, :], ALU.mult))
            consts.step(v.tensor_copy(sim_hi[:, :], sim_r[:, 0, :]))
            consts.step(v.tensor_tensor(sim_lo[:, :], sim_r[:, 0, :], sim_hi[:, :], ALU.subtract))
            dve.wait_ge(gates_exp, 1)
            consts.step(v.tensor_scalar(sig[:, 1, :], sig[:, 0, :], 1.0, None, ALU.add))
            consts.step(v.reciprocal(sigmoid[:, :], sig[:, 1, :]))
            by_place = "p (g s m) -> p s g m"
            consts.step(v.tensor_copy(lin_w[:, 2, :].rearrange("p (s g m) -> p s g m", g=G, m=M),
                                      wv_raw[:, :].rearrange(by_place, g=G, m=M)))
            consts.step(v.tensor_copy(bv_row[:, :].rearrange("p (s g m) -> p s g m", g=G, m=M),
                                      bv_raw[:, :].rearrange(by_place, g=G, m=M)))
            consts.step(v.tensor_copy(lin_hi[:, :, :], lin_w[:, :, :]))
            consts.step(v.tensor_tensor(lin_lo[:, :, :], lin_w[:, :, :], lin_hi[:, :, :], ALU.subtract))

            def statistics(n):
                st = Chain(dve, stats_step, STATS, n)
                dve.wait_ge(x_loaded, (n + 1) * 16)
                for i in range(NT):
                    last = v.bn_stats(stats[:, i, :], x[:, i, :])
                st.step(last)
                v.memset(wait_pad[:, :], 0.0)
                for i in range(NT):
                    last = v.bn_aggr(mv[:, i, :], stats[:, i, :])
                st.step(last)
                v.tensor_scalar(var_eps[:, :], mv[:, :, 1], LN_EPS, None, ALU.add).then_inc(var_ready, 1)
                dve.wait_ge(rstd_ready, n + 1)
                st.step(v.tensor_tensor(nrm[:, 0, :], mv[:, :, 1], rstd[:, :], ALU.mult))
                st.step(v.tensor_tensor(nrm[:, 4, :], nrm[:, 0, :], rstd[:, :], ALU.mult))
                v.tensor_scalar(nrm[:, 1, :], nrm[:, 4, :], float(D), None, ALU.mult)\
                 .then_inc(norm_sq_ready, 1)
                if due(n):
                    dve.wait_ge(xt_ready, n)
                for i in range(NT):
                    v.tensor_scalar(xn[:, i, :], x[:, i, :], mv[:, i, 0:1], rstd[:, i:i + 1],
                                    ALU.subtract, ALU.mult).then_inc(xn_ready, 1)
                dve.wait_ge(norm_ready, n + 1)
                st.step(v.tensor_scalar(nrm[:, 0, :], nrm[:, 2, :], NORM_EPS, None, ALU.max))
                st.step(v.reciprocal(nrm[:, 3, :], nrm[:, 0, :]))
                st.end()

            STATS = 6

            def xt_low(n):
                dve.wait_ge(xt_hi_ready, n + 1)
                v.tensor_tensor(xt_lo[:, :], g_ps[4][:, :], xt_hi[:, :], ALU.subtract)\
                 .then_inc(xt_lo_ready, 1)

            GATES = 24

            def over_e(t):
                return t.unsqueeze(2).broadcast_to([P, NT, E])

            def over_i(t):
                return t.unsqueeze(1).broadcast_to([P, NT, E])

            def gate_mask(n):
                st = Chain(dve, gate_step, GATES, n)
                dve.wait_ge(logits_ready, n + 1)
                l, l2 = logit[:, 1, :, :], gate[:, 3, :, :]
                v.tensor_tensor(logit[:, 0, :, :], g_ps[2][:, 0:NT * E].rearrange("p (i e) -> p i e", e=E),
                                over_e(nrm[:, 3, :]), ALU.mult).then_inc(logits_read, 1)
                dve.wait_ge(logits_read, n + 1)
                st.step(v.tensor_tensor(l, logit[:, 0, :, :], over_i(sigmoid[:, :]), ALU.subtract))
                st.step(v.tensor_reduce(gmax[:, 0, :], l, AX.X, ALU.max))
                st.step(v.tensor_scalar(gmax[:, 1, :], gmax[:, 0, :], 0.0, None, ALU.max))
                st.step(v.tensor_scalar(gate[:, 9, :, :], l, 0.0, None, ALU.max))
                v.tensor_tensor(gate[:, 10, :, :], gate[:, 9, :, :], over_e(gmax[:, 1, :]), ALU.subtract)\
                 .then_inc(gate_arg_ready, 1)
                st.step(v.tensor_tensor(gate[:, 0, :, :], l, over_e(gmax[:, 0, :]), ALU.is_ge))
                st.step(v.tensor_tensor(gate[:, 1, :, :], gate[:, 0, :, :], over_i(rank[:, :]), ALU.mult))
                st.step(v.tensor_reduce(gmax[:, 2, :], gate[:, 1, :, :], AX.X, ALU.max))
                st.step(v.tensor_tensor(gate[:, 2, :, :], gate[:, 1, :, :], over_e(gmax[:, 2, :]), ALU.is_ge))
                st.step(v.tensor_scalar(gate[:, 11, :, :], gate[:, 2, :, :], -BIG, None, ALU.mult))
                st.step(v.tensor_tensor(l2, gate[:, 11, :, :], l, ALU.add))
                st.step(v.tensor_reduce(gmax[:, 3, :], l2, AX.X, ALU.max))
                st.step(v.tensor_tensor(gate[:, 4, :, :], l2, over_e(gmax[:, 3, :]), ALU.is_ge))
                st.step(v.tensor_tensor(gate[:, 5, :, :], gate[:, 4, :, :], over_i(rank[:, :]), ALU.mult))
                st.step(v.tensor_reduce(gmax[:, 4, :], gate[:, 5, :, :], AX.X, ALU.max))
                st.step(v.tensor_tensor(gate[:, 6, :, :], gate[:, 5, :, :], over_e(gmax[:, 4, :]), ALU.is_ge))
                st.step(v.tensor_tensor(gate[:, 7, :, :], gate[:, 2, :, :], gate[:, 6, :, :], ALU.add))
                st.step(v.tensor_scalar(gmax[:, 5, :], gmax[:, 0, :], 0.0, None, ALU.is_le))
                st.step(v.tensor_tensor(gate[:, 8, :, :], gate[:, 7, :, :], over_e(gmax[:, 5, :]), ALU.mult))
                st.step(v.tensor_scalar(gate[:, 0, :, :], l, 0.0, None, ALU.is_gt))
                st.step(v.tensor_tensor(gate[:, 1, :, :], gate[:, 0, :, :], gate[:, 8, :, :], ALU.add))
                return st

            def gate_weights(n, st):
                dve.wait_ge(gate_exp_ready, n + 1)
                st.step(v.tensor_tensor(gate[:, 2, :, :], gexp[:, :, :], gate[:, 1, :, :], ALU.mult))
                st.step(v.tensor_reduce(gmax[:, 6, :], gate[:, 2, :, :], AX.X, ALU.add))
                st.step(v.reciprocal(gmax[:, 7, :], gmax[:, 6, :]))
                if due(n * YN):
                    dve.wait_ge(y_scaled_s, n * YN)
                if due(n * YN):
                    dve.wait_ge(y_added_v, n * YN)
                st.step(v.tensor_copy(rw_prev[:, :, :], rw[:, :, :]) if not isinstance(n, int) or n
                        else v.memset(rw_prev[:, :, :], 0.0))
                v.tensor_tensor(rw[:, :, :], gate[:, 2, :, :], over_e(gmax[:, 7, :]), ALU.mult)\
                 .then_inc(rw_ready, 1)
                dve.wait_ge(rw_ready, n + 1)
                st.end()

            def y_add(b, first, last):
                for n in range(first, last):
                    i, p = n // PAIRS, n % PAIRS
                    if p % 2:
                        continue
                    dve.wait_ge(y_ready[0], b * YN // 2 + n // 2 + 1)
                    if p == 0:
                        if due((b - 1) * NT + i + 1):
                            dve.wait_ge(y_summed, (b - 1) * NT + i + 1)
                    for u in range(2):
                        e = 2 * p + u
                        y = y_view[0][:, u * W3:(u + 1) * W3]
                        if p == 0:
                            v.tensor_scalar(acc_v[:, i, u, :], y, rw[:, i, e:e + 1], None, ALU.mult)\
                             .then_inc(y_added_v, 1)
                        else:
                            if due(b * YN + n + u - 1):
                                dve.wait_ge(y_added_v, b * YN + n + u - 1)
                            v.scalar_tensor_tensor(out=acc_v[:, i, u, :], in0=y, scalar=rw[:, i, e:e + 1],
                                                   in1=acc_v[:, i, u, :], op0=ALU.mult, op1=ALU.add)\
                             .then_inc(y_added_v, 1)

            def values(b):
                dve.wait_ge(proj_ready, b * 3 + 3)
                if due(16 * 16 * b):
                    dve.wait_ge(v_spread, 16 * 16 * b)
                if due(ND * b):
                    dve.wait_ge(d_ready, ND * b)
                v.tensor_tensor(v_ones[:, :, :, :, 0:M].rearrange("p i s g m -> p (i s g) m"),
                                g_ps[4][:, :].rearrange("p (a m) -> p a m", m=M),
                                bv_row[:, :].unsqueeze(1).broadcast_to([P, NT, D]), ALU.add)\
                 .then_inc(v_ready, 1)

            def elu(b):
                for n, (dst, ready) in enumerate(((q_t, q_ready), (k_t, k_ready))):
                    dve.wait_ge(elu_parts, b * 4 + 2 * n + 2)
                    if n == 0:
                        if due(b * NT):
                            dve.wait_ge(la_ready, b * NT)
                        if due(b * G):
                            dve.wait_ge(q_groups_ready, b * G)
                    else:
                        if due(b):
                            dve.wait_ge(k_tok_ready, b)
                        if due(b * S4):
                            dve.wait_ge(k_places_ready, b * S4)
                    v.scalar_tensor_tensor(out=dst[:, :], in0=elu_e[:, n, :], scalar=1.0, in1=elu_r[:, n, :],
                                           op0=ALU.min, op1=ALU.add).then_inc(ready, 1)

            def place_k(b):
                dve.wait_ge(k_ready, b + 1)
                if due(b * NT):
                    dve.wait_ge(score_ready, b * NT)
                for s in range(S4):
                    v.tensor_scalar(k_places[:, :, s, :], k_t[:, :].rearrange("p (c t) -> p c t", t=C),
                                    place_mask[:, s:s + 1], None, ALU.mult).then_inc(k_places_ready, 1)

            def mask_scores(b, i):
                dve.wait_ge(score_ready, b * NT + i + 1)
                if due((b - 1) * NT + i + 1):
                    dve.wait_ge(la_ready, (b - 1) * NT + i + 1)
                v.tensor_tensor(scores[:, i, :].rearrange("p (a q) -> p a q", q=C),
                                g_ps[3 + i % 2][:, :].rearrange("p (a q) -> p a q", q=C),
                                past[:, :].unsqueeze(1).broadcast_to([P, CT * G, C]), ALU.mult)\
                 .then_inc(score_masked, 1)

            def mask_states(b, n):
                dve.wait_ge(d_ready, b * ND + n + 1)
                if due(b * (NC - 1)):
                    dve.wait_ge(state_ready, b * (NC - 1))
                v.tensor_tensor(d_state[:, n * DB:(n + 1) * DB, :],
                                g_ps[2 + n % 2][:, 0:DB * VW].rearrange("p (a w) -> p a w", w=VW),
                                block_mask[:, :].unsqueeze(1).broadcast_to([P, DB, VW]), ALU.mult)\
                 .then_inc(d_masked, 1)

            def la_values(b, n):
                st = Chain(dve, den_step, 2, b * 2 + n)
                o = g_ps[(4, 3)[n]][:, 0:2 * VW].rearrange("p (a m) -> p a m", m=M1)
                dve.wait_ge(la_ready, b * NT + 2 * n + 2)
                if due(b):
                    dve.wait_ge(val_tr_ready, b)
                st.step(v.tensor_scalar(den[:, n, 0, :].unsqueeze(2), o[:, :, M:M1], DEN_EPS, None, ALU.add))
                st.step(v.reciprocal(den[:, n, 1, :], den[:, n, 0, :]))
                v.tensor_tensor(val[:, 2 * n:2 * n + 2, :].rearrange("p i (a m) -> p (i a) m", m=M),
                                o[:, :, 0:M], den[:, n, 1, :].unsqueeze(2).broadcast_to([P, 2 * H, M]),
                                ALU.mult).then_inc(val_ready, 1)

            def k_out(a):
                dve.wait_ge(qk_tr_ready, a + 1)
                if due(a * NT):
                    dve.wait_ge(s_ready, a * NT)
                v.tensor_copy(k_zero[0:HD, :], g_ps[1][0:HD, :]).then_inc(k_zero_ready, 1)

            def row_max(a, i):
                dve.wait_ge(s_ready, a * NT + i + 1)
                if due(a * NT):
                    dve.wait_ge(neg_max_ready, a * NT)
                v.tensor_reduce(smax[:, i:i + 1], g_ps[i % 2][:, 0:(i + 1) * P], AX.X, ALU.max)\
                 .then_inc(max_ready, 1)
                dve.wait_ge(max_ready, a * NT + i + 1)
                if due(a * NT):
                    dve.wait_ge(probs_ready, a * NT)
                v.tensor_scalar(neg_max[:, i:i + 1], smax[:, i:i + 1], -SCALE, None, ALU.mult)\
                 .then_inc(neg_max_ready, 1)

            def output_weights(a):
                st = Chain(dve, rwo_step, 5, a)
                dve.wait_ge(probs_ready, (a + 1) * NT)
                if due(a):
                    dve.wait_ge(rwo_tr_ready, a)
                st.step(v.reciprocal(srec[:, :], ssum[:, :]))
                st.step(v.tensor_tensor(rwo[:, 0, :, :], rw_prev[:, :, :] if a is not None else None,
                                        over_e(srec[:, :]), ALU.mult))
                st.step(v.tensor_copy(rwo_parts[:, :, 0:E], rwo[:, 0, :, :]))
                st.step(v.tensor_tensor(rwo[:, 1, :, :], rwo[:, 0, :, :], rwo_parts[:, :, 0:E], ALU.subtract))
                st.step(v.tensor_copy(rwo_parts[:, :, E:2 * E], rwo[:, 1, :, :]))
                v.tensor_tensor(rwo_parts[:, :, 2 * E:3 * E], rwo[:, 1, :, :], rwo_parts[:, :, E:2 * E],
                                ALU.subtract).then_inc(rwo_ready, 1)
                st.end()

            def mix(a, first, last):
                for p in range(first, last):
                    dve.wait_ge(rwb_ready, a * PAIRS + p + 1)
                    dve.wait_ge(attn_t_ready, a + 1)
                    if due(a * PAIRS + max(p - 1, 0)):
                        dve.wait_ge(pair_added, a * PAIRS + max(p - 1, 0))
                    v.tensor_tensor(mixed[:, p % 2, :], g_ps[p % 2][:, :], attn_t[:, :], ALU.mult)\
                     .then_inc(mixed_ready, 1)

            def finish(a):
                dve.wait_ge(pair_added, (a + 1) * PAIRS)
                dve.wait_ge(res_ready, a + 1)
                if due(a * 16):
                    dve.wait_ge(out_stored, a * 16)
                v.tensor_tensor(out_sb[:, :, :], out_ps[:, :, :], res[:, :, :], ALU.add)\
                 .then_inc(out_ready, 1)

            statistics(0)
            dve.wait_ge(act_const_ready, 1)
            consts.step(v.tensor_tensor(w3_lo[:, :, :], stage[:, :, :], w3_hi[:, :, :], ALU.subtract))
            v.memset(rwo[:, 0, 0, 0:1], 0.0).then_inc(dve_const_ready, 1)
            xt_low(0)
            gate_weights(0, gate_mask(0))

            def body(b, attn, norm):
                if attn:
                    k_out(b - 1)
                y_add(b, 0, 2)
                values(b)
                y_add(b, 2, 4)
                elu(b)
                place_k(b)
                y_add(b, 4, 6)
                if attn:
                    row_max(b - 1, 0)
                    row_max(b - 1, 1)
                y_add(b, 6, 8)
                mask_scores(b, 0)
                mask_scores(b, 1)
                if attn:
                    row_max(b - 1, 2)
                    row_max(b - 1, 3)
                y_add(b, 8, 10)
                mask_scores(b, 2)
                mask_scores(b, 3)
                if attn:
                    output_weights(b - 1)
                y_add(b, 10, 12)
                mask_states(b, 0)
                mask_states(b, 1)
                y_add(b, 12, 14)
                mask_states(b, 2)
                mask_states(b, 3)
                y_add(b, 14, 16)
                mask_states(b, 4)
                y_add(b, 16, 20)
                if norm:
                    statistics(b + 1)
                la_values(b, 0)
                y_add(b, 20, 24)
                la_values(b, 1)
                y_add(b, 24, 32)
                if attn:
                    mix(b - 1, 0, 2)
                if norm:
                    xt_low(b + 1)
                if attn:
                    mix(b - 1, 2, 5)
                if norm:
                    st = gate_mask(b + 1)
                if attn:
                    mix(b - 1, 5, 8)
                if norm:
                    gate_weights(b + 1, st)
                if attn:
                    finish(b - 1)

            passes(body)(dve)
            a = B - 1
            v.tensor_copy(rw_prev[:, :, :], rw[:, :, :]).then_inc(rw_ready, 1)
            dve.wait_ge(rw_ready, B + 1)
            k_out(a)
            for i in range(NT):
                row_max(a, i)
            output_weights(a)
            mix(a, 0, PAIRS)
            finish(a)

        @block.tensor
        def _(pe):
            t_ = nc.tensor

            def product(dst, lhs, rhs, done=None, start=True):
                (lh, ll), (rh, rl) = lhs, rhs
                t_.matmul(dst, lh, rh, start=start, stop=False)
                t_.matmul(dst, lh, rl, start=False, stop=False)
                last = t_.matmul(dst, ll, rh, start=False, stop=True)
                if done is not None:
                    last.then_inc(done, 1)

            pe.wait_ge(dve_const_step, 1)
            t_.matmul(g_ps[0][:, 0:E], ones[:, :], sim_sq[:, :], start=True, stop=True).then_inc(sim_norm, 1)

            def tile(t, i):
                return t[:, i * P:(i + 1) * P]

            def xn_transpose(n):
                pe.wait_ge(xn_ready, (n + 1) * NT)
                if due(n * 2 - 1):
                    pe.wait_ge(val_ready, n * 2 - 1)
                for i in range(NT):
                    last = t_.transpose(tile(g_ps[4], i), xn[:, i, :], ident[:, :])
                last.then_inc(xt_ready, 1)

            def gate_logits(n):
                pe.wait_ge(xt_lo_ready, n + 1)
                if due(n):
                    pe.wait_ge(val_t_ready, n)
                for i in range(NT):
                    product(g_ps[2][:, i * E:(i + 1) * E], (tile(xt_hi, i), tile(xt_lo, i)),
                            (sim_hi[:, :], sim_lo[:, :]), logits_ready if i == NT - 1 else None)

            def y_pairs(b, first, last):
                for n in range(first, last):
                    i, p = n // PAIRS, n % PAIRS
                    if n % 2 == 0:
                        if due(b * YN + n):
                            pe.wait_ge(y_added_v, b * YN + n)
                    else:
                        if due(b * YN + n - 1):
                            pe.wait_ge(y_scaled_s, b * YN + n - 1)
                    cols = slice(2 * p, 2 * p + 2)
                    product(y_view[n % 2], (tile(xt_hi, i), tile(xt_lo, i)),
                            (w3_hi[:, cols, :].rearrange("p a b -> p (a b)"),
                             w3_lo[:, cols, :].rearrange("p a b -> p (a b)")), y_ready[n % 2])

            def projections(b):
                pe.wait_ge(logits_read, b + 1)
                for n in range(2):
                    if n == 1:
                        if due(b * 2):
                            pe.wait_ge(val_ready, b * 2)
                    product(g_ps[2 + n][:, :], (lin_hi[:, n, :], lin_lo[:, n, :]),
                            (xt_hi[:, :], xt_lo[:, :]), proj_ready)
                pe.wait_ge(xt_lo_ready, b + 1)
                for i in range(NT):
                    product(tile(g_ps[4], i), (tile(xt_hi, i), tile(xt_lo, i)),
                            (lin_hi[:, 2, :], lin_lo[:, 2, :]), proj_ready if i == NT - 1 else None)

            def k_to_tokens(b):
                pe.wait_ge(k_ready, b + 1)
                pe.wait_ge(elu_parts, b * 4 + 2)
                for i in range(NT):
                    last = t_.transpose(tile(g_ps[2], i), tile(k_t, i), ident[:, :])
                last.then_inc(k_tok_ready, 1)

            def score(b, i):
                pe.wait_ge(k_places_ready, (b + 1) * S4)
                pe.wait_ge(q_groups_ready, (b + 1) * G)
                if i == 0:
                    pe.wait_ge(elu_parts, b * 4 + 4)
                elif i == 1:
                    pe.wait_ge(v_ready, b + 1)
                else:
                    if due(b * NT + i - 1):
                        pe.wait_ge(score_masked, b * NT + i - 1)
                for j in range(CT):
                    c = i * CT + j
                    last = t_.matmul(tile(g_ps[3 + i % 2], j),
                                     k_places[:, c, :, :].rearrange("p s t -> p (s t)"),
                                     q_groups[:, c, :, :].rearrange("p g t -> p (g t)"), start=True, stop=True)
                last.then_inc(score_ready, 1)

            def chunk_states(b, n):
                if n == 0:
                    pe.wait_ge(k_chunks_ready, (b + 1) * CT)
                    pe.wait_ge(v_ready, b + 1)
                elif n == 1:
                    pe.wait_ge(score_masked, b * NT + 3)
                else:
                    if due(b * ND + n - 1):
                        pe.wait_ge(d_masked, b * ND + n - 1)
                for m in range(DB):
                    c = n * DB + m
                    i, j = c // CT, c % CT
                    last = t_.matmul(g_ps[2 + n % 2][:, m * VW:(m + 1) * VW], k_chunks[:, j, i, :],
                                     v_ones[:, i, :, :, :].rearrange("p s g m -> p (s g m)"),
                                     start=True, stop=True)
                last.then_inc(d_ready, 1)

            def la_tile(b, i):
                pe.wait_ge(v_spread, 16 * 16 * (b + 1))
                pe.wait_ge(state_ready, b * (NC - 1) + min(i * CT + CT - 1, NC - 1))
                pe.wait_ge(score_masked, (b + 1) * NT)
                pe.wait_ge(d_masked, b * ND + 4)
                bank = g_ps[(4, 3)[i // 2]]
                o = bank[:, (i % 2) * VW:(i % 2 + 1) * VW]
                for j in range(CT):
                    c = i * CT + j
                    t_.matmul(o[C * j:C * j + C, :], q_t[:, c * C:(c + 1) * C],
                              state[:, c, :].rearrange("p (s g m) -> p g s m", s=S4, g=G),
                              start=True, stop=False, skip_group_check=True)
                for g in range(G):
                    for j in range(CT):
                        c = i * CT + j
                        last = t_.matmul(o[C * j:C * j + C, g * S4 * M1:(g + 1) * S4 * M1],
                                         scores[:, i, (j * G + g) * C:(j * G + g + 1) * C],
                                         v_blocks[:, c, :, g, :], start=False, stop=(g == G - 1),
                                         skip_group_check=True)
                last.then_inc(la_ready, 1)

            def val_transpose(b):
                pe.wait_ge(val_ready, (b + 1) * 2)
                pe.wait_ge(d_masked, (b + 1) * ND)
                for i in range(NT):
                    last = t_.transpose(tile(g_ps[2], i), val[:, i, :], ident[:, :])
                last.then_inc(val_tr_ready, 1)

            def start_output(a):
                pe.wait_ge(val_t_ready, a + 1)
                if due(a):
                    pe.wait_ge(out_ready, a)
                for i in range(NT):
                    last = t_.matmul(out_ps[:, i, :], tile(val_t, i), wo[:, :], start=(i == 0), stop=False,
                                     skip_group_check=True)
                last.then_inc(wo_added, 1)

            def qk_transpose(a):
                pe.wait_ge(qkv_ready, (a + 1) * NT * 2)
                if due(a * PAIRS):
                    pe.wait_ge(mixed_ready, a * PAIRS)
                for i in range(NT):
                    t_.transpose(tile(g_ps[0], i), qk[:, i, :], ident[:, :])
                    last = t_.transpose(g_ps[1][0:HD, i * P:(i + 1) * P], qk[:, i, HD:2 * HD], ident[:, :])
                last.then_inc(qk_tr_ready, 1)

            def soft_scores(a, i):
                pe.wait_ge(qk_t_ready, a + 1)
                pe.wait_ge(k_zero_ready, a + 1)
                if i >= 2:
                    if due(a * NT + i - 1):
                        pe.wait_ge(probs_ready, a * NT + i - 1)
                n = (i + 1) * P
                s = g_ps[i % 2]
                t_.matmul(s[:, 0:n], tile(qk_t, i), k_zero[:, 0:n], start=True, stop=False,
                          skip_group_check=True)
                t_.matmul(s[:, n - P:n], ident_bf[:, :], future_bf[:, :], start=False, stop=True,
                          skip_group_check=True).then_inc(s_ready, 1)

            def probs_transpose(a, i):
                pe.wait_ge(probs_ready, a * NT + i + 1)
                if i < 2:
                    pe.wait_ge(probs_ready, a * NT + i + 3)
                else:
                    if due(a * NT + i - 1):
                        pe.wait_ge(probs_t_ready, a * NT + i - 1)
                for k in range(i + 1):
                    last = t_.transpose(tile(g_ps[i % 2], k), probs[:, i, k * P:(k + 1) * P], ident[:, :])
                last.then_inc(probs_tr_ready, 1)

            def attend(a):
                pe.wait_ge(probs_t_ready, (a + 1) * NT)
                for k in range(NT):
                    last = t_.matmul(g_ps[0][:, k * P:T], v_dup[:, k, :, :].rearrange("p u d -> p (u d)"),
                                     probs_t[:, k, k * P:T], start=(k == 0), stop=(k == NT - 1),
                                     skip_group_check=True)
                last.then_inc(attn_ready, 1)
                pe.wait_ge(rwo_ready, a + 1)
                for i in range(NT):
                    last = t_.transpose(g_ps[1].bitcast(BF16)[:, i * P:(i + 1) * P], rwo_parts[:, i, :],
                                        ident_bf[:, :])
                last.then_inc(rwo_tr_ready, 1)

            def spread_weights(a, p):
                pe.wait_ge(rwo_t_ready, a + 1)
                if p < 2:
                    pe.wait_ge(attn_t_ready, a + 1)
                else:
                    if due(a * PAIRS + p - 1):
                        pe.wait_ge(mixed_ready, a * PAIRS + p - 1)
                t_.matmul(g_ps[p % 2][:, :], pair_sel[:, p, :, :].rearrange("p u d -> p (u d)"), rwo_t[:, :],
                          start=True, stop=True).then_inc(rwb_ready, 1)

            def add_pair(a, p):
                pe.wait_ge(mixed_ready, a * PAIRS + p + 1)
                for i in range(NT):
                    last = t_.matmul(out_ps[:, i, :], mixed[:, p % 2, i * P:(i + 1) * P], eo[:, p, :],
                                     start=False, stop=(p == PAIRS - 1 and i == NT - 1),
                                     skip_group_check=True)
                last.then_inc(pair_added, 1)

            def output_pairs(a, first, last):
                for p in range(first, last):
                    if p == 0:
                        spread_weights(a, 0)
                    if p + 1 < PAIRS:
                        spread_weights(a, p + 1)
                    add_pair(a, p)

            pe.wait_ge(const_ready, 1)
            xn_transpose(0)
            gate_logits(0)
            pe.wait_ge(dve_const_ready, 1)

            def body(b, attn, norm):
                if attn:
                    start_output(b - 1)
                    qk_transpose(b - 1)
                y_pairs(b, 0, 2)
                projections(b)
                y_pairs(b, 2, 6)
                if attn:
                    soft_scores(b - 1, 0)
                    soft_scores(b - 1, 1)
                y_pairs(b, 6, 8)
                k_to_tokens(b)
                score(b, 0)
                score(b, 1)
                if attn:
                    soft_scores(b - 1, 2)
                    soft_scores(b - 1, 3)
                y_pairs(b, 8, 10)
                score(b, 2)
                score(b, 3)
                if attn:
                    probs_transpose(b - 1, 0)
                    probs_transpose(b - 1, 1)
                y_pairs(b, 10, 12)
                chunk_states(b, 0)
                chunk_states(b, 1)
                if attn:
                    probs_transpose(b - 1, 2)
                    probs_transpose(b - 1, 3)
                y_pairs(b, 12, 14)
                chunk_states(b, 2)
                chunk_states(b, 3)
                y_pairs(b, 14, 16)
                chunk_states(b, 4)
                if attn:
                    attend(b - 1)
                y_pairs(b, 16, 20)
                la_tile(b, 0)
                la_tile(b, 1)
                y_pairs(b, 20, 24)
                la_tile(b, 2)
                la_tile(b, 3)
                y_pairs(b, 24, 28)
                val_transpose(b)
                y_pairs(b, 28, 32)
                if norm:
                    xn_transpose(b + 1)
                if attn:
                    output_pairs(b - 1, 0, 3)
                if norm:
                    gate_logits(b + 1)
                if attn:
                    output_pairs(b - 1, 3, PAIRS)

            passes(body)(pe)
            a = B - 1
            start_output(a)
            qk_transpose(a)
            soft_scores(a, 0)
            soft_scores(a, 1)
            soft_scores(a, 2)
            soft_scores(a, 3)
            for i in range(NT):
                probs_transpose(a, i)
            attend(a)
            output_pairs(a, 0, PAIRS)


_INS = ["L0_attn_x", "L0_attn_Wq", "L0_attn_bq", "L0_attn_Wk", "L0_attn_bk", "L0_attn_Wv", "L0_attn_bv",
        "L0_attn_Wo", "L0_attn_bo", "L0_ffn_sim_matrix", "L0_ffn_gates", "L0_ffn_q_proj", "L0_ffn_k_proj",
        "L0_ffn_v_proj", "L0_ffn_o_proj"]


def kernel(**inputs):
    import numpy as _np
    import concourse.bacc as _bacc
    from concourse import mybir as _mybir
    from concourse.bass_utils import run_bass_kernel_spmd as _run

    nc = _bacc.Bacc("TRN2", target_bir_lowering=False, num_devices=1)
    arrays, args = {}, []
    for name in _INS:
        a = _np.ascontiguousarray(inputs[name])
        arrays[name] = a
        args.append(nc.dram_tensor(name, a.shape, _mybir.dt.from_np(a.dtype), kind="ExternalInput").ap())
    shape = inputs["L0_attn_x"].shape
    args.append(nc.dram_tensor("out", shape, _mybir.dt.float32, kind="ExternalOutput").ap())
    build(nc, *args)
    r = _run(nc, [arrays], core_ids=[0])
    return r.results[0]["out"]
```

```python
from contextlib import ExitStack

import concourse.bass as bass
from concourse import mybir

F32 = mybir.dt.float32
F16 = mybir.dt.float16
BF16 = mybir.dt.bfloat16
ALU = mybir.AluOpType
ACT = mybir.ActivationFunctionType
AX = mybir.AxisListType

P = 128
BIG = 1.0e30
LN_EPS = 1e-5
NORM_EPS = 1e-12
DEN_EPS = 1e-6


def due(count):
    return not isinstance(count, int) or count > 0


class Chain:

    def __init__(self, engine, semaphore, per_pass, index):
        self.engine, self.semaphore, self.n = engine, semaphore, 0
        self.per_pass, self.index = per_pass, index

    def step(self, instruction):
        self.n += 1
        instruction.then_inc(self.semaphore, 1)
        self.engine.wait_ge(self.semaphore, self.index * self.per_pass + self.n)

    def end(self):
        assert self.n == self.per_pass, self.n


def build(nc, x_in, wq_in, bq_in, wk_in, bk_in, wv_in, bv_in, wo_in, bo_in,
          sim_in, gates_in, eq_in, ek_in, ev_in, eo_in, out):
    B, T, D = x_in.shape
    E, _, HD = eq_in.shape
    NT = T // P
    C = 32
    CT = P // C
    NC = T // C
    H, M = 16, 8
    G = 4
    S4 = H // G
    M1 = M + 1
    VW = H * M1
    W3 = 3 * HD
    PAIRS = E // 2
    YN = NT * PAIRS
    TMP = 4
    DB = 3
    ND = NC // DB
    SCALE = float(HD) ** -0.5
    assert D == P and H * M == D and NC == 16 and ND * DB == NC - 1

    ctx = ExitStack()
    with ctx:
        def sb(name, shape, dt=F32):
            return ctx.enter_context(nc.sbuf_tensor(name, shape, dt))

        def sem(name):
            return ctx.enter_context(nc.semaphore(name))

        ident = sb("ident", [P, P])
        ident_bf = sb("ident_bf", [P, P], BF16)
        ones = sb("ones", [P, P])
        future_bf = sb("future_bf", [P, P], BF16)
        past = sb("past", [P, C])
        place_mask = sb("place_mask", [P, S4])
        block_mask = sb("block_mask", [P, VW])
        pair_sel = sb("pair_sel", [P, PAIRS, 2, HD], BF16)
        rank = sb("rank", [P, E])
        half = sb("half", [P, NT])
        neg_half = sb("neg_half", [P, NT])
        half16 = sb("half16", [P, E])
        stage = sb("stage", [P, E, W3])
        w3_hi = sb("w3_hi", [P, E, W3], F16)
        w3_lo = sb("w3_lo", [P, E, W3], F16)
        lin_w = sb("lin_w", [P, 3, D])
        lin_hi = sb("lin_hi", [P, 3, D], F16)
        lin_lo = sb("lin_lo", [P, 3, D], F16)
        wv_raw = sb("wv_raw", [P, D])
        bv_raw = sb("bv_raw", [P, D])
        bv_row = sb("bv_row", [P, D])
        bo_row = sb("bo_row", [P, D])
        bqk = sb("bqk", [P, 2])
        wo = sb("wo", [P, D])
        eo = sb("eo", [P, PAIRS, D])
        sim = sb("sim", [P, E])
        sim_sq = sb("sim_sq", [P, E])
        sim_r = sb("sim_r", [P, 4, E])
        sim_hi = sb("sim_hi", [P, E], F16)
        sim_lo = sb("sim_lo", [P, E], F16)
        gates = sb("gates", [P, E])
        sig = sb("sig", [P, 3, E])
        sigmoid = sb("sigmoid", [P, E])

        x = sb("x", [P, NT, D])
        stats = sb("stats", [P, NT, 6])
        mv = sb("mv", [P, NT, 2])
        wait_pad = sb("wait_pad", [P, 1])
        var_eps = sb("var_eps", [P, NT])
        rstd = sb("rstd", [P, NT])
        nrm = sb("nrm", [P, 5, NT])
        xn = sb("xn", [P, NT, D])
        xt_hi = sb("xt_hi", [P, T], F16)
        xt_lo = sb("xt_lo", [P, T], F16)
        logit = sb("logit", [P, 2, NT, E])
        gmax = sb("gmax", [P, 8, NT])
        gate_sb = sb("gate_sb", [P, 11, NT, E])
        gexp = sb("gexp", [P, NT, E])
        rw = sb("rw", [P, NT, E])
        rw_prev = sb("rw_prev", [P, NT, E])

        acc_v = sb("acc_v", [P, NT, 2, W3])
        acc_s = sb("acc_s", [P, NT, 2, W3])
        y_tmp = sb("y_tmp", [P, TMP, 2, W3])
        y_sum = sb("y_sum", [P, NT, 2, W3])
        qk = sb("qk", [P, NT, 2 * HD])
        v_dup = sb("v_dup", [P, NT, 2, HD])

        elu_e = sb("elu_e", [P, 2, T])
        elu_r = sb("elu_r", [P, 2, T])
        q_t = sb("q_t", [P, T])
        k_t = sb("k_t", [P, T])
        q_groups = sb("q_groups", [P, NC, G, C])
        k_places = sb("k_places", [P, NC, S4, C])
        k_chunks = sb("k_chunks", [P, CT, NT, D])
        v_ones = sb("v_ones", [P, NT, S4, G, M1])
        v_blocks = sb("v_blocks", [P, NC, S4, G, M1])
        scores = sb("scores", [P, NT, CT * G * C])
        d_state = sb("d_state", [P, NC - 1, VW])
        state = sb("state", [P, NC, VW])
        den = sb("den", [P, 2, 2, 2 * H])
        val = sb("val", [P, NT, D])
        val_t = sb("val_t", [P, T])

        qk_t = sb("qk_t", [P, T])
        k_zero = sb("k_zero", [P, T])
        smax = sb("smax", [P, NT])
        neg_max = sb("neg_max", [P, NT])
        ssum = sb("ssum", [P, NT])
        srec = sb("srec", [P, NT])
        probs = sb("probs", [P, NT, T])
        probs_t = sb("probs_t", [P, NT, T])
        attn_t = sb("attn_t", [P, T])
        rwo = sb("rwo", [P, 2, NT, E])
        rwo_parts = sb("rwo_parts", [P, NT, P], BF16)
        rwo_t = sb("rwo_t", [P, T], BF16)
        mixed = sb("mixed", [P, 2, T])
        x_res = sb("x_res", [P, NT, D])
        res = sb("res", [P, NT, D])
        out_sb = sb("out_sb", [P, NT, D])

        y_ps = [ctx.enter_context(nc.psum_tensor(f"y_ps{n}", [P, 2, 256], F32)) for n in range(2)]
        out_ps = ctx.enter_context(nc.psum_tensor("out_ps", [P, NT, D], F32))
        g_ps = [ctx.enter_context(nc.psum_tensor(f"g_ps{n}", [P, 512], F32)) for n in range(5)]
        y_view = [t[:, :, :].rearrange("p a b -> p (a b)")[:, 0:2 * W3] for t in y_ps]

        gate_loaded = sem("gate_loaded")
        experts_loaded = sem("experts_loaded")
        lin_loaded = sem("lin_loaded")
        out_w_loaded = sem("out_w_loaded")
        filled = sem("filled")
        ident_ready = sem("ident_ready")
        const_step = sem("const_step")
        const_ready = sem("const_ready")
        dve_const_step = sem("dve_const_step")
        w3_hi_ready = sem("w3_hi_ready")
        sim_norm = sem("sim_norm")
        sim_ready = sem("sim_ready")
        lin_ready = sem("lin_ready")
        w3_ready = sem("w3_ready")
        sim_norm_read = sem("sim_norm_read")
        sim_root = sem("sim_root")
        gates_exp = sem("gates_exp")

        x_loaded = sem("x_loaded")
        stats_step = sem("stats_step")
        var_ready = sem("var_ready")
        rstd_ready = sem("rstd_ready")
        norm_sq_ready = sem("norm_sq_ready")
        norm_ready = sem("norm_ready")
        xn_ready = sem("xn_ready")
        xt_ready = sem("xt_ready")
        xt_hi_ready = sem("xt_hi_ready")
        xt_lo_ready = sem("xt_lo_ready")
        logits_ready = sem("logits_ready")
        logits_read = sem("logits_read")
        gate_step = sem("gate_step")
        gate_arg_ready = sem("gate_arg_ready")
        gate_exp_ready = sem("gate_exp_ready")
        rw_ready = sem("rw_ready")

        y_ready = [sem("y_ready_v"), sem("y_ready_s")]
        y_added_v = sem("y_added_v")
        y_scaled_s = sem("y_scaled_s")
        y_added_s = sem("y_added_s")
        y_summed = sem("y_summed")
        qkv_ready = sem("qkv_ready")

        proj_ready = sem("proj_ready")
        elu_parts = sem("elu_parts")
        q_ready = sem("q_ready")
        k_ready = sem("k_ready")
        v_ready = sem("v_ready")
        v_spread = sem("v_spread")
        q_groups_ready = sem("q_groups_ready")
        k_places_ready = sem("k_places_ready")
        k_tok_ready = sem("k_tok_ready")
        k_chunks_ready = sem("k_chunks_ready")
        score_ready = sem("score_ready")
        score_masked = sem("score_masked")
        d_ready = sem("d_ready")
        d_masked = sem("d_masked")
        state_ready = sem("state_ready")
        la_ready = sem("la_ready")
        den_step = sem("den_step")
        val_ready = sem("val_ready")
        val_tr_ready = sem("val_tr_ready")
        val_t_ready = sem("val_t_ready")

        wo_added = sem("wo_added")
        qk_tr_ready = sem("qk_tr_ready")
        qk_t_ready = sem("qk_t_ready")
        k_zero_ready = sem("k_zero_ready")
        s_ready = sem("s_ready")
        max_ready = sem("max_ready")
        neg_max_ready = sem("neg_max_ready")
        probs_ready = sem("probs_ready")
        probs_tr_ready = sem("probs_tr_ready")
        probs_t_ready = sem("probs_t_ready")
        attn_ready = sem("attn_ready")
        attn_t_ready = sem("attn_t_ready")
        rwo_step = sem("rwo_step")
        rwo_ready = sem("rwo_ready")
        rwo_tr_ready = sem("rwo_tr_ready")
        rwo_t_ready = sem("rwo_t_ready")
        rwb_ready = sem("rwb_ready")
        mixed_ready = sem("mixed_ready")
        pair_added = sem("pair_added")
        xr_loaded = sem("xr_loaded")
        res_ready = sem("res_ready")
        out_ready = sem("out_ready")
        out_stored = sem("out_stored")

        def passes(body):
            def run(engine):
                body(0, False, True)
                body(1, True, True)
                with engine.Fori(2, B - 1) as b:
                    body(b, True, True)
                body(B - 1, True, False)
            return run

        def x_of(b):
            return x_in[b].rearrange("(i p) d -> p i d", p=P)

        def out_of(b):
            return out[b].rearrange("(i p) d -> p i d", p=P)

        block = ctx.enter_context(nc.Block())

        @block.sync
        def _(sp):
            sp.dma_start(x[:, :, :], x_of(0)).then_inc(x_loaded, 16)
            sp.dma_start(sim[:, :], sim_in).then_inc(gate_loaded, 16)
            sp.dma_start(gates[:, :], gates_in.partition_broadcast(P)).then_inc(gate_loaded, 16)
            for n, w in enumerate((eq_in, ek_in, ev_in)):
                sp.dma_start(stage[:, :, n * HD:(n + 1) * HD],
                             w.rearrange("e c d -> c e d")).then_inc(experts_loaded, 16)
            sp.dma_start(eo[:, :, :], eo_in.rearrange("(p u) d c -> (u d) p c", u=2))\
              .then_inc(out_w_loaded, 16)
            sp.dma_start(wo[:, :], wo_in).then_inc(out_w_loaded, 16)
            sp.dma_start(bo_row[:, :], bo_in.partition_broadcast(P)).then_inc(out_w_loaded, 16)

            def body(b, attn, norm):
                if norm:
                    sp.wait_ge(xn_ready, (b + 1) * NT)
                    sp.dma_start(x[:, :, :], x_of(b + 1)).then_inc(x_loaded, 16)
                if attn:
                    if due(b - 1):
                        sp.wait_ge(res_ready, b - 1)
                    sp.dma_start(x_res[:, :, :], x_of(b - 1)).then_inc(xr_loaded, 16)
                if due(b * NT):
                    sp.wait_ge(la_ready, b * NT)
                sp.wait_ge(v_ready, b + 1)
                for s in range(S4):
                    for j in range(CT):
                        sp.dma_start(v_blocks[C * s:C * s + C, j:NC:CT, s, :, :],
                                     v_ones[C * j:C * j + C, :, s, :, :]).then_inc(v_spread, 16)
                if attn:
                    if due(b):
                        sp.wait_ge(out_ready, b)
                    sp.dma_start(out_of(b - 1), out_sb[:, :, :]).then_inc(out_stored, 16)

            passes(body)(sp)
            sp.wait_ge(res_ready, B - 1)
            sp.dma_start(x_res[:, :, :], x_of(B - 1)).then_inc(xr_loaded, 16)
            sp.wait_ge(out_ready, B)
            sp.dma_start(out_of(B - 1), out_sb[:, :, :]).then_inc(out_stored, 16)
            sp.wait_ge(out_stored, 16 * B)

        @block.gpsimd
        def _(pool):
            g = nc.gpsimd
            g.memset(ident[:, :], 0.0).then_inc(filled, 1)
            g.memset(ones[:, :], 1.0)
            g.memset(half[:, :], 0.5)
            g.memset(half16[:, :], 0.5)
            g.memset(neg_half[:, :], -0.5).then_inc(filled, 1)
            pool.wait_ge(filled, 2)
            g.affine_select(out=ident[:, :], in_=ident[:, :], compare_op=ALU.not_equal,
                            fill=1.0, base=0, pattern=[[-1, P]], channel_multiplier=1)\
             .then_inc(ident_ready, 1)

            def norm_powers(n):
                pool.wait_ge(var_ready, n + 1)
                if due(n * NT):
                    pool.wait_ge(xn_ready, n * NT)
                g.tensor_tensor(rstd[:, :], var_eps[:, :], neg_half[:, :], ALU.pow).then_inc(rstd_ready, 1)
                pool.wait_ge(norm_sq_ready, n + 1)
                g.tensor_tensor(nrm[:, 2, :], nrm[:, 1, :], half[:, :], ALU.pow).then_inc(norm_ready, 1)

            def residual(a):
                pool.wait_ge(xr_loaded, (a + 1) * 16)
                if due(a):
                    pool.wait_ge(out_ready, a)
                pool.wait_ge(out_w_loaded, 16 * 3)
                g.tensor_tensor(res[:, :, :], x_res[:, :, :],
                                bo_row[:, :].unsqueeze(1).broadcast_to([P, NT, D]), ALU.add)\
                 .then_inc(res_ready, 1)

            ADDS = 3

            def y_add(b, first, last):
                for n in range(first, last):
                    i, p = n // PAIRS, n % PAIRS
                    if p % 2 == 0 or p == 1:
                        continue
                    count = i * ADDS + (p - 3) // 2
                    pool.wait_ge(y_scaled_s, (b * NT * (PAIRS // 2) + i * (PAIRS // 2) + p // 2 + 1) * 2)
                    if due(b * NT * ADDS + count):
                        pool.wait_ge(y_added_s, b * NT * ADDS + count)
                    g.tensor_tensor(acc_s[:, i, :, :], acc_s[:, i, :, :],
                                    y_tmp[:, count % TMP, :, :], ALU.add).then_inc(y_added_s, 1)

            def y_finish(b, i):
                pool.wait_ge(y_added_s, b * NT * ADDS + (i + 1) * ADDS)
                pool.wait_ge(y_added_v, (b * NT + i + 1) * PAIRS)
                if due((b * NT) * 2):
                    pool.wait_ge(qkv_ready, (b * NT) * 2)
                g.tensor_tensor(y_sum[:, i, :, :], acc_v[:, i, :, :], acc_s[:, i, :, :], ALU.add)\
                 .then_inc(y_summed, 1)
                pool.wait_ge(y_summed, b * NT + i + 1)
                if due(b):
                    pool.wait_ge(attn_ready, b)
                if due(b):
                    pool.wait_ge(qk_tr_ready, b)
                g.tensor_tensor(qk[:, i, :], y_sum[:, i, 0, 0:2 * HD], y_sum[:, i, 1, 0:2 * HD], ALU.add)\
                 .then_inc(qkv_ready, 1)
                g.tensor_tensor(v_dup[:, i, :, :],
                                y_sum[:, i, 0, 2 * HD:W3].unsqueeze(1).broadcast_to([P, 2, HD]),
                                y_sum[:, i, 1, 2 * HD:W3].unsqueeze(1).broadcast_to([P, 2, HD]), ALU.add)\
                 .then_inc(qkv_ready, 1)

            def state_add(b, first, last):
                for c in range(first, last):
                    pool.wait_ge(d_masked, b * ND + c // DB + 1)
                    if c == 0:
                        if due(b * NT):
                            pool.wait_ge(la_ready, b * NT)
                    else:
                        if due(b * (NC - 1) + c):
                            pool.wait_ge(state_ready, b * (NC - 1) + c)
                    g.tensor_tensor(state[:, c + 1, :], state[:, c, :], d_state[:, c, :], ALU.add)\
                     .then_inc(state_ready, 1)

            norm_powers(0)
            pool.wait_ge(sim_norm_read, 1)
            g.tensor_tensor(sim_r[:, 1, :], sim_r[:, 0, :], half16[:, :], ALU.pow).then_inc(sim_root, 1)
            for e in range(E):
                g.memset(rank[:, e:e + 1], float(E - e))
            for t in (past, place_mask, block_mask):
                g.memset(t[:, :], 1.0)
            g.memset(v_ones[:, :, :, :, :], 1.0)
            g.memset(pair_sel[:, :, :, :], 0.0)
            g.memset(q_groups[:, :, :, :], 0.0)
            g.memset(state[:, 0, :], 0.0)
            g.memset(future_bf[:, :], 0.0).then_inc(filled, 1)
            pool.wait_ge(filled, 3)
            pool.wait_ge(ident_ready, 1)
            consts = Chain(pool, const_step, 19, 0)
            consts.step(g.tensor_copy(ident_bf[:, :], ident[:, :]))
            consts.step(g.affine_select(out=future_bf[:, :], in_=future_bf[:, :], compare_op=ALU.is_ge,
                                        fill=-BIG, base=0, pattern=[[-1, P]], channel_multiplier=1))
            for s in range(S4):
                rows = slice(C * s, C * s + C)
                consts.step(g.affine_select(out=past[rows, :], in_=past[rows, :], compare_op=ALU.is_ge,
                                            fill=0.0, base=0, pattern=[[1, C]], channel_multiplier=-1))
            view = block_mask[:, :].rearrange("p (s g m) -> p s g m", s=S4, g=G)
            for side, base in ((1, 0), (-1, M - 1)):
                for s in range(S4):
                    rows = slice(C * s, C * s + C)
                    consts.step(g.affine_select(out=place_mask[rows, :], in_=place_mask[rows, :],
                                                compare_op=ALU.is_ge, fill=0.0, base=base,
                                                pattern=[[-side * M, S4]], channel_multiplier=side))
                consts.step(g.affine_select(out=view, in_=view, compare_op=ALU.is_ge, fill=0.0, base=base,
                                            pattern=[[-side * M, S4], [-side * M * S4, G], [0, M1]],
                                            channel_multiplier=side))
            for part in range(3):
                consts.step(g.affine_select(out=pair_sel[:, :, :, :], in_=pair_sel[:, :, :, :],
                                            compare_op=ALU.not_equal, fill=1.0, base=-E * part,
                                            pattern=[[-2, PAIRS], [-1, 2], [0, HD]],
                                            channel_multiplier=1))
            consts.end()
            g.memset(y_sum[:, 0, 0, 0:1], 0.0).then_inc(const_ready, 1)

            def body(b, attn, norm):
                if attn:
                    residual(b - 1)
                y_add(b, 0, 12)
                state_add(b, 0, 3)
                y_add(b, 12, 16)
                state_add(b, 3, 6)
                if norm:
                    norm_powers(b + 1)
                state_add(b, 6, 9)
                y_add(b, 16, 20)
                state_add(b, 9, 12)
                y_add(b, 20, 22)
                state_add(b, 12, 15)
                y_add(b, 22, 24)
                y_finish(b, 0)
                y_add(b, 24, 28)
                y_finish(b, 1)
                y_add(b, 28, 30)
                y_finish(b, 2)
                y_add(b, 30, 32)
                y_finish(b, 3)

            passes(body)(pool)
            residual(B - 1)

        @block.scalar
        def _(act):
            a_ = nc.scalar
            act.dma_start(lin_w[:, 0, :], wq_in).then_inc(lin_loaded, 16)
            act.dma_start(lin_w[:, 1, :], wk_in).then_inc(lin_loaded, 16)
            act.dma_start(wv_raw[:, :], wv_in).then_inc(lin_loaded, 16)
            act.dma_start(bqk[:, 0:1], bq_in.rearrange("(p a) -> p a", a=1)).then_inc(lin_loaded, 16)
            act.dma_start(bqk[:, 1:2], bk_in.rearrange("(p a) -> p a", a=1)).then_inc(lin_loaded, 16)
            act.dma_start(bv_raw[:, :], bv_in.partition_broadcast(P)).then_inc(lin_loaded, 16)
            act.wait_ge(gate_loaded, 16 * 2)
            a_.activation(sig[:, 0, :], gates[:, :], ACT.Exp, scale=-1.0).then_inc(gates_exp, 1)

            def xt_high(n):
                act.wait_ge(xt_ready, n + 1)
                if due(n * YN // 2):
                    act.wait_ge(y_ready[0], n * YN // 2)
                if due(n * YN // 2):
                    act.wait_ge(y_ready[1], n * YN // 2)
                if due(n):
                    act.wait_ge(logits_ready, n)
                a_.activation(xt_hi[:, :], g_ps[4][:, :], ACT.Copy).then_inc(xt_hi_ready, 1)

            def gate_exp(n):
                act.wait_ge(gate_arg_ready, n + 1)
                a_.activation(gexp[:, :, :], gate_sb[:, 10, :, :], ACT.Exp).then_inc(gate_exp_ready, 1)

            def y_scale(b, first, last):
                for n in range(first, last):
                    i, p = n // PAIRS, n % PAIRS
                    if p % 2 == 0:
                        continue
                    act.wait_ge(rw_ready, b + 1)
                    act.wait_ge(y_ready[1], b * YN // 2 + n // 2 + 1)
                    count = i * 3 + (p - 3) // 2
                    if p == 1:
                        if due((b - 1) * NT + i + 1):
                            act.wait_ge(y_summed, (b - 1) * NT + i + 1)
                    else:
                        if due(b * NT * 3 + count - TMP + 1):
                            act.wait_ge(y_added_s, b * NT * 3 + count - TMP + 1)
                    for u in range(2):
                        dst = acc_s[:, i, u, :] if p == 1 else y_tmp[:, count % TMP, u, :]
                        a_.activation(dst, y_view[1][:, u * W3:(u + 1) * W3], ACT.Copy,
                                      scale=rw[:, i, 2 * p + u:2 * p + u + 1]).then_inc(y_scaled_s, 1)

            def elu_pieces(b):
                for n in range(2):
                    act.wait_ge(proj_ready, b * 3 + n + 1)
                    if due(b):
                        act.wait_ge((q_ready, k_ready)[n], b)
                    a_.activation(elu_e[:, n, :], g_ps[2 + n][:, :], ACT.Exp, bias=bqk[:, n:n + 1])\
                      .then_inc(elu_parts, 1)
                    a_.activation(elu_r[:, n, :], g_ps[2 + n][:, :], ACT.Relu, bias=bqk[:, n:n + 1])\
                      .then_inc(elu_parts, 1)

            def group_q(b):
                act.wait_ge(q_ready, b + 1)
                if due(b * NT):
                    act.wait_ge(score_ready, b * NT)
                for g in range(G):
                    rows = slice(C * g, C * g + C)
                    a_.activation(q_groups[rows, :, g, :],
                                  q_t[rows, :].rearrange("p (c t) -> p c t", t=C), ACT.Copy)\
                      .then_inc(q_groups_ready, 1)

            def chunk_k(b):
                act.wait_ge(k_tok_ready, b + 1)
                if due(b * ND):
                    act.wait_ge(d_ready, b * ND)
                for j in range(CT):
                    rows = slice(C * j, C * j + C)
                    a_.activation(k_chunks[rows, j, :, :],
                                  g_ps[2][rows, :].rearrange("p (i f) -> p i f", f=D), ACT.Copy)\
                      .then_inc(k_chunks_ready, 1)

            def soft_exp(a, i):
                act.wait_ge(neg_max_ready, a * NT + i + 1)
                if due(a * NT):
                    act.wait_ge(probs_tr_ready, a * NT)
                if due(a):
                    act.wait_ge(rwo_ready, a)
                n = (i + 1) * P
                a_.activation(probs[:, i, 0:n], g_ps[i % 2][:, 0:n], ACT.Exp, bias=neg_max[:, i:i + 1],
                              scale=SCALE, accum_out=ssum[:, i:i + 1]).then_inc(probs_ready, 1)

            def probs_out(a, i):
                act.wait_ge(probs_tr_ready, a * NT + i + 1)
                if due(a):
                    act.wait_ge(attn_ready, a)
                a_.activation(probs_t[:, 0:i + 1, i * P:(i + 1) * P],
                              g_ps[i % 2][:, 0:(i + 1) * P].rearrange("p (k q) -> p k q", q=P), ACT.Copy)\
                  .then_inc(probs_t_ready, 1)

            def qk_out(a):
                act.wait_ge(qk_tr_ready, a + 1)
                if due(a):
                    act.wait_ge(s_ready, a * NT)
                a_.activation(qk_t[:, :], g_ps[0][:, :], ACT.Copy).then_inc(qk_t_ready, 1)

            def attn_out(a):
                act.wait_ge(attn_ready, a + 1)
                if due(a):
                    act.wait_ge(mixed_ready, a * PAIRS)
                a_.activation(attn_t[:, :], g_ps[0][:, :], ACT.Copy).then_inc(attn_t_ready, 1)
                act.wait_ge(rwo_tr_ready, a + 1)
                if due(a):
                    act.wait_ge(rwb_ready, a * PAIRS)
                a_.activation(rwo_t[:, :], g_ps[1].bitcast(BF16)[:, 0:T], ACT.Copy)\
                  .then_inc(rwo_t_ready, 1)

            def val_out(b):
                act.wait_ge(val_tr_ready, b + 1)
                if due(b):
                    act.wait_ge(wo_added, b)
                a_.activation(val_t[:, :], g_ps[2][:, :], ACT.Copy).then_inc(val_t_ready, 1)

            xt_high(0)
            act.wait_ge(experts_loaded, 16 * 3)
            a_.activation(w3_hi[:, :, :], stage[:, :, :], ACT.Copy).then_inc(w3_hi_ready, 1)
            gate_exp(0)
            act.wait_ge(lin_loaded, 16 * 6)
            act.wait_ge(const_ready, 1)

            def body(b, attn, norm):
                if attn:
                    qk_out(b - 1)
                y_scale(b, 0, 2)
                elu_pieces(b)
                y_scale(b, 2, 4)
                group_q(b)
                if attn:
                    soft_exp(b - 1, 0)
                    soft_exp(b - 1, 1)
                y_scale(b, 4, 6)
                chunk_k(b)
                y_scale(b, 6, 8)
                if attn:
                    soft_exp(b - 1, 2)
                y_scale(b, 8, 10)
                if attn:
                    soft_exp(b - 1, 3)
                y_scale(b, 10, 12)
                if attn:
                    probs_out(b - 1, 0)
                y_scale(b, 12, 14)
                if attn:
                    probs_out(b - 1, 1)
                y_scale(b, 14, 16)
                if attn:
                    probs_out(b - 1, 2)
                    probs_out(b - 1, 3)
                y_scale(b, 16, 18)
                if attn:
                    attn_out(b - 1)
                y_scale(b, 18, 30)
                val_out(b)
                y_scale(b, 30, 32)
                if norm:
                    xt_high(b + 1)
                    gate_exp(b + 1)

            passes(body)(act)
            a = B - 1
            qk_out(a)
            for i in range(NT):
                soft_exp(a, i)
            for i in range(NT):
                probs_out(a, i)
            attn_out(a)

        @block.vector
        def _(dve):
            v = nc.vector
            def variance(n):
                st = Chain(dve, stats_step, STATS, n)
                dve.wait_ge(x_loaded, (n + 1) * 16)
                for i in range(NT):
                    last = v.bn_stats(stats[:, i, :], x[:, i, :])
                st.step(last)
                v.memset(wait_pad[:, :], 0.0)
                for i in range(NT):
                    last = v.bn_aggr(mv[:, i, :], stats[:, i, :])
                st.step(last)
                v.tensor_scalar(var_eps[:, :], mv[:, :, 1], LN_EPS, None, ALU.add).then_inc(var_ready, 1)
                return st

            def normalise(n, st):
                dve.wait_ge(rstd_ready, n + 1)
                st.step(v.tensor_tensor(nrm[:, 0, :], mv[:, :, 1], rstd[:, :], ALU.mult))
                st.step(v.tensor_tensor(nrm[:, 4, :], nrm[:, 0, :], rstd[:, :], ALU.mult))
                v.tensor_scalar(nrm[:, 1, :], nrm[:, 4, :], float(D), None, ALU.mult)\
                 .then_inc(norm_sq_ready, 1)
                if due(n):
                    dve.wait_ge(xt_ready, n)
                for i in range(NT):
                    v.tensor_scalar(xn[:, i, :], x[:, i, :], mv[:, i, 0:1], rstd[:, i:i + 1],
                                    ALU.subtract, ALU.mult).then_inc(xn_ready, 1)
                dve.wait_ge(norm_ready, n + 1)
                st.step(v.tensor_scalar(nrm[:, 0, :], nrm[:, 2, :], NORM_EPS, None, ALU.max))
                st.step(v.reciprocal(nrm[:, 3, :], nrm[:, 0, :]))
                st.end()

            STATS = 6

            def xt_low(n):
                dve.wait_ge(xt_hi_ready, n + 1)
                v.tensor_tensor(xt_lo[:, :], g_ps[4][:, :], xt_hi[:, :], ALU.subtract)\
                 .then_inc(xt_lo_ready, 1)

            GATES = 19

            def over_e(t):
                return t.unsqueeze(2).broadcast_to([P, NT, E])

            def over_i(t):
                return t.unsqueeze(1).broadcast_to([P, NT, E])

            top, top_relu, top_rank, second, second_rank, idle, total, inv = \
                (gmax[:, k, :] for k in range(8))
            logits = logit[:, 1, :, :]
            below, ranked, first, rest, below2, ranked2, both, fallback, active, weight = \
                (gate_sb[:, k, :, :] for k in range(10))

            def gate_logits(n):
                st = Chain(dve, gate_step, GATES, n)
                dve.wait_ge(logits_ready, n + 1)
                v.tensor_tensor(logit[:, 0, :, :], g_ps[2][:, 0:NT * E].rearrange("p (i e) -> p i e", e=E),
                                over_e(nrm[:, 3, :]), ALU.mult).then_inc(logits_read, 1)
                dve.wait_ge(logits_read, n + 1)
                st.step(v.tensor_tensor(logits, logit[:, 0, :, :], over_i(sigmoid[:, :]), ALU.subtract))
                st.step(v.tensor_reduce(top, logits, AX.X, ALU.max))
                st.step(v.tensor_scalar(top_relu, top, 0.0, None, ALU.max))
                v.scalar_tensor_tensor(out=gate_sb[:, 10, :, :], in0=logits, scalar=0.0, in1=over_e(top_relu),
                                       op0=ALU.max, op1=ALU.subtract).then_inc(gate_arg_ready, 1)
                return st

            def gate_first(st):
                st.step(v.tensor_tensor(below, logits, over_e(top), ALU.subtract))
                st.step(v.scalar_tensor_tensor(out=ranked, in0=below, scalar=0.0, in1=over_i(rank[:, :]),
                                               op0=ALU.is_ge, op1=ALU.mult))
                st.step(v.tensor_reduce(top_rank, ranked, AX.X, ALU.max))
                st.step(v.tensor_tensor(first, ranked, over_e(top_rank), ALU.is_ge))

            def gate_second(st):
                st.step(v.scalar_tensor_tensor(out=rest, in0=first, scalar=-BIG, in1=logits,
                                               op0=ALU.mult, op1=ALU.add))
                st.step(v.tensor_reduce(second, rest, AX.X, ALU.max))
                st.step(v.tensor_tensor(below2, rest, over_e(second), ALU.subtract))
                st.step(v.scalar_tensor_tensor(out=ranked2, in0=below2, scalar=0.0, in1=over_i(rank[:, :]),
                                               op0=ALU.is_ge, op1=ALU.mult))

            def gate_weights(n):
                st = Chain(dve, gate_step, GATES, n)
                st.n = 11
                st.step(v.tensor_reduce(second_rank, ranked2, AX.X, ALU.max))
                st.step(v.tensor_tensor(both, ranked2, over_e(second_rank), ALU.is_ge))
                v.tensor_scalar(idle, top, 0.0, None, ALU.is_le)
                st.step(v.tensor_tensor(both, both, first, ALU.add))
                st.step(v.tensor_tensor(fallback, both, over_e(idle), ALU.mult))
                st.step(v.scalar_tensor_tensor(out=active, in0=logits, scalar=0.0, in1=fallback,
                                               op0=ALU.is_gt, op1=ALU.add))
                dve.wait_ge(gate_exp_ready, n + 1)
                st.step(v.tensor_tensor(weight, gexp[:, :, :], active, ALU.mult))
                st.step(v.tensor_reduce(total, weight, AX.X, ALU.add))
                if due(n):
                    v.tensor_copy(rw_prev[:, :, :], rw[:, :, :])
                st.step(v.reciprocal(inv, total))
                if due(n):
                    dve.wait_ge(y_scaled_s, n * YN)
                v.tensor_tensor(rw[:, :, :], weight, over_e(inv), ALU.mult).then_inc(rw_ready, 1)
                dve.wait_ge(rw_ready, n + 1)
                st.end()

            def y_add(b, first, last):
                for n in range(first, last):
                    i, p = n // PAIRS, n % PAIRS
                    if p % 2:
                        continue
                    dve.wait_ge(y_ready[0], b * YN // 2 + n // 2 + 1)
                    if p == 0:
                        if due((b - 1) * NT + i + 1):
                            dve.wait_ge(y_summed, (b - 1) * NT + i + 1)
                    for u in range(2):
                        e = 2 * p + u
                        y = y_view[0][:, u * W3:(u + 1) * W3]
                        if p == 0:
                            v.tensor_scalar(acc_v[:, i, u, :], y, rw[:, i, e:e + 1], None, ALU.mult)\
                             .then_inc(y_added_v, 1)
                        else:
                            if due(b * YN + n + u - 1):
                                dve.wait_ge(y_added_v, b * YN + n + u - 1)
                            v.scalar_tensor_tensor(out=acc_v[:, i, u, :], in0=y, scalar=rw[:, i, e:e + 1],
                                                   in1=acc_v[:, i, u, :], op0=ALU.mult, op1=ALU.add)\
                             .then_inc(y_added_v, 1)

            def values(b):
                dve.wait_ge(proj_ready, b * 3 + 3)
                if due(16 * 16 * b):
                    dve.wait_ge(v_spread, 16 * 16 * b)
                if due(ND * b):
                    dve.wait_ge(d_ready, ND * b)
                v.tensor_tensor(v_ones[:, :, :, :, 0:M].rearrange("p i s g m -> p (i s g) m"),
                                g_ps[4][:, :].rearrange("p (a m) -> p a m", m=M),
                                bv_row[:, :].unsqueeze(1).broadcast_to([P, NT, D]), ALU.add)\
                 .then_inc(v_ready, 1)

            def elu(b):
                for n, (dst, ready) in enumerate(((q_t, q_ready), (k_t, k_ready))):
                    dve.wait_ge(elu_parts, b * 4 + 2 * n + 2)
                    if n == 0:
                        if due(b * NT):
                            dve.wait_ge(la_ready, b * NT)
                        if due(b * G):
                            dve.wait_ge(q_groups_ready, b * G)
                    else:
                        if due(b):
                            dve.wait_ge(k_tok_ready, b)
                        if due(b * S4):
                            dve.wait_ge(k_places_ready, b * S4)
                    v.scalar_tensor_tensor(out=dst[:, :], in0=elu_e[:, n, :], scalar=1.0, in1=elu_r[:, n, :],
                                           op0=ALU.min, op1=ALU.add).then_inc(ready, 1)

            def place_k(b):
                dve.wait_ge(k_ready, b + 1)
                if due(b * NT):
                    dve.wait_ge(score_ready, b * NT)
                for s in range(S4):
                    v.tensor_scalar(k_places[:, :, s, :], k_t[:, :].rearrange("p (c t) -> p c t", t=C),
                                    place_mask[:, s:s + 1], None, ALU.mult).then_inc(k_places_ready, 1)

            def mask_scores(b, i):
                dve.wait_ge(score_ready, b * NT + i + 1)
                if due((b - 1) * NT + i + 1):
                    dve.wait_ge(la_ready, (b - 1) * NT + i + 1)
                v.tensor_tensor(scores[:, i, :].rearrange("p (a q) -> p a q", q=C),
                                g_ps[3 + i % 2][:, :].rearrange("p (a q) -> p a q", q=C),
                                past[:, :].unsqueeze(1).broadcast_to([P, CT * G, C]), ALU.mult)\
                 .then_inc(score_masked, 1)

            def mask_states(b, n):
                dve.wait_ge(d_ready, b * ND + n + 1)
                if due(b * (NC - 1)):
                    dve.wait_ge(state_ready, b * (NC - 1))
                v.tensor_tensor(d_state[:, n * DB:(n + 1) * DB, :],
                                g_ps[2 + n % 2][:, 0:DB * VW].rearrange("p (a w) -> p a w", w=VW),
                                block_mask[:, :].unsqueeze(1).broadcast_to([P, DB, VW]), ALU.mult)\
                 .then_inc(d_masked, 1)

            def la_values(b, n):
                st = Chain(dve, den_step, 2, b * 2 + n)
                o = g_ps[(4, 3)[n]][:, 0:2 * VW].rearrange("p (a m) -> p a m", m=M1)
                dve.wait_ge(la_ready, b * NT + 2 * n + 2)
                if due(b):
                    dve.wait_ge(val_tr_ready, b)
                st.step(v.tensor_scalar(den[:, n, 0, :].unsqueeze(2), o[:, :, M:M1], DEN_EPS, None, ALU.add))
                st.step(v.reciprocal(den[:, n, 1, :], den[:, n, 0, :]))
                v.tensor_tensor(val[:, 2 * n:2 * n + 2, :].rearrange("p i (a m) -> p (i a) m", m=M),
                                o[:, :, 0:M], den[:, n, 1, :].unsqueeze(2).broadcast_to([P, 2 * H, M]),
                                ALU.mult).then_inc(val_ready, 1)

            def k_out(a):
                dve.wait_ge(qk_tr_ready, a + 1)
                if due(a * NT):
                    dve.wait_ge(s_ready, a * NT)
                v.tensor_copy(k_zero[0:HD, :], g_ps[1][0:HD, :]).then_inc(k_zero_ready, 1)

            def row_max(a, i):
                dve.wait_ge(s_ready, a * NT + i + 1)
                if due(a * NT):
                    dve.wait_ge(neg_max_ready, a * NT)
                v.tensor_reduce(smax[:, i:i + 1], g_ps[i % 2][:, 0:(i + 1) * P], AX.X, ALU.max)\
                 .then_inc(max_ready, 1)
                dve.wait_ge(max_ready, a * NT + i + 1)
                if due(a * NT):
                    dve.wait_ge(probs_ready, a * NT)
                v.tensor_scalar(neg_max[:, i:i + 1], smax[:, i:i + 1], -SCALE, None, ALU.mult)\
                 .then_inc(neg_max_ready, 1)

            def output_weights(a):
                st = Chain(dve, rwo_step, 5, a)
                dve.wait_ge(probs_ready, (a + 1) * NT)
                if due(a):
                    dve.wait_ge(rwo_tr_ready, a)
                st.step(v.reciprocal(srec[:, :], ssum[:, :]))
                st.step(v.tensor_tensor(rwo[:, 0, :, :], rw_prev[:, :, :] if a is not None else None,
                                        over_e(srec[:, :]), ALU.mult))
                st.step(v.tensor_copy(rwo_parts[:, :, 0:E], rwo[:, 0, :, :]))
                st.step(v.tensor_tensor(rwo[:, 1, :, :], rwo[:, 0, :, :], rwo_parts[:, :, 0:E], ALU.subtract))
                st.step(v.tensor_copy(rwo_parts[:, :, E:2 * E], rwo[:, 1, :, :]))
                v.tensor_tensor(rwo_parts[:, :, 2 * E:3 * E], rwo[:, 1, :, :], rwo_parts[:, :, E:2 * E],
                                ALU.subtract).then_inc(rwo_ready, 1)
                st.end()

            def mix(a, p):
                dve.wait_ge(rwb_ready, a * PAIRS + p + 1)
                dve.wait_ge(attn_t_ready, a + 1)
                if due(a * PAIRS + max(p - 1, 0)):
                    dve.wait_ge(pair_added, a * PAIRS + max(p - 1, 0))
                v.tensor_tensor(mixed[:, p % 2, :], g_ps[p % 2][:, :], attn_t[:, :], ALU.mult)\
                 .then_inc(mixed_ready, 1)

            def finish(a):
                dve.wait_ge(pair_added, (a + 1) * PAIRS)
                dve.wait_ge(res_ready, a + 1)
                if due(a * 16):
                    dve.wait_ge(out_stored, a * 16)
                v.tensor_tensor(out_sb[:, :, :], out_ps[:, :, :], res[:, :, :], ALU.add)\
                 .then_inc(out_ready, 1)

            st = variance(0)
            dve.wait_ge(gate_loaded, 16 * 2)
            consts = Chain(dve, dve_const_step, 12, 0)
            consts.step(v.tensor_tensor(sim_sq[:, :], sim[:, :], sim[:, :], ALU.mult))
            normalise(0, st)
            dve.wait_ge(sim_norm, 1)
            v.tensor_copy(sim_r[:, 0, :], g_ps[0][:, 0:E]).then_inc(sim_norm_read, 1)
            dve.wait_ge(gates_exp, 1)
            consts.step(v.tensor_scalar(sig[:, 1, :], sig[:, 0, :], 1.0, None, ALU.add))
            consts.step(v.reciprocal(sigmoid[:, :], sig[:, 1, :]))
            dve.wait_ge(sim_root, 1)
            consts.step(v.tensor_scalar(sim_r[:, 2, :], sim_r[:, 1, :], NORM_EPS, None, ALU.max))
            consts.step(v.reciprocal(sim_r[:, 3, :], sim_r[:, 2, :]))
            consts.step(v.tensor_tensor(sim_r[:, 0, :], sim[:, :], sim_r[:, 3, :], ALU.mult))
            consts.step(v.tensor_copy(sim_hi[:, :], sim_r[:, 0, :]))
            v.tensor_tensor(sim_lo[:, :], sim_r[:, 0, :], sim_hi[:, :], ALU.subtract).then_inc(sim_ready, 1)
            xt_low(0)
            dve.wait_ge(lin_loaded, 16 * 6)
            by_place = "p (g s m) -> p s g m"
            consts.step(v.tensor_copy(lin_w[:, 2, :].rearrange("p (s g m) -> p s g m", g=G, m=M),
                                      wv_raw[:, :].rearrange(by_place, g=G, m=M)))
            consts.step(v.tensor_copy(bv_row[:, :].rearrange("p (s g m) -> p s g m", g=G, m=M),
                                      bv_raw[:, :].rearrange(by_place, g=G, m=M)))
            consts.step(v.tensor_copy(lin_hi[:, :, :], lin_w[:, :, :]))
            v.tensor_tensor(lin_lo[:, :, :], lin_w[:, :, :], lin_hi[:, :, :], ALU.subtract)\
             .then_inc(lin_ready, 1)
            for t in (k_chunks, v_blocks, rwo_parts):
                v.memset(t[tuple(slice(None) for _ in t.shape)], 0.0)
            consts.step(v.memset(k_zero[HD:P, :], 0.0))
            dve.wait_ge(const_ready, 1)
            gate = gate_logits(0)
            gate_first(gate)
            gate_second(gate)
            dve.wait_ge(w3_hi_ready, 1)
            v.tensor_tensor(w3_lo[:, :, :], stage[:, :, :], w3_hi[:, :, :], ALU.subtract)\
             .then_inc(w3_ready, 1)
            consts.step(v.memset(wait_pad[:, :], 0.0))
            consts.end()

            def body(b, attn, norm):
                if attn:
                    k_out(b - 1)
                gate_weights(b)
                y_add(b, 0, 2)
                values(b)
                if attn:
                    row_max(b - 1, 0)
                    row_max(b - 1, 1)
                elu(b)
                y_add(b, 2, 4)
                place_k(b)
                y_add(b, 4, 6)
                if attn:
                    row_max(b - 1, 2)
                y_add(b, 6, 8)
                mask_scores(b, 0)
                y_add(b, 8, 10)
                mask_scores(b, 1)
                if attn:
                    row_max(b - 1, 3)
                y_add(b, 10, 12)
                mask_states(b, 0)
                mask_scores(b, 2)
                y_add(b, 12, 14)
                mask_scores(b, 3)
                mask_states(b, 1)
                if norm:
                    st = variance(b + 1)
                y_add(b, 14, 16)
                mask_states(b, 2)
                if attn:
                    output_weights(b - 1)
                y_add(b, 16, 18)
                mask_states(b, 3)
                if norm:
                    normalise(b + 1, st)
                y_add(b, 18, 20)
                mask_states(b, 4)
                if attn:
                    mix(b - 1, 0)
                    mix(b - 1, 1)
                y_add(b, 20, 22)
                y_add(b, 22, 24)
                la_values(b, 0)
                if attn:
                    mix(b - 1, 2)
                y_add(b, 24, 26)
                if attn:
                    mix(b - 1, 3)
                la_values(b, 1)
                y_add(b, 26, 28)
                if attn:
                    mix(b - 1, 4)
                y_add(b, 28, 30)
                if attn:
                    mix(b - 1, 5)
                y_add(b, 30, 32)
                if attn:
                    mix(b - 1, 6)
                if norm:
                    xt_low(b + 1)
                if attn:
                    mix(b - 1, 7)
                if norm:
                    gate = gate_logits(b + 1)
                    gate_first(gate)
                if attn:
                    finish(b - 1)
                if norm:
                    gate_second(gate)

            passes(body)(dve)
            a = B - 1
            v.tensor_copy(rw_prev[:, :, :], rw[:, :, :]).then_inc(rw_ready, 1)
            dve.wait_ge(rw_ready, B + 1)
            k_out(a)
            for i in range(NT):
                row_max(a, i)
            output_weights(a)
            for p in range(PAIRS):
                mix(a, p)
            finish(a)

        @block.tensor
        def _(pe):
            t_ = nc.tensor

            def product(dst, lhs, rhs, done=None, start=True):
                (lh, ll), (rh, rl) = lhs, rhs
                t_.matmul(dst, lh, rh, start=start, stop=False)
                t_.matmul(dst, lh, rl, start=False, stop=False)
                last = t_.matmul(dst, ll, rh, start=False, stop=True)
                if done is not None:
                    last.then_inc(done, 1)

            pe.wait_ge(ident_ready, 1)
            pe.wait_ge(dve_const_step, 1)
            t_.matmul(g_ps[0][:, 0:E], ones[:, :], sim_sq[:, :], start=True, stop=True).then_inc(sim_norm, 1)

            def tile(t, i):
                return t[:, i * P:(i + 1) * P]

            def xn_transpose(n):
                pe.wait_ge(xn_ready, (n + 1) * NT)
                if due(n * 2 - 1):
                    pe.wait_ge(val_ready, n * 2 - 1)
                for i in range(NT):
                    last = t_.transpose(tile(g_ps[4], i), xn[:, i, :], ident[:, :])
                last.then_inc(xt_ready, 1)

            def gate_logits(n):
                pe.wait_ge(xt_lo_ready, n + 1)
                if due(n):
                    pe.wait_ge(val_t_ready, n)
                for i in range(NT):
                    product(g_ps[2][:, i * E:(i + 1) * E], (tile(xt_hi, i), tile(xt_lo, i)),
                            (sim_hi[:, :], sim_lo[:, :]), logits_ready if i == NT - 1 else None)

            def y_pairs(b, first, last):
                for n in range(first, last):
                    i, p = n // PAIRS, n % PAIRS
                    if n % 2 == 0:
                        if due(b * YN + n):
                            pe.wait_ge(y_added_v, b * YN + n)
                    else:
                        if due(b * YN + n - 1):
                            pe.wait_ge(y_scaled_s, b * YN + n - 1)
                    cols = slice(2 * p, 2 * p + 2)
                    product(y_view[n % 2], (tile(xt_hi, i), tile(xt_lo, i)),
                            (w3_hi[:, cols, :].rearrange("p a b -> p (a b)"),
                             w3_lo[:, cols, :].rearrange("p a b -> p (a b)")), y_ready[n % 2])

            def projections(b):
                pe.wait_ge(logits_read, b + 1)
                for n in range(2):
                    if n == 1:
                        if due(b * 2):
                            pe.wait_ge(val_ready, b * 2)
                    product(g_ps[2 + n][:, :], (lin_hi[:, n, :], lin_lo[:, n, :]),
                            (xt_hi[:, :], xt_lo[:, :]), proj_ready)
                pe.wait_ge(xt_lo_ready, b + 1)
                for i in range(NT):
                    product(tile(g_ps[4], i), (tile(xt_hi, i), tile(xt_lo, i)),
                            (lin_hi[:, 2, :], lin_lo[:, 2, :]), proj_ready if i == NT - 1 else None)

            def k_to_tokens(b):
                pe.wait_ge(k_ready, b + 1)
                pe.wait_ge(elu_parts, b * 4 + 2)
                for i in range(NT):
                    last = t_.transpose(tile(g_ps[2], i), tile(k_t, i), ident[:, :])
                last.then_inc(k_tok_ready, 1)

            def score(b, i):
                pe.wait_ge(k_places_ready, (b + 1) * S4)
                pe.wait_ge(q_groups_ready, (b + 1) * G)
                if i == 0:
                    pe.wait_ge(elu_parts, b * 4 + 4)
                elif i == 1:
                    pe.wait_ge(v_ready, b + 1)
                else:
                    if due(b * NT + i - 1):
                        pe.wait_ge(score_masked, b * NT + i - 1)
                for j in range(CT):
                    c = i * CT + j
                    last = t_.matmul(tile(g_ps[3 + i % 2], j),
                                     k_places[:, c, :, :].rearrange("p s t -> p (s t)"),
                                     q_groups[:, c, :, :].rearrange("p g t -> p (g t)"), start=True, stop=True)
                last.then_inc(score_ready, 1)

            def chunk_states(b, n):
                if n == 0:
                    pe.wait_ge(k_chunks_ready, (b + 1) * CT)
                    pe.wait_ge(v_ready, b + 1)
                elif n == 1:
                    pe.wait_ge(score_masked, b * NT + 3)
                else:
                    if due(b * ND + n - 1):
                        pe.wait_ge(d_masked, b * ND + n - 1)
                for m in range(DB):
                    c = n * DB + m
                    i, j = c // CT, c % CT
                    last = t_.matmul(g_ps[2 + n % 2][:, m * VW:(m + 1) * VW], k_chunks[:, j, i, :],
                                     v_ones[:, i, :, :, :].rearrange("p s g m -> p (s g m)"),
                                     start=True, stop=True)
                last.then_inc(d_ready, 1)

            def la_tile(b, i):
                pe.wait_ge(v_spread, 16 * 16 * (b + 1))
                pe.wait_ge(state_ready, b * (NC - 1) + min(i * CT + CT - 1, NC - 1))
                if i == 0:
                    pe.wait_ge(score_masked, (b + 1) * NT)
                if i == 2:
                    pe.wait_ge(d_masked, b * ND + 4)
                bank = g_ps[(4, 3)[i // 2]]
                o = bank[:, (i % 2) * VW:(i % 2 + 1) * VW]
                for j in range(CT):
                    c = i * CT + j
                    t_.matmul(o[C * j:C * j + C, :], q_t[:, c * C:(c + 1) * C],
                              state[:, c, :].rearrange("p (s g m) -> p g s m", s=S4, g=G),
                              start=True, stop=False, skip_group_check=True)
                for g in range(G):
                    for j in range(CT):
                        c = i * CT + j
                        last = t_.matmul(o[C * j:C * j + C, g * S4 * M1:(g + 1) * S4 * M1],
                                         scores[:, i, (j * G + g) * C:(j * G + g + 1) * C],
                                         v_blocks[:, c, :, g, :], start=False, stop=(g == G - 1),
                                         skip_group_check=True)
                last.then_inc(la_ready, 1)

            def val_transpose(b):
                pe.wait_ge(val_ready, (b + 1) * 2)
                pe.wait_ge(d_masked, (b + 1) * ND)
                for i in range(NT):
                    last = t_.transpose(tile(g_ps[2], i), val[:, i, :], ident[:, :])
                last.then_inc(val_tr_ready, 1)

            def start_output(a):
                pe.wait_ge(val_t_ready, a + 1)
                if due(a):
                    pe.wait_ge(out_ready, a)
                for i in range(NT):
                    last = t_.matmul(out_ps[:, i, :], tile(val_t, i), wo[:, :], start=(i == 0), stop=False,
                                     skip_group_check=True)
                last.then_inc(wo_added, 1)

            def qk_transpose(a):
                pe.wait_ge(qkv_ready, (a + 1) * NT * 2)
                if due(a * PAIRS):
                    pe.wait_ge(mixed_ready, a * PAIRS)
                for i in range(NT):
                    t_.transpose(tile(g_ps[0], i), qk[:, i, :], ident[:, :])
                    last = t_.transpose(g_ps[1][0:HD, i * P:(i + 1) * P], qk[:, i, HD:2 * HD], ident[:, :])
                last.then_inc(qk_tr_ready, 1)

            def soft_scores(a, i):
                pe.wait_ge(qk_t_ready, a + 1)
                pe.wait_ge(k_zero_ready, a + 1)
                if i >= 2:
                    if due(a * NT + i - 1):
                        pe.wait_ge(probs_ready, a * NT + i - 1)
                n = (i + 1) * P
                s = g_ps[i % 2]
                t_.matmul(s[:, 0:n], tile(qk_t, i), k_zero[:, 0:n], start=True, stop=False,
                          skip_group_check=True)
                t_.matmul(s[:, n - P:n], ident_bf[:, :], future_bf[:, :], start=False, stop=True,
                          skip_group_check=True).then_inc(s_ready, 1)

            def probs_transpose(a, i):
                pe.wait_ge(probs_ready, a * NT + i + 1)
                if i < 2:
                    pe.wait_ge(probs_ready, a * NT + i + 3)
                else:
                    if due(a * NT + i - 1):
                        pe.wait_ge(probs_t_ready, a * NT + i - 1)
                for k in range(i + 1):
                    last = t_.transpose(tile(g_ps[i % 2], k), probs[:, i, k * P:(k + 1) * P], ident[:, :])
                last.then_inc(probs_tr_ready, 1)

            def attend(a):
                pe.wait_ge(probs_t_ready, (a + 1) * NT)
                for k in range(NT):
                    last = t_.matmul(g_ps[0][:, k * P:T], v_dup[:, k, :, :].rearrange("p u d -> p (u d)"),
                                     probs_t[:, k, k * P:T], start=(k == 0), stop=(k == NT - 1),
                                     skip_group_check=True)
                last.then_inc(attn_ready, 1)
                pe.wait_ge(rwo_ready, a + 1)
                for i in range(NT):
                    last = t_.transpose(g_ps[1].bitcast(BF16)[:, i * P:(i + 1) * P], rwo_parts[:, i, :],
                                        ident_bf[:, :])
                last.then_inc(rwo_tr_ready, 1)

            def spread_weights(a, p):
                pe.wait_ge(rwo_t_ready, a + 1)
                if p < 2:
                    pe.wait_ge(attn_t_ready, a + 1)
                else:
                    if due(a * PAIRS + p - 1):
                        pe.wait_ge(mixed_ready, a * PAIRS + p - 1)
                t_.matmul(g_ps[p % 2][:, :], pair_sel[:, p, :, :].rearrange("p u d -> p (u d)"), rwo_t[:, :],
                          start=True, stop=True).then_inc(rwb_ready, 1)

            def add_pair(a, p):
                pe.wait_ge(mixed_ready, a * PAIRS + p + 1)
                for i in range(NT):
                    last = t_.matmul(out_ps[:, i, :], mixed[:, p % 2, i * P:(i + 1) * P], eo[:, p, :],
                                     start=False, stop=(p == PAIRS - 1 and i == NT - 1),
                                     skip_group_check=True)
                last.then_inc(pair_added, 1)

            def output_pair(a, p):
                add_pair(a, p)
                if p + 2 < PAIRS:
                    spread_weights(a, p + 2)

            xn_transpose(0)
            pe.wait_ge(sim_ready, 1)
            gate_logits(0)
            pe.wait_ge(lin_ready, 1)

            def body(b, attn, norm):
                if attn:
                    qk_transpose(b - 1)
                if isinstance(b, int) and b == 0:
                    projections(b)
                    pe.wait_ge(w3_ready, 1)
                    pe.wait_ge(const_ready, 1)
                    y_pairs(b, 0, 2)
                else:
                    y_pairs(b, 0, 2)
                    projections(b)
                if attn:
                    soft_scores(b - 1, 0)
                    soft_scores(b - 1, 1)
                y_pairs(b, 2, 4)
                if attn:
                    start_output(b - 1)
                y_pairs(b, 4, 6)
                k_to_tokens(b)
                if attn:
                    soft_scores(b - 1, 2)
                y_pairs(b, 6, 8)
                score(b, 0)
                score(b, 1)
                y_pairs(b, 8, 10)
                if attn:
                    soft_scores(b - 1, 3)
                chunk_states(b, 0)
                y_pairs(b, 10, 12)
                score(b, 2)
                if attn:
                    probs_transpose(b - 1, 0)
                y_pairs(b, 12, 14)
                score(b, 3)
                chunk_states(b, 1)
                if attn:
                    probs_transpose(b - 1, 1)
                y_pairs(b, 14, 16)
                chunk_states(b, 2)
                if attn:
                    probs_transpose(b - 1, 2)
                    probs_transpose(b - 1, 3)
                y_pairs(b, 16, 18)
                chunk_states(b, 3)
                if attn:
                    attend(b - 1)
                y_pairs(b, 18, 20)
                chunk_states(b, 4)
                if attn:
                    spread_weights(b - 1, 0)
                    spread_weights(b - 1, 1)
                la_tile(b, 0)
                y_pairs(b, 20, 22)
                la_tile(b, 1)
                if attn:
                    output_pair(b - 1, 0)
                y_pairs(b, 22, 24)
                la_tile(b, 2)
                if attn:
                    output_pair(b - 1, 1)
                y_pairs(b, 24, 26)
                la_tile(b, 3)
                if attn:
                    output_pair(b - 1, 2)
                y_pairs(b, 26, 28)
                if attn:
                    output_pair(b - 1, 3)
                y_pairs(b, 28, 30)
                if attn:
                    output_pair(b - 1, 4)
                val_transpose(b)
                y_pairs(b, 30, 32)
                if norm:
                    xn_transpose(b + 1)
                if attn:
                    output_pair(b - 1, 5)
                    output_pair(b - 1, 6)
                if norm:
                    gate_logits(b + 1)
                if attn:
                    output_pair(b - 1, 7)

            passes(body)(pe)
            a = B - 1
            start_output(a)
            qk_transpose(a)
            soft_scores(a, 0)
            soft_scores(a, 1)
            soft_scores(a, 2)
            soft_scores(a, 3)
            for i in range(NT):
                probs_transpose(a, i)
            attend(a)
            spread_weights(a, 0)
            spread_weights(a, 1)
            for p in range(PAIRS):
                output_pair(a, p)


_INS = ["L0_attn_x", "L0_attn_Wq", "L0_attn_bq", "L0_attn_Wk", "L0_attn_bk", "L0_attn_Wv", "L0_attn_bv",
        "L0_attn_Wo", "L0_attn_bo", "L0_ffn_sim_matrix", "L0_ffn_gates", "L0_ffn_q_proj", "L0_ffn_k_proj",
        "L0_ffn_v_proj", "L0_ffn_o_proj"]


def kernel(**inputs):
    import numpy as _np
    import concourse.bacc as _bacc
    from concourse import mybir as _mybir
    from concourse.bass_utils import run_bass_kernel_spmd as _run

    nc = _bacc.Bacc("TRN2", target_bir_lowering=False, num_devices=1)
    arrays, args = {}, []
    for name in _INS:
        a = _np.ascontiguousarray(inputs[name])
        arrays[name] = a
        args.append(nc.dram_tensor(name, a.shape, _mybir.dt.from_np(a.dtype), kind="ExternalInput").ap())
    shape = inputs["L0_attn_x"].shape
    args.append(nc.dram_tensor("out", shape, _mybir.dt.float32, kind="ExternalOutput").ap())
    build(nc, *args)
    r = _run(nc, [arrays], core_ids=[0])
    return r.results[0]["out"]
```

```python
from contextlib import ExitStack

import concourse.bass as bass
from concourse import mybir

F32 = mybir.dt.float32
F16 = mybir.dt.float16
BF16 = mybir.dt.bfloat16
ALU = mybir.AluOpType
ACT = mybir.ActivationFunctionType
AX = mybir.AxisListType

P = 128
BIG = 1.0e30
LN_EPS = 1e-5
NORM_EPS = 1e-12
DEN_EPS = 1e-6


def due(count):
    return not isinstance(count, int) or count > 0


class Chain:

    def __init__(self, engine, semaphore, per_pass, index):
        self.engine, self.semaphore, self.n = engine, semaphore, 0
        self.per_pass, self.index = per_pass, index

    def step(self, instruction):
        self.n += 1
        instruction.then_inc(self.semaphore, 1)
        self.engine.wait_ge(self.semaphore, self.index * self.per_pass + self.n)

    def end(self):
        assert self.n == self.per_pass, self.n


def build(nc, x_in, wq_in, bq_in, wk_in, bk_in, wv_in, bv_in, wo_in, bo_in,
          sim_in, gates_in, eq_in, ek_in, ev_in, eo_in, out):
    B, T, D = x_in.shape
    E, _, HD = eq_in.shape
    NT = T // P
    C = 32
    CT = P // C
    NC = T // C
    H, M = 16, 8
    G = 4
    S4 = H // G
    M1 = M + 1
    VW = H * M1
    W3 = 3 * HD
    PAIRS = E // 2
    STACKS = 16 * 3 * CT
    W3_PARTS = 4
    YN = NT * PAIRS
    ADDS = 3
    TMP = 4
    DB = 3
    ND = NC // DB
    SCALE = float(HD) ** -0.5
    assert D == P and H * M == D and NC == 16 and ND * DB == NC - 1

    ctx = ExitStack()
    with ctx:
        def sb(name, shape, dt=F32):
            return ctx.enter_context(nc.sbuf_tensor(name, shape, dt))

        def sem(name):
            return ctx.enter_context(nc.semaphore(name))

        ident = sb("ident", [P, P])
        ident_bf = sb("ident_bf", [P, P], BF16)
        ones = sb("ones", [P, P])
        future_bf = sb("future_bf", [P, P], BF16)
        past = sb("past", [P, C])
        place_mask = sb("place_mask", [P, S4])
        group_mask = sb("group_mask", [P, G])
        block_mask = sb("block_mask", [P, VW])
        pair_sel = sb("pair_sel", [P, PAIRS, 2, HD], BF16)
        rank = sb("rank", [P, E])
        half = sb("half", [P, NT])
        neg_half = sb("neg_half", [P, NT])
        half16 = sb("half16", [P, E])
        stage = sb("stage", [P, E, W3])
        w3_hi = sb("w3_hi", [P, E, W3], F16)
        w3_lo = sb("w3_lo", [P, E, W3], F16)
        lin_w = sb("lin_w", [P, 3, D])
        lin_hi = sb("lin_hi", [P, 3, D], F16)
        lin_lo = sb("lin_lo", [P, 3, D], F16)
        wv_raw = sb("wv_raw", [P, D])
        bv_raw = sb("bv_raw", [P, D])
        bv_row = sb("bv_row", [P, D])
        bo_row = sb("bo_row", [P, D])
        bqk = sb("bqk", [P, 2])
        wo = sb("wo", [P, D])
        eo = sb("eo", [P, PAIRS, D])
        sim = sb("sim", [P, E])
        sim_sq = sb("sim_sq", [P, E])
        sim_r = sb("sim_r", [P, 4, E])
        sim_hi = sb("sim_hi", [P, E], F16)
        sim_lo = sb("sim_lo", [P, E], F16)
        gates = sb("gates", [P, E])
        sig = sb("sig", [P, 3, E])
        sigmoid = sb("sigmoid", [P, E])

        x = sb("x", [P, NT, D])
        stats = sb("stats", [P, NT, 6])
        mv = sb("mv", [P, NT, 2])
        wait_pad = sb("wait_pad", [P, 1])
        var_eps = sb("var_eps", [P, NT])
        rstd = sb("rstd", [P, NT])
        nrm = sb("nrm", [P, 5, NT])
        xn = sb("xn", [P, NT, D])
        xt_next = sb("xt_next", [P, 2, T], F16)
        xt_now = sb("xt_now", [P, 2, T], F16)
        logit = sb("logit", [P, 2, NT, E])
        gmax = sb("gmax", [P, 8, NT])
        gate_sb = sb("gate_sb", [P, 11, NT, E])
        gexp = sb("gexp", [P, NT, E])
        rw = sb("rw", [P, NT, E])
        rw_prev = sb("rw_prev", [P, NT, E])

        acc_v = sb("acc_v", [P, NT, 2, W3])
        acc_s = sb("acc_s", [P, NT, 2, W3])
        y_tmp = sb("y_tmp", [P, TMP, 2, W3])
        y_sum = sb("y_sum", [P, NT, 2, W3])
        qkv = sb("qkv", [P, NT, 3, 2, HD])

        elu_e = sb("elu_e", [P, 2, T])
        elu_r = sb("elu_r", [P, 2, T])
        q_t = sb("q_t", [P, T])
        k_t = sb("k_t", [P, T])
        q_groups = sb("q_groups", [P, NC, G, C])
        k_places = sb("k_places", [P, NC, S4, C])
        kv_parts = sb("kv_parts", [P, NT, 4, VW], F16)
        kv_stack = sb("kv_stack", [P, CT, NT, 2, VW], F16)
        v_ones = sb("v_ones", [P, NT, S4, G, M1])
        v_blocks = sb("v_blocks", [P, NC, S4, G, M1])
        scores = sb("scores", [P, NT, CT * G * C])
        d_state = sb("d_state", [P, NC - 1, VW])
        state = sb("state", [P, NC, VW])
        den = sb("den", [P, 2, 2, 2 * H])
        val = sb("val", [P, NT, D])
        val_t = sb("val_t", [P, T])

        q_halves = sb("q_halves", [P, T], F16)
        k_high = sb("k_high", [P, T], F16)
        k_low = sb("k_low", [P, T], F16)
        neg_max = sb("neg_max", [P, NT])
        ssum = sb("ssum", [P, NT])
        srec = sb("srec", [P, NT])
        probs = sb("probs", [P, NT, T])
        probs_t = sb("probs_t", [P, NT, T])
        attn_t = sb("attn_t", [P, T])
        rwo = sb("rwo", [P, 2, NT, E])
        rwo_parts = sb("rwo_parts", [P, NT, P], BF16)
        rwo_t = sb("rwo_t", [P, T], BF16)
        mixed = sb("mixed", [P, 2, T])
        x_res = sb("x_res", [P, NT, D])
        res = sb("res", [P, NT, D])
        out_sb = sb("out_sb", [P, NT, D])

        y_ps = [ctx.enter_context(nc.psum_tensor(f"y_ps{n}", [P, 2, 256], F32)) for n in range(2)]
        out_ps = ctx.enter_context(nc.psum_tensor("out_ps", [P, NT, D], F32))
        g_ps = [ctx.enter_context(nc.psum_tensor(f"g_ps{n}", [P, 512], F32)) for n in range(5)]
        y_ps_flat = [t[:, :, :].rearrange("p a b -> p (a b)") for t in y_ps]
        y_view = [t[:, 0:2 * W3] for t in y_ps_flat]
        score_banks = [[g_ps[0], g_ps[1], g_ps[0], g_ps[1]],
                       [g_ps[2], g_ps[3], g_ps[4], y_ps_flat[0]]]
        attn_banks = [g_ps[0], y_ps_flat[1]]
        pair_banks = [[g_ps[0], g_ps[1]], [g_ps[0], g_ps[1], g_ps[2], g_ps[3]]]
        next_hi, next_lo = xt_next[:, 0, :], xt_next[:, 1, :]
        xt_hi, xt_lo = xt_now[:, 0, :], xt_now[:, 1, :]

        gate_loaded = sem("gate_loaded")
        experts_loaded = sem("experts_loaded")
        lin_loaded = sem("lin_loaded")
        out_w_loaded = sem("out_w_loaded")
        filled = sem("filled")
        ident_ready = sem("ident_ready")
        const_step = sem("const_step")
        const_ready = sem("const_ready")
        rank_ready = sem("rank_ready")
        places_ready = sem("places_ready")
        zeros_ready = sem("zeros_ready")
        blocks_zero = sem("blocks_zero")
        groups_zero = sem("groups_zero")
        dve_const_step = sem("dve_const_step")
        w3_hi_ready = sem("w3_hi_ready")
        sim_norm = sem("sim_norm")
        sim_ready = sem("sim_ready")
        lin_ready = sem("lin_ready")
        w3_ready = sem("w3_ready")
        sim_norm_read = sem("sim_norm_read")
        sim_root = sem("sim_root")
        gates_exp = sem("gates_exp")

        x_loaded = sem("x_loaded")
        stats_step = sem("stats_step")
        row_stats_ready = sem("row_stats_ready")
        var_ready = sem("var_ready")
        rstd_ready = sem("rstd_ready")
        norm_sq_ready = sem("norm_sq_ready")
        norm_ready = sem("norm_ready")
        xn_ready = sem("xn_ready")
        xt_ready = sem("xt_ready")
        xt_hi_ready = sem("xt_hi_ready")
        xt_lo_ready = sem("xt_lo_ready")
        xt_moved = sem("xt_moved")
        logits_ready = sem("logits_ready")
        logits_read = sem("logits_read")
        gate_step = sem("gate_step")
        gate_arg_ready = sem("gate_arg_ready")
        gate_exp_ready = sem("gate_exp_ready")
        rw_ready = sem("rw_ready")
        rw_kept = sem("rw_kept")

        y_ready = [sem("y_ready_v"), sem("y_ready_s")]
        y_added_v = sem("y_added_v")
        y_scaled_s = sem("y_scaled_s")
        y_added_s = sem("y_added_s")
        y_summed = sem("y_summed")
        qkv_ready = sem("qkv_ready")

        proj_ready = sem("proj_ready")
        elu_parts = sem("elu_parts")
        q_ready = sem("q_ready")
        k_ready = sem("k_ready")
        v_ready = sem("v_ready")
        v_spread = sem("v_spread")
        q_groups_ready = sem("q_groups_ready")
        k_places_ready = sem("k_places_ready")
        k_tok_ready = sem("k_tok_ready")
        k_high_ready = sem("k_high_ready")
        v_high_ready = sem("v_high_ready")
        k_low_ready = sem("k_low_ready")
        v_low_ready = sem("v_low_ready")
        kv_stacked = sem("kv_stacked")
        score_ready = sem("score_ready")
        score_masked = sem("score_masked")
        d_ready = sem("d_ready")
        d_masked = sem("d_masked")
        state_ready = sem("state_ready")
        la_ready = sem("la_ready")
        den_step = sem("den_step")
        val_ready = sem("val_ready")
        val_tr_ready = sem("val_tr_ready")
        val_t_ready = sem("val_t_ready")

        wo_added = sem("wo_added")
        qk_tr_ready = sem("qk_tr_ready")
        qk_high_ready = sem("qk_high_ready")
        qk_low_ready = sem("qk_low_ready")
        s_ready = sem("s_ready")
        neg_max_ready = sem("neg_max_ready")
        probs_ready = sem("probs_ready")
        probs_tr_ready = sem("probs_tr_ready")
        probs_t_ready = sem("probs_t_ready")
        attn_ready = sem("attn_ready")
        attn_t_ready = sem("attn_t_ready")
        rwo_step = sem("rwo_step")
        rwo_ready = sem("rwo_ready")
        rwo_tr_ready = sem("rwo_tr_ready")
        rwo_t_ready = sem("rwo_t_ready")
        rwb_ready = sem("rwb_ready")
        mixed_ready = sem("mixed_ready")
        pair_added = sem("pair_added")
        xr_loaded = sem("xr_loaded")
        res_ready = sem("res_ready")
        out_ready = sem("out_ready")
        out_stored = sem("out_stored")

        def passes(body):
            def run(engine):
                body(0, False, True)
                body(1, True, True)
                with engine.Fori(2, B - 1) as b:
                    body(b, True, True)
                body(B - 1, True, False)
            return run

        def x_of(b):
            return x_in[b].rearrange("(i p) d -> p i d", p=P)

        def out_of(b):
            return out[b].rearrange("(i p) d -> p i d", p=P)

        block = ctx.enter_context(nc.Block())

        @block.sync
        def _(sp):
            sp.dma_start(x[:, :, :], x_of(0)).then_inc(x_loaded, 16)
            sp.dma_start(sim[:, :], sim_in).then_inc(gate_loaded, 16)
            sp.dma_start(gates[:, :], gates_in.partition_broadcast(P)).then_inc(gate_loaded, 16)
            sp.dma_start(lin_w[:, 0, :], wq_in).then_inc(lin_loaded, 16)
            sp.dma_start(lin_w[:, 1, :], wk_in).then_inc(lin_loaded, 16)
            sp.dma_start(wv_raw[:, :], wv_in).then_inc(lin_loaded, 16)
            for n, w in enumerate((eq_in, ek_in, ev_in)):
                sp.dma_start(stage[:, :, n * HD:(n + 1) * HD],
                             w.rearrange("e c d -> c e d")).then_inc(experts_loaded, 16)
            sp.dma_start(eo[:, :, :], eo_in.rearrange("(p u) d c -> (u d) p c", u=2))\
              .then_inc(out_w_loaded, 16)
            sp.dma_start(wo[:, :], wo_in).then_inc(out_w_loaded, 16)
            sp.dma_start(bo_row[:, :], bo_in.partition_broadcast(P)).then_inc(out_w_loaded, 16)

            def spread_values(first, last):
                for s in range(first, last):
                    for j in range(CT):
                        sp.dma_start(v_blocks[C * s:C * s + C, j:NC:CT, s, :, :],
                                     v_ones[C * j:C * j + C, :, s, :, :]).then_inc(v_spread, 16)

            def body(b, attn, norm):
                if norm:
                    sp.wait_ge(xn_ready, (b + 1) * NT)
                    sp.dma_start(x[:, :, :], x_of(b + 1)).then_inc(x_loaded, 16)
                if attn:
                    if due(b - 1):
                        sp.wait_ge(res_ready, b - 1)
                    sp.dma_start(x_res[:, :, :], x_of(b - 1)).then_inc(xr_loaded, 16)
                if due(b * NT):
                    sp.wait_ge(la_ready, b * NT)
                if isinstance(b, int) and b == 0:
                    sp.wait_ge(blocks_zero, 1)
                sp.wait_ge(v_ready, b + 1)
                spread_values(0, 1)
                sp.wait_ge(k_low_ready, b + 1)
                sp.wait_ge(v_low_ready, b + 1)
                for r, pair in enumerate((slice(1, 3), slice(0, 3, 2), slice(1, 4, 2))):
                    for j in range(CT):
                        sp.dma_start(kv_stack[C * r:C * r + C, j, :, :, :],
                                     kv_parts[C * j:C * j + C, :, pair, :]).then_inc(kv_stacked, 16)
                spread_values(1, S4)
                if attn and (not isinstance(b, int) or b > 1):
                    sp.wait_ge(out_ready, b - 1)
                    sp.dma_start(out_of(b - 2), out_sb[:, :, :]).then_inc(out_stored, 16)

            passes(body)(sp)
            sp.wait_ge(res_ready, B - 1)
            sp.dma_start(x_res[:, :, :], x_of(B - 1)).then_inc(xr_loaded, 16)
            sp.wait_ge(out_ready, B - 1)
            sp.dma_start(out_of(B - 2), out_sb[:, :, :]).then_inc(out_stored, 16)
            sp.wait_ge(out_ready, B)
            sp.dma_start(out_of(B - 1), out_sb[:, :, :]).then_inc(out_stored, 16)
            sp.wait_ge(out_stored, 16 * B)

        @block.gpsimd
        def _(pool):
            g = nc.gpsimd
            g.memset(ident[:, :], 0.0).then_inc(filled, 1)
            g.memset(ones[:, :], 1.0)
            g.memset(half[:, :], 0.5)
            g.memset(half16[:, :], 0.5)
            g.memset(neg_half[:, :], -0.5).then_inc(filled, 1)
            pool.wait_ge(filled, 2)
            g.affine_select(out=ident[:, :], in_=ident[:, :], compare_op=ALU.not_equal,
                            fill=1.0, base=0, pattern=[[-1, P]], channel_multiplier=1)\
             .then_inc(ident_ready, 1)

            def inverse_deviation(n):
                pool.wait_ge(var_ready, n + 1)
                if due(n * NT):
                    pool.wait_ge(xn_ready, n * NT)
                g.tensor_tensor(rstd[:, :], var_eps[:, :], neg_half[:, :], ALU.pow).then_inc(rstd_ready, 1)

            def row_norm(n):
                pool.wait_ge(norm_sq_ready, n + 1)
                g.tensor_tensor(nrm[:, 2, :], nrm[:, 1, :], half[:, :], ALU.pow).then_inc(norm_ready, 1)

            def residual(a):
                pool.wait_ge(xr_loaded, (a + 1) * 16)
                if due(a):
                    pool.wait_ge(out_ready, a)
                pool.wait_ge(out_w_loaded, 16 * 3)
                g.tensor_tensor(res[:, :, :], x_res[:, :, :],
                                bo_row[:, :].unsqueeze(1).broadcast_to([P, NT, D]), ALU.add)\
                 .then_inc(res_ready, 1)

            def y_add(b, first, last):
                for n in range(first, last):
                    i, p = n // PAIRS, n % PAIRS
                    if p % 2 == 0 or p == 1:
                        continue
                    count = i * ADDS + (p - 3) // 2
                    pool.wait_ge(y_scaled_s, (b * NT * (PAIRS // 2) + i * (PAIRS // 2) + p // 2 + 1) * 2)
                    if due(b * NT * ADDS + count):
                        pool.wait_ge(y_added_s, b * NT * ADDS + count)
                    g.tensor_tensor(acc_s[:, i, :, :], acc_s[:, i, :, :],
                                    y_tmp[:, count % TMP, :, :], ALU.add).then_inc(y_added_s, 1)

            def y_finish(b, i):
                pool.wait_ge(y_added_s, b * NT * ADDS + (i + 1) * ADDS)
                pool.wait_ge(y_added_v, (b * NT + i + 1) * PAIRS)
                if due(b * NT):
                    pool.wait_ge(qkv_ready, b * NT)
                g.tensor_tensor(y_sum[:, i, :, :], acc_v[:, i, :, :], acc_s[:, i, :, :], ALU.add)\
                 .then_inc(y_summed, 1)
                pool.wait_ge(y_summed, b * NT + i + 1)
                if due(b):
                    pool.wait_ge(attn_ready, b)
                if due(b):
                    pool.wait_ge(qk_tr_ready, b)
                odd, even = (y_sum[:, i, u, :].rearrange("p (n d) -> p n d", d=HD).unsqueeze(2)
                             .broadcast_to([P, 3, 2, HD]) for u in range(2))
                g.tensor_tensor(qkv[:, i, :, :, :], odd, even, ALU.add).then_inc(qkv_ready, 1)

            def place_k(b):
                pool.wait_ge(k_ready, b + 1)
                if due(b * NT):
                    pool.wait_ge(score_ready, b * NT)
                for s in range(2, S4):
                    g.tensor_tensor(k_places[:, :, s, :], k_t[:, :].rearrange("p (c t) -> p c t", t=C),
                                    place_mask[:, s:s + 1].unsqueeze(2).broadcast_to([P, NC, C]), ALU.mult)\
                     .then_inc(k_places_ready, 1)

            def group_q(b):
                pool.wait_ge(q_ready, b + 1)
                if due(b * NT):
                    pool.wait_ge(score_ready, b * NT)
                for n in range(2, G):
                    g.tensor_tensor(q_groups[:, :, n, :], q_t[:, :].rearrange("p (c t) -> p c t", t=C),
                                    group_mask[:, n:n + 1].unsqueeze(2).broadcast_to([P, NC, C]), ALU.mult)\
                     .then_inc(q_groups_ready, 1)

            def v_low(b):
                pool.wait_ge(v_high_ready, b + 1)
                g.tensor_tensor(kv_parts[:, :, 3, :], v_ones[:, :, :, :, :].rearrange("p i s g m -> p i (s g m)"),
                                kv_parts[:, :, 2, :], ALU.subtract).then_inc(v_low_ready, 1)

            def state_add(b, first, last):
                for c in range(first, last):
                    pool.wait_ge(d_masked, b * ND + c // DB + 1)
                    if c == 0:
                        if due(b * NT):
                            pool.wait_ge(la_ready, b * NT)
                    else:
                        if due(b * (NC - 1) + c):
                            pool.wait_ge(state_ready, b * (NC - 1) + c)
                    g.tensor_tensor(state[:, c + 1, :], state[:, c, :], d_state[:, c, :], ALU.add)\
                     .then_inc(state_ready, 1)

            inverse_deviation(0)
            row_norm(0)
            pool.wait_ge(sim_norm_read, 1)
            g.tensor_tensor(sim_r[:, 1, :], sim_r[:, 0, :], half16[:, :], ALU.pow).then_inc(sim_root, 1)
            for e in range(E):
                last = g.memset(rank[:, e:e + 1], float(E - e))
            last.then_inc(rank_ready, 1)
            for t in (past, place_mask, block_mask):
                g.memset(t[:, :], 1.0)
            g.memset(v_ones[:, :, :, :, :], 1.0)
            g.memset(state[:, 0, :], 0.0)
            g.memset(future_bf[:, :], 0.0).then_inc(filled, 1)
            pool.wait_ge(filled, 3)
            pool.wait_ge(ident_ready, 1)
            consts = Chain(pool, const_step, 19, 0)
            for side, base in ((1, 0), (-1, M - 1)):
                for s in range(S4):
                    rows = slice(C * s, C * s + C)
                    consts.step(g.affine_select(out=place_mask[rows, :], in_=place_mask[rows, :],
                                                compare_op=ALU.is_ge, fill=0.0, base=base,
                                                pattern=[[-side * M, S4]], channel_multiplier=side))
            g.memset(pair_sel[:, :, :, :], 0.0).then_inc(places_ready, 1)
            g.memset(v_blocks[:, :, :, :, :], 0.0).then_inc(blocks_zero, 1)
            consts.step(g.tensor_copy(ident_bf[:, :], ident[:, :]))
            consts.step(g.affine_select(out=future_bf[:, :], in_=future_bf[:, :], compare_op=ALU.is_ge,
                                        fill=BIG, base=0, pattern=[[-1, P]], channel_multiplier=1))
            for s in range(S4):
                rows = slice(C * s, C * s + C)
                consts.step(g.affine_select(out=past[rows, :], in_=past[rows, :], compare_op=ALU.is_ge,
                                            fill=0.0, base=0, pattern=[[1, C]], channel_multiplier=-1))
            view = block_mask[:, :].rearrange("p (s g m) -> p s g m", s=S4, g=G)
            for side, base in ((1, 0), (-1, M - 1)):
                consts.step(g.affine_select(out=view, in_=view, compare_op=ALU.is_ge, fill=0.0, base=base,
                                            pattern=[[-side * M, S4], [-side * M * S4, G], [0, M1]],
                                            channel_multiplier=side))
            g.memset(y_sum[:, 0, 0, 0:1], 0.0).then_inc(const_ready, 1)
            pool.wait_ge(zeros_ready, 1)
            pool.wait_ge(groups_zero, 1)

            def pair_selection():
                pool.wait_ge(places_ready, 1)
                for part in range(3):
                    last = g.affine_select(out=pair_sel[:, :, :, :], in_=pair_sel[:, :, :, :],
                                           compare_op=ALU.not_equal, fill=1.0, base=-E * part,
                                           pattern=[[-2, PAIRS], [-1, 2], [0, HD]], channel_multiplier=1)
                    consts.step(last)
                consts.end()

            def body(b, attn, norm):
                place_k(b)
                group_q(b)
                v_low(b)
                if isinstance(b, int) and b == 0:
                    y_add(b, 0, 8)
                    pair_selection()
                    y_add(b, 8, 14)
                else:
                    y_add(b, 0, 14)
                if norm:
                    inverse_deviation(b + 1)
                y_add(b, 14, 16)
                state_add(b, 0, 3)
                state_add(b, 3, 5)
                if norm:
                    row_norm(b + 1)
                y_add(b, 16, 18)
                state_add(b, 5, 10)
                y_add(b, 18, 20)
                state_add(b, 10, 12)
                y_add(b, 20, 22)
                state_add(b, 12, 15)
                y_add(b, 22, 24)
                if attn:
                    residual(b - 1)
                y_finish(b, 0)
                y_add(b, 24, 28)
                y_finish(b, 1)
                y_add(b, 28, 30)
                if norm:
                    y_finish(b, 2)
                y_add(b, 30, 32)
                if norm:
                    y_finish(b, 3)

            passes(body)(pool)
            residual(B - 1)

        @block.scalar
        def _(act):
            a_ = nc.scalar
            act.dma_start(bqk[:, 0:1], bq_in.rearrange("(p a) -> p a", a=1)).then_inc(lin_loaded, 16)
            act.dma_start(bqk[:, 1:2], bk_in.rearrange("(p a) -> p a", a=1)).then_inc(lin_loaded, 16)
            act.dma_start(bv_raw[:, :], bv_in.partition_broadcast(P)).then_inc(lin_loaded, 16)
            act.wait_ge(gate_loaded, 16 * 2)
            a_.activation(sig[:, 0, :], gates[:, :], ACT.Exp, scale=-1.0).then_inc(gates_exp, 1)

            def xt_high(n):
                act.wait_ge(xt_ready, n + 1)
                if due(n):
                    act.wait_ge(xt_moved, n)
                if due(n):
                    act.wait_ge(logits_ready, n)
                a_.activation(next_hi, g_ps[4][:, :], ACT.Copy).then_inc(xt_hi_ready, 1)

            def gate_exp(n):
                act.wait_ge(gate_arg_ready, n + 1)
                a_.activation(gexp[:, :, :], gate_sb[:, 10, :, :], ACT.Exp).then_inc(gate_exp_ready, 1)

            def y_scale(b, first, last):
                for n in range(first, last):
                    i, p = n // PAIRS, n % PAIRS
                    if p % 2 == 0:
                        continue
                    act.wait_ge(rw_ready, b + 1)
                    act.wait_ge(y_ready[1], b * YN // 2 + n // 2 + 1)
                    count = i * 3 + (p - 3) // 2
                    if p == 1:
                        if due((b - 1) * NT + i + 1):
                            act.wait_ge(y_summed, (b - 1) * NT + i + 1)
                    else:
                        if due(b * NT * 3 + count - TMP + 1):
                            act.wait_ge(y_added_s, b * NT * 3 + count - TMP + 1)
                    for u in range(2):
                        dst = acc_s[:, i, u, :] if p == 1 else y_tmp[:, count % TMP, u, :]
                        a_.activation(dst, y_view[1][:, u * W3:(u + 1) * W3], ACT.Copy,
                                      scale=rw[:, i, 2 * p + u:2 * p + u + 1]).then_inc(y_scaled_s, 1)

            def elu_pieces(b):
                for n in range(2):
                    act.wait_ge(proj_ready, b * 3 + n + 1)
                    if due(b):
                        act.wait_ge((q_ready, k_ready)[n], b)
                    a_.activation(elu_e[:, n, :], g_ps[2 + n][:, :], ACT.Exp, bias=bqk[:, n:n + 1])\
                      .then_inc(elu_parts, 1)
                    a_.activation(elu_r[:, n, :], g_ps[2 + n][:, :], ACT.Relu, bias=bqk[:, n:n + 1])\
                      .then_inc(elu_parts, 1)

            def group_q(b, first, last):
                act.wait_ge(q_ready, b + 1)
                if due(b * NT):
                    act.wait_ge(score_ready, b * NT)
                for g in range(first, last):
                    rows = slice(C * g, C * g + C)
                    a_.activation(q_groups[rows, :, g, :],
                                  q_t[rows, :].rearrange("p (c t) -> p c t", t=C), ACT.Copy)\
                      .then_inc(q_groups_ready, 1)

            def k_high_tokens(b):
                act.wait_ge(k_tok_ready, b + 1)
                if due(b * STACKS):
                    act.wait_ge(kv_stacked, b * STACKS)
                a_.activation(kv_parts[:, :, 1, 0:D], g_ps[2][:, :].rearrange("p (i f) -> p i f", f=D), ACT.Copy)\
                 .then_inc(k_high_ready, 1)

            def v_high(b):
                act.wait_ge(v_ready, b + 1)
                a_.activation(kv_parts[:, :, 2, :], v_ones[:, :, :, :, :].rearrange("p i s g m -> p i (s g m)"),
                              ACT.Copy).then_inc(v_high_ready, 1)

            def soft_exp(a, i, alone=False):
                act.wait_ge(neg_max_ready, a * NT + i + 1)
                if due(a * NT):
                    act.wait_ge(probs_tr_ready, a * NT)
                if due(a):
                    act.wait_ge(rwo_ready, a)
                n = (i + 1) * P
                a_.activation(probs[:, i, 0:n], score_banks[alone][i][:, 0:n], ACT.Exp, bias=neg_max[:, i:i + 1],
                              scale=-1.0, accum_out=ssum[:, i:i + 1]).then_inc(probs_ready, 1)

            def probs_out(a, i, alone=False):
                act.wait_ge(probs_tr_ready, a * NT + i + 1)
                if due(a):
                    act.wait_ge(attn_ready, a)
                a_.activation(probs_t[:, 0:i + 1, i * P:(i + 1) * P],
                              score_banks[alone][i][:, 0:(i + 1) * P].rearrange("p (k q) -> p k q", q=P), ACT.Copy)\
                  .then_inc(probs_t_ready, 1)

            def qk_high(a):
                act.wait_ge(qk_tr_ready, a + 1)
                if due(a):
                    act.wait_ge(s_ready, a * NT)
                a_.activation(q_halves[:, :], g_ps[0][:, :], ACT.Copy).then_inc(qk_high_ready, 1)
                a_.activation(k_high[:, :], g_ps[1][:, :], ACT.Copy, scale=-SCALE).then_inc(qk_high_ready, 1)

            def attn_out(a, alone=False):
                act.wait_ge(attn_ready, a + 1)
                if due(a):
                    act.wait_ge(mixed_ready, a * PAIRS)
                a_.activation(attn_t[:, :], attn_banks[alone][:, :], ACT.Copy).then_inc(attn_t_ready, 1)

            def weights_out(a):
                act.wait_ge(rwo_tr_ready, a + 1)
                if due(a):
                    act.wait_ge(rwb_ready, a * PAIRS)
                a_.activation(rwo_t[:, :], g_ps[1].bitcast(BF16)[:, 0:T], ACT.Copy)\
                  .then_inc(rwo_t_ready, 1)

            def val_out(b):
                act.wait_ge(val_tr_ready, b + 1)
                if due(b):
                    act.wait_ge(wo_added, b)
                a_.activation(val_t[:, :], g_ps[2][:, :], ACT.Copy).then_inc(val_t_ready, 1)

            xt_high(0)
            act.wait_ge(filled, 2)
            a_.activation(q_groups[:, :, :, :].rearrange("p c g t -> p (c g t)"),
                          ones[:, 0:1].broadcast_to([P, NC * G * C]), ACT.Copy, scale=0.0)\
              .then_inc(groups_zero, 1)
            gate_exp(0)
            act.wait_ge(experts_loaded, 16 * 3)
            for n in range(W3_PARTS):
                part = slice(n * E // W3_PARTS, (n + 1) * E // W3_PARTS)
                a_.activation(w3_hi[:, part, :], stage[:, part, :], ACT.Copy).then_inc(w3_hi_ready, 1)
            act.wait_ge(lin_loaded, 16 * 6)
            act.wait_ge(groups_zero, 1)

            def body(b, attn, norm):
                elu_pieces(b)
                y_scale(b, 0, 2)
                if attn:
                    qk_high(b - 1)
                y_scale(b, 2, 4)
                group_q(b, 0, 2)
                k_high_tokens(b)
                y_scale(b, 4, 6)
                v_high(b)
                if attn:
                    soft_exp(b - 1, 0)
                if attn:
                    soft_exp(b - 1, 1)
                y_scale(b, 6, 8)
                if attn:
                    soft_exp(b - 1, 2)
                y_scale(b, 8, 10)
                if attn:
                    soft_exp(b - 1, 3)
                y_scale(b, 10, 12)
                if attn:
                    probs_out(b - 1, 0)
                y_scale(b, 12, 14)
                if attn:
                    probs_out(b - 1, 1)
                    probs_out(b - 1, 2)
                y_scale(b, 14, 16)
                if attn:
                    probs_out(b - 1, 3)
                y_scale(b, 16, 18)
                if attn:
                    attn_out(b - 1)
                    weights_out(b - 1)
                y_scale(b, 18, 20)
                if norm:
                    xt_high(b + 1)
                y_scale(b, 20, 26)
                if norm:
                    gate_exp(b + 1)
                y_scale(b, 26, 30)
                val_out(b)
                y_scale(b, 30, 32)

            passes(body)(act)
            a = B - 1
            qk_high(a)
            for i in range(NT):
                soft_exp(a, i, alone=True)
            for i in range(NT):
                probs_out(a, i, alone=True)
            weights_out(a)
            attn_out(a, alone=True)

        @block.vector
        def _(dve):
            v = nc.vector
            def row_stats(n, first, last):
                dve.wait_ge(x_loaded, (n + 1) * 16)
                for i in range(first, last):
                    v.bn_stats(stats[:, i, :], x[:, i, :]).then_inc(row_stats_ready, 1)

            def variance(n):
                st = Chain(dve, stats_step, STATS, n)
                dve.wait_ge(row_stats_ready, (n + 1) * NT)
                v.memset(wait_pad[:, :], 0.0)
                for i in range(NT):
                    last = v.bn_aggr(mv[:, i, :], stats[:, i, :])
                st.step(last)
                v.tensor_scalar(var_eps[:, :], mv[:, :, 1], LN_EPS, None, ALU.add).then_inc(var_ready, 1)
                return st

            def normalise(n, st):
                dve.wait_ge(rstd_ready, n + 1)
                st.step(v.tensor_tensor(nrm[:, 0, :], mv[:, :, 1], rstd[:, :], ALU.mult))
                st.step(v.tensor_tensor(nrm[:, 4, :], nrm[:, 0, :], rstd[:, :], ALU.mult))
                v.tensor_scalar(nrm[:, 1, :], nrm[:, 4, :], float(D), None, ALU.mult)\
                 .then_inc(norm_sq_ready, 1)
                if due(n):
                    dve.wait_ge(xt_ready, n)
                for i in range(NT):
                    v.tensor_scalar(xn[:, i, :], x[:, i, :], mv[:, i, 0:1], rstd[:, i:i + 1],
                                    ALU.subtract, ALU.mult).then_inc(xn_ready, 1)

            def norm_inverse(n, st):
                dve.wait_ge(norm_ready, n + 1)
                st.step(v.tensor_scalar(nrm[:, 0, :], nrm[:, 2, :], NORM_EPS, None, ALU.max))
                st.step(v.reciprocal(nrm[:, 3, :], nrm[:, 0, :]))
                st.end()

            STATS = 5

            def xt_low(n):
                dve.wait_ge(xt_hi_ready, n + 1)
                v.tensor_tensor(next_lo, g_ps[4][:, :], next_hi, ALU.subtract).then_inc(xt_lo_ready, 1)

            def xt_move(n):
                dve.wait_ge(xt_lo_ready, n + 1)
                if due(n * YN // 2):
                    dve.wait_ge(y_ready[0], n * YN // 2)
                if due(n * YN // 2):
                    dve.wait_ge(y_ready[1], n * YN // 2)
                v.tensor_copy(xt_now[:, :, :], xt_next[:, :, :]).then_inc(xt_moved, 1)

            GATES = 19

            def over_e(t):
                return t.unsqueeze(2).broadcast_to([P, NT, E])

            def over_i(t):
                return t.unsqueeze(1).broadcast_to([P, NT, E])

            top, top_relu, top_rank, second, second_rank, idle, total, inv = \
                (gmax[:, k, :] for k in range(8))
            logits = logit[:, 1, :, :]
            below, ranked, first, rest, below2, ranked2, both, fallback, active, weight = \
                (gate_sb[:, k, :, :] for k in range(10))

            def gate_logits(n):
                st = Chain(dve, gate_step, GATES, n)
                dve.wait_ge(logits_ready, n + 1)
                v.tensor_tensor(logit[:, 0, :, :], g_ps[2][:, 0:NT * E].rearrange("p (i e) -> p i e", e=E),
                                over_e(nrm[:, 3, :]), ALU.mult).then_inc(logits_read, 1)
                dve.wait_ge(logits_read, n + 1)
                st.step(v.tensor_tensor(logits, logit[:, 0, :, :], over_i(sigmoid[:, :]), ALU.subtract))
                st.step(v.tensor_reduce(top, logits, AX.X, ALU.max))
                st.step(v.tensor_scalar(top_relu, top, 0.0, None, ALU.max))
                v.scalar_tensor_tensor(out=gate_sb[:, 10, :, :], in0=logits, scalar=0.0, in1=over_e(top_relu),
                                       op0=ALU.max, op1=ALU.subtract).then_inc(gate_arg_ready, 1)
                return st

            def gate_first(st):
                st.step(v.tensor_tensor(below, logits, over_e(top), ALU.subtract))
                st.step(v.scalar_tensor_tensor(out=ranked, in0=below, scalar=0.0, in1=over_i(rank[:, :]),
                                               op0=ALU.is_ge, op1=ALU.mult))
                st.step(v.tensor_reduce(top_rank, ranked, AX.X, ALU.max))
                st.step(v.tensor_tensor(first, ranked, over_e(top_rank), ALU.is_ge))

            def gate_second(st):
                st.step(v.scalar_tensor_tensor(out=rest, in0=first, scalar=-BIG, in1=logits,
                                               op0=ALU.mult, op1=ALU.add))
                st.step(v.tensor_reduce(second, rest, AX.X, ALU.max))
                st.step(v.tensor_tensor(below2, rest, over_e(second), ALU.subtract))
                st.step(v.scalar_tensor_tensor(out=ranked2, in0=below2, scalar=0.0, in1=over_i(rank[:, :]),
                                               op0=ALU.is_ge, op1=ALU.mult))

            def gate_active(n, st):
                st.step(v.tensor_reduce(second_rank, ranked2, AX.X, ALU.max))
                st.step(v.tensor_tensor(both, ranked2, over_e(second_rank), ALU.is_ge))
                v.tensor_scalar(idle, top, 0.0, None, ALU.is_le)
                st.step(v.tensor_tensor(both, both, first, ALU.add))
                st.step(v.tensor_tensor(fallback, both, over_e(idle), ALU.mult))
                st.step(v.scalar_tensor_tensor(out=active, in0=logits, scalar=0.0, in1=fallback,
                                               op0=ALU.is_gt, op1=ALU.add))
                dve.wait_ge(gate_exp_ready, n + 1)
                st.step(v.tensor_tensor(weight, gexp[:, :, :], active, ALU.mult))
                st.step(v.tensor_reduce(total, weight, AX.X, ALU.add))
                st.step(v.reciprocal(inv, total))
                st.end()

            def keep_weights(a):
                v.tensor_copy(rw_prev[:, :, :], rw[:, :, :]).then_inc(rw_kept, 1)

            def gate_weights(n):
                if due(n):
                    dve.wait_ge(rw_kept, n)
                if due(n):
                    dve.wait_ge(y_scaled_s, n * YN)
                v.tensor_tensor(rw[:, :, :], weight, over_e(inv), ALU.mult).then_inc(rw_ready, 1)

            def y_add(b, first, last):
                for n in range(first, last):
                    i, p = n // PAIRS, n % PAIRS
                    if p % 2:
                        continue
                    dve.wait_ge(rw_ready, b + 1)
                    dve.wait_ge(y_ready[0], b * YN // 2 + n // 2 + 1)
                    if p == 0:
                        if due((b - 1) * NT + i + 1):
                            dve.wait_ge(y_summed, (b - 1) * NT + i + 1)
                    for u in range(2):
                        e = 2 * p + u
                        y = y_view[0][:, u * W3:(u + 1) * W3]
                        if p == 0:
                            v.tensor_scalar(acc_v[:, i, u, :], y, rw[:, i, e:e + 1], None, ALU.mult)\
                             .then_inc(y_added_v, 1)
                        else:
                            if due(b * YN + n + u - 1):
                                dve.wait_ge(y_added_v, b * YN + n + u - 1)
                            v.scalar_tensor_tensor(out=acc_v[:, i, u, :], in0=y, scalar=rw[:, i, e:e + 1],
                                                   in1=acc_v[:, i, u, :], op0=ALU.mult, op1=ALU.add)\
                             .then_inc(y_added_v, 1)

            def y_finish(b, i):
                dve.wait_ge(qkv_ready, b * NT + i)
                dve.wait_ge(y_added_s, b * NT * ADDS + (i + 1) * ADDS)
                dve.wait_ge(y_added_v, (b * NT + i + 1) * PAIRS)
                v.tensor_tensor(y_sum[:, i, :, :], acc_v[:, i, :, :], acc_s[:, i, :, :], ALU.add)\
                 .then_inc(y_summed, 1)
                dve.wait_ge(y_summed, b * NT + i + 1)
                dve.wait_ge(attn_ready, b)
                dve.wait_ge(qk_tr_ready, b)
                odd, even = (y_sum[:, i, u, :].rearrange("p (n d) -> p n d", d=HD).unsqueeze(2)
                             .broadcast_to([P, 3, 2, HD]) for u in range(2))
                v.tensor_tensor(qkv[:, i, :, :, :], odd, even, ALU.add).then_inc(qkv_ready, 1)

            def values(b):
                dve.wait_ge(proj_ready, b * 3 + 3)
                if due(16 * 16 * b):
                    dve.wait_ge(v_spread, 16 * 16 * b)
                if due(b):
                    dve.wait_ge(v_low_ready, b)
                v.tensor_tensor(v_ones[:, :, :, :, 0:M].rearrange("p i s g m -> p (i s g) m"),
                                g_ps[4][:, :].rearrange("p (a m) -> p a m", m=M),
                                bv_row[:, :].unsqueeze(1).broadcast_to([P, NT, D]), ALU.add)\
                 .then_inc(v_ready, 1)

            def elu(b, first, last):
                for n in range(first, last):
                    dst, ready = ((q_t, q_ready), (k_t, k_ready))[n]
                    dve.wait_ge(elu_parts, b * 4 + 2 * n + 2)
                    if n == 0:
                        if due(b * NT):
                            dve.wait_ge(la_ready, b * NT)
                        if due(b * G):
                            dve.wait_ge(q_groups_ready, b * G)
                    else:
                        if due(b):
                            dve.wait_ge(k_tok_ready, b)
                        if due(b * S4):
                            dve.wait_ge(k_places_ready, b * S4)
                    v.scalar_tensor_tensor(out=dst[:, :], in0=elu_e[:, n, :], scalar=1.0, in1=elu_r[:, n, :],
                                           op0=ALU.min, op1=ALU.add).then_inc(ready, 1)

            def place_k(b):
                dve.wait_ge(k_ready, b + 1)
                if due(b * NT):
                    dve.wait_ge(score_ready, b * NT)
                for s in range(2):
                    v.tensor_scalar(k_places[:, :, s, :], k_t[:, :].rearrange("p (c t) -> p c t", t=C),
                                    place_mask[:, s:s + 1], None, ALU.mult).then_inc(k_places_ready, 1)

            def mask_scores(b, i):
                dve.wait_ge(score_ready, b * NT + i + 1)
                if due((b - 1) * NT + i + 1):
                    dve.wait_ge(la_ready, (b - 1) * NT + i + 1)
                v.tensor_tensor(scores[:, i, :].rearrange("p (a q) -> p a q", q=C),
                                g_ps[3 + i % 2][:, :].rearrange("p (a q) -> p a q", q=C),
                                past[:, :].unsqueeze(1).broadcast_to([P, CT * G, C]), ALU.mult)\
                 .then_inc(score_masked, 1)

            def k_low_tokens(b):
                dve.wait_ge(k_high_ready, b + 1)
                v.tensor_tensor(kv_parts[:, :, 0, 0:D], g_ps[2][:, :].rearrange("p (i f) -> p i f", f=D),
                                kv_parts[:, :, 1, 0:D], ALU.subtract).then_inc(k_low_ready, 1)

            def mask_states(b, n):
                dve.wait_ge(d_ready, b * ND + n + 1)
                if due(b * (NC - 1)):
                    dve.wait_ge(state_ready, b * (NC - 1))
                v.tensor_tensor(d_state[:, n * DB:(n + 1) * DB, :],
                                g_ps[2 + n % 2][:, 0:DB * VW].rearrange("p (a w) -> p a w", w=VW),
                                block_mask[:, :].unsqueeze(1).broadcast_to([P, DB, VW]), ALU.mult)\
                 .then_inc(d_masked, 1)

            def la_values(b, n):
                st = Chain(dve, den_step, 2, b * 2 + n)
                o = g_ps[(4, 3)[n]][:, 0:2 * VW].rearrange("p (a m) -> p a m", m=M1)
                dve.wait_ge(la_ready, b * NT + 2 * n + 2)
                if due(b):
                    dve.wait_ge(val_tr_ready, b)
                st.step(v.tensor_scalar(den[:, n, 0, :].unsqueeze(2), o[:, :, M:M1], DEN_EPS, None, ALU.add))
                st.step(v.reciprocal(den[:, n, 1, :], den[:, n, 0, :]))
                v.tensor_tensor(val[:, 2 * n:2 * n + 2, :].rearrange("p i (a m) -> p (i a) m", m=M),
                                o[:, :, 0:M], den[:, n, 1, :].unsqueeze(2).broadcast_to([P, 2 * H, M]),
                                ALU.mult).then_inc(val_ready, 1)

            def qk_low(a):
                dve.wait_ge(qk_high_ready, 2 * a + 1)
                v.tensor_tensor(q_halves[HD:P, :], g_ps[0][HD:P, :], q_halves[HD:P, :], ALU.subtract)\
                 .then_inc(qk_low_ready, 1)
                dve.wait_ge(qk_high_ready, 2 * a + 2)
                v.scalar_tensor_tensor(out=k_low[:, :], in0=g_ps[1][:, :], scalar=-SCALE, in1=k_high[:, :],
                                       op0=ALU.mult, op1=ALU.subtract).then_inc(qk_low_ready, 1)

            def row_max(a, i, alone=False):
                dve.wait_ge(s_ready, a * NT + i + 1)
                if due(a * NT):
                    dve.wait_ge(probs_ready, a * NT)
                v.tensor_reduce(neg_max[:, i:i + 1], score_banks[alone][i][:, 0:(i + 1) * P], AX.X, ALU.min)\
                 .then_inc(neg_max_ready, 1)

            def output_weights(a):
                st = Chain(dve, rwo_step, 5, a)
                dve.wait_ge(probs_ready, (a + 1) * NT)
                dve.wait_ge(rw_kept, a + 1)
                if due(a):
                    dve.wait_ge(rwo_tr_ready, a)
                st.step(v.reciprocal(srec[:, :], ssum[:, :]))
                st.step(v.tensor_tensor(rwo[:, 0, :, :], rw_prev[:, :, :], over_e(srec[:, :]), ALU.mult))
                st.step(v.tensor_copy(rwo_parts[:, :, 0:E], rwo[:, 0, :, :]))
                st.step(v.tensor_tensor(rwo[:, 1, :, :], rwo[:, 0, :, :], rwo_parts[:, :, 0:E], ALU.subtract))
                st.step(v.tensor_copy(rwo_parts[:, :, E:2 * E], rwo[:, 1, :, :]))
                v.tensor_tensor(rwo_parts[:, :, 2 * E:3 * E], rwo[:, 1, :, :], rwo_parts[:, :, E:2 * E],
                                ALU.subtract).then_inc(rwo_ready, 1)
                st.end()

            def mix(a, p, alone=False):
                dve.wait_ge(rwb_ready, a * PAIRS + p + 1)
                dve.wait_ge(attn_t_ready, a + 1)
                if due(a * PAIRS + max(p - 1, 0)):
                    dve.wait_ge(pair_added, a * PAIRS + max(p - 1, 0))
                bank = pair_banks[alone][p % len(pair_banks[alone])]
                v.tensor_tensor(mixed[:, p % 2, :], bank[:, :], attn_t[:, :], ALU.mult)\
                 .then_inc(mixed_ready, 1)

            def finish(a):
                dve.wait_ge(pair_added, (a + 1) * PAIRS)
                dve.wait_ge(res_ready, a + 1)
                if due(a * 16):
                    dve.wait_ge(out_stored, a * 16)
                v.tensor_tensor(out_sb[:, :, :], out_ps[:, :, :], res[:, :, :], ALU.add)\
                 .then_inc(out_ready, 1)

            v.memset(kv_stack[3 * C:P, :, :, :, :], 0.0)
            v.memset(kv_parts[:, :, 0:2, D:VW], 0.0)
            v.memset(rwo_parts[:, :, :], 0.0)
            row_stats(0, 0, NT)
            st = variance(0)
            dve.wait_ge(gate_loaded, 16 * 2)
            consts = Chain(dve, dve_const_step, 11, 0)
            consts.step(v.tensor_tensor(sim_sq[:, :], sim[:, :], sim[:, :], ALU.mult))
            normalise(0, st)
            norm_inverse(0, st)
            dve.wait_ge(sim_norm, 1)
            v.tensor_copy(sim_r[:, 0, :], g_ps[0][:, 0:E]).then_inc(sim_norm_read, 1)
            dve.wait_ge(gates_exp, 1)
            consts.step(v.tensor_scalar(sig[:, 1, :], sig[:, 0, :], 1.0, None, ALU.add))
            consts.step(v.reciprocal(sigmoid[:, :], sig[:, 1, :]))
            consts.step(v.memset(group_mask[:, :], 0.0))
            for n in range(G):
                last = v.memset(group_mask[C * n:C * n + C, n:n + 1], 1.0)
            last.then_inc(zeros_ready, 1)
            dve.wait_ge(lin_loaded, 16 * 6)
            by_place = "p (g s m) -> p s g m"
            v.tensor_copy(bv_row[:, :].rearrange("p (s g m) -> p s g m", g=G, m=M),
                          bv_raw[:, :].rearrange(by_place, g=G, m=M))
            consts.step(v.tensor_copy(lin_w[:, 2, :].rearrange("p (s g m) -> p s g m", g=G, m=M),
                                      wv_raw[:, :].rearrange(by_place, g=G, m=M)))
            consts.step(v.tensor_copy(lin_hi[:, :, :], lin_w[:, :, :]))
            v.tensor_tensor(lin_lo[:, :, :], lin_w[:, :, :], lin_hi[:, :, :], ALU.subtract)\
             .then_inc(lin_ready, 1)
            xt_low(0)
            xt_move(0)
            dve.wait_ge(sim_root, 1)
            consts.step(v.tensor_scalar(sim_r[:, 2, :], sim_r[:, 1, :], NORM_EPS, None, ALU.max))
            consts.step(v.reciprocal(sim_r[:, 3, :], sim_r[:, 2, :]))
            consts.step(v.tensor_tensor(sim_r[:, 0, :], sim[:, :], sim_r[:, 3, :], ALU.mult))
            consts.step(v.tensor_copy(sim_hi[:, :], sim_r[:, 0, :]))
            v.tensor_tensor(sim_lo[:, :], sim_r[:, 0, :], sim_hi[:, :], ALU.subtract).then_inc(sim_ready, 1)
            gate = gate_logits(0)
            dve.wait_ge(rank_ready, 1)
            gate_first(gate)

            def w3_low(n):
                part = slice(n * E // W3_PARTS, (n + 1) * E // W3_PARTS)
                dve.wait_ge(w3_hi_ready, n + 1)
                v.tensor_tensor(w3_lo[:, part, :], stage[:, part, :], w3_hi[:, part, :], ALU.subtract)\
                 .then_inc(w3_ready, 1)

            gate_second(gate)
            w3_low(0)
            w3_low(1)
            gate_active(0, gate)
            gate_weights(0)
            dve.wait_ge(places_ready, 1)
            consts.step(v.memset(wait_pad[:, :], 0.0))
            consts.end()

            def body(b, attn, norm):
                elu(b, 0, 1)
                y_add(b, 0, 2)
                elu(b, 1, 2)
                if isinstance(b, int) and b == 0:
                    w3_low(2)
                y_add(b, 2, 4)
                if isinstance(b, int) and b == 0:
                    w3_low(3)
                if attn:
                    qk_low(b - 1)
                values(b)
                y_add(b, 4, 6)
                if attn:
                    row_max(b - 1, 0)
                    row_max(b - 1, 1)
                k_low_tokens(b)
                y_add(b, 6, 8)
                place_k(b)
                if attn:
                    row_max(b - 1, 2)
                if attn and (not isinstance(b, int) or b > 1):
                    finish(b - 2)
                if isinstance(b, int) and b == 0:
                    dve.wait_ge(const_ready, 1)
                mask_scores(b, 0)
                y_add(b, 8, 10)
                mask_scores(b, 1)
                if attn:
                    row_max(b - 1, 3)
                y_add(b, 10, 12)
                mask_scores(b, 2)
                y_add(b, 12, 14)
                if norm:
                    row_stats(b + 1, 0, NT)
                mask_scores(b, 3)
                if norm:
                    st = variance(b + 1)
                y_add(b, 14, 16)
                mask_states(b, 0)
                mask_states(b, 1)
                if attn:
                    output_weights(b - 1)
                y_add(b, 16, 18)
                mask_states(b, 2)
                if norm:
                    normalise(b + 1, st)
                mask_states(b, 3)
                y_add(b, 18, 20)
                mask_states(b, 4)
                if norm:
                    xt_low(b + 1)
                if attn:
                    mix(b - 1, 0)
                    mix(b - 1, 1)
                y_add(b, 20, 22)
                if attn:
                    mix(b - 1, 2)
                if norm:
                    norm_inverse(b + 1, st)
                    gate = gate_logits(b + 1)
                la_values(b, 0)
                y_add(b, 22, 24)
                if norm:
                    gate_first(gate)
                if attn:
                    mix(b - 1, 3)
                y_add(b, 24, 26)
                if norm:
                    gate_second(gate)
                if attn:
                    mix(b - 1, 4)
                y_add(b, 26, 28)
                la_values(b, 1)
                if attn:
                    mix(b - 1, 5)
                y_add(b, 28, 30)
                if attn:
                    mix(b - 1, 6)
                if norm:
                    xt_move(b + 1)
                y_add(b, 30, 32)
                keep_weights(b)
                if attn:
                    mix(b - 1, 7)
                if norm:
                    gate_active(b + 1, gate)
                    gate_weights(b + 1)

            passes(body)(dve)
            a = B - 1
            y_finish(a, 2)
            y_finish(a, 3)
            finish(a - 1)
            qk_low(a)
            for i in range(NT):
                row_max(a, i, alone=True)
            output_weights(a)
            for p in range(PAIRS):
                mix(a, p, alone=True)
            finish(a)

        @block.tensor
        def _(pe):
            t_ = nc.tensor

            def product(dst, lhs, rhs, done=None, start=True):
                (lh, ll), (rh, rl) = lhs, rhs
                t_.matmul(dst, lh, rh, start=start, stop=False)
                t_.matmul(dst, lh, rl, start=False, stop=False)
                last = t_.matmul(dst, ll, rh, start=False, stop=True)
                if done is not None:
                    last.then_inc(done, 1)

            pe.wait_ge(ident_ready, 1)
            pe.wait_ge(dve_const_step, 1)
            t_.matmul(g_ps[0][:, 0:E], ones[:, :], sim_sq[:, :], start=True, stop=True).then_inc(sim_norm, 1)

            def tile(t, i):
                return t[:, i * P:(i + 1) * P]

            def xn_transpose(n):
                pe.wait_ge(xn_ready, (n + 1) * NT)
                if due(n * NT):
                    pe.wait_ge(score_masked, n * NT)
                for i in range(NT):
                    last = t_.transpose(tile(g_ps[4], i), xn[:, i, :], ident[:, :])
                last.then_inc(xt_ready, 1)

            def gate_logits(n):
                pe.wait_ge(xt_lo_ready, n + 1)
                if due(n * ND):
                    pe.wait_ge(d_masked, n * ND)
                for i in range(NT):
                    product(g_ps[2][:, i * E:(i + 1) * E], (tile(next_hi, i), tile(next_lo, i)),
                            (sim_hi[:, :], sim_lo[:, :]), logits_ready if i == NT - 1 else None)

            def y_pairs(b, first, last):
                for n in range(first, last):
                    i, p = n // PAIRS, n % PAIRS
                    if n % 2 == 0:
                        if due(b * YN + n):
                            pe.wait_ge(y_added_v, b * YN + n)
                    else:
                        if due(b * YN + n - 1):
                            pe.wait_ge(y_scaled_s, b * YN + n - 1)
                    cols = slice(2 * p, 2 * p + 2)
                    if isinstance(b, int) and b == 0 and i == 0:
                        pe.wait_ge(w3_ready, p * W3_PARTS // PAIRS + 1)
                    product(y_view[n % 2], (tile(xt_hi, i), tile(xt_lo, i)),
                            (w3_hi[:, cols, :].rearrange("p a b -> p (a b)"),
                             w3_lo[:, cols, :].rearrange("p a b -> p (a b)")), y_ready[n % 2])

            def projections(b):
                pe.wait_ge(xt_moved, b + 1)
                pe.wait_ge(logits_read, b + 1)
                if due(b):
                    pe.wait_ge(val_t_ready, b)
                for n in range(2):
                    if n == 1:
                        if due(b * 2):
                            pe.wait_ge(val_ready, b * 2)
                    product(g_ps[2 + n][:, :], (lin_hi[:, n, :], lin_lo[:, n, :]),
                            (xt_hi[:, :], xt_lo[:, :]), proj_ready)
                for i in range(NT):
                    product(tile(g_ps[4], i), (tile(xt_hi, i), tile(xt_lo, i)),
                            (lin_hi[:, 2, :], lin_lo[:, 2, :]), proj_ready if i == NT - 1 else None)

            def k_to_tokens(b):
                pe.wait_ge(k_ready, b + 1)
                pe.wait_ge(elu_parts, b * 4 + 2)
                for i in range(NT):
                    last = t_.transpose(tile(g_ps[2], i), tile(k_t, i), ident[:, :])
                last.then_inc(k_tok_ready, 1)

            def score(b, i):
                pe.wait_ge(k_places_ready, (b + 1) * S4)
                pe.wait_ge(q_groups_ready, (b + 1) * G)
                if i == 0:
                    pe.wait_ge(elu_parts, b * 4 + 4)
                elif i == 1:
                    pe.wait_ge(v_ready, b + 1)
                else:
                    if due(b * NT + i - 1):
                        pe.wait_ge(score_masked, b * NT + i - 1)
                for j in range(CT):
                    c = i * CT + j
                    last = t_.matmul(tile(g_ps[3 + i % 2], j),
                                     k_places[:, c, :, :].rearrange("p s t -> p (s t)"),
                                     q_groups[:, c, :, :].rearrange("p g t -> p (g t)"), start=True, stop=True)
                last.then_inc(score_ready, 1)

            def chunk_states(b, n):
                if n == 0:
                    pe.wait_ge(k_low_ready, b + 1)
                    pe.wait_ge(kv_stacked, (b + 1) * STACKS)
                elif n == 1:
                    pe.wait_ge(score_masked, b * NT + 3)
                else:
                    if due(b * ND + n - 1):
                        pe.wait_ge(d_masked, b * ND + n - 1)
                for m in range(DB):
                    c = n * DB + m
                    i, j = c // CT, c % CT
                    last = t_.matmul(g_ps[2 + n % 2][:, m * VW:(m + 1) * VW], kv_stack[:, j, i, 0, 0:D],
                                     kv_stack[:, j, i, 1, :], start=True, stop=True)
                last.then_inc(d_ready, 1)

            def la_tile(b, i, norm):
                pe.wait_ge(v_spread, 16 * 16 * (b + 1))
                pe.wait_ge(state_ready, b * (NC - 1) + min(i * CT + CT - 1, NC - 1))
                if i == 0:
                    pe.wait_ge(score_masked, (b + 1) * NT)
                    if norm:
                        pe.wait_ge(xt_lo_ready, b + 2)
                if i == 2:
                    pe.wait_ge(d_masked, b * ND + 4)
                bank = g_ps[(4, 3)[i // 2]]
                o = bank[:, (i % 2) * VW:(i % 2 + 1) * VW]
                for j in range(CT):
                    c = i * CT + j
                    t_.matmul(o[C * j:C * j + C, :], q_t[:, c * C:(c + 1) * C],
                              state[:, c, :].rearrange("p (s g m) -> p g s m", s=S4, g=G),
                              start=True, stop=False, skip_group_check=True)
                for g in range(G):
                    for j in range(CT):
                        c = i * CT + j
                        last = t_.matmul(o[C * j:C * j + C, g * S4 * M1:(g + 1) * S4 * M1],
                                         scores[:, i, (j * G + g) * C:(j * G + g + 1) * C],
                                         v_blocks[:, c, :, g, :], start=False, stop=(g == G - 1),
                                         skip_group_check=True)
                last.then_inc(la_ready, 1)

            def val_transpose(b, norm):
                pe.wait_ge(val_ready, (b + 1) * 2)
                pe.wait_ge(d_masked, (b + 1) * ND)
                if norm:
                    pe.wait_ge(logits_read, b + 2)
                for i in range(NT):
                    last = t_.transpose(tile(g_ps[2], i), val[:, i, :], ident[:, :])
                last.then_inc(val_tr_ready, 1)

            def start_output(a):
                pe.wait_ge(val_t_ready, a + 1)
                if due(a):
                    pe.wait_ge(out_ready, a)
                for i in range(NT):
                    last = t_.matmul(out_ps[:, i, :], tile(val_t, i), wo[:, :], start=(i == 0), stop=False,
                                     skip_group_check=True)
                last.then_inc(wo_added, 1)

            def qk_transpose(a):
                if due(a * PAIRS):
                    pe.wait_ge(mixed_ready, a * PAIRS)
                for i in range(NT):
                    pe.wait_ge(qkv_ready, a * NT + i + 1)
                    for n in range(2):
                        last = t_.transpose(tile(g_ps[n], i), qkv[:, i, n, :, :].rearrange("p u d -> p (u d)"),
                                            ident[:, :])
                last.then_inc(qk_tr_ready, 1)

            def soft_scores(a, i, alone=False):
                pe.wait_ge(qk_low_ready, 2 * a + 2)
                if alone:
                    pe.wait_ge(val_t_ready, B)
                    pe.wait_ge(val_ready, B * 2)
                    pe.wait_ge(y_added_v, B * YN)
                elif i >= 2:
                    if due(a * NT + i - 1):
                        pe.wait_ge(probs_ready, a * NT + i - 1)
                n = (i + 1) * P
                s = score_banks[alone][i]
                for k in (k_high, k_low):
                    t_.matmul(s[:, 0:n], tile(q_halves, i), k[:, 0:n], start=(k is k_high), stop=False,
                              skip_group_check=True)
                t_.matmul(s[:, n - P:n], ident_bf[:, :], future_bf[:, :], start=False, stop=True,
                          skip_group_check=True).then_inc(s_ready, 1)

            def probs_transpose(a, i, alone=False):
                pe.wait_ge(probs_ready, a * NT + i + 1)
                if not alone and i < 2:
                    pe.wait_ge(probs_ready, a * NT + i + 3)
                elif not alone:
                    if due(a * NT + i - 1):
                        pe.wait_ge(probs_t_ready, a * NT + i - 1)
                for k in range(i + 1):
                    last = t_.transpose(tile(score_banks[alone][i], k), probs[:, i, k * P:(k + 1) * P], ident[:, :])
                last.then_inc(probs_tr_ready, 1)

            def attend(a, alone=False):
                if alone:
                    pe.wait_ge(y_scaled_s, B * YN)
                pe.wait_ge(probs_t_ready, (a + 1) * NT)
                for k in range(NT):
                    last = t_.matmul(attn_banks[alone][:, k * P:T], qkv[:, k, 2, :, :].rearrange("p u d -> p (u d)"),
                                     probs_t[:, k, k * P:T], start=(k == 0), stop=(k == NT - 1),
                                     skip_group_check=True)
                last.then_inc(attn_ready, 1)

            def weights_transpose(a):
                pe.wait_ge(rwo_ready, a + 1)
                for i in range(NT):
                    last = t_.transpose(g_ps[1].bitcast(BF16)[:, i * P:(i + 1) * P], rwo_parts[:, i, :],
                                        ident_bf[:, :])
                last.then_inc(rwo_tr_ready, 1)

            def spread_weights(a, p, alone=False):
                banks = pair_banks[alone]
                pe.wait_ge(rwo_t_ready, a + 1)
                if alone:
                    pe.wait_ge(probs_t_ready, (a + 1) * NT)
                    if p >= len(banks):
                        pe.wait_ge(mixed_ready, a * PAIRS + p - len(banks) + 1)
                elif p < 2:
                    pe.wait_ge(attn_t_ready, a + 1)
                else:
                    if due(a * PAIRS + p - 1):
                        pe.wait_ge(mixed_ready, a * PAIRS + p - 1)
                t_.matmul(banks[p % len(banks)][:, :], pair_sel[:, p, :, :].rearrange("p u d -> p (u d)"),
                          rwo_t[:, :], start=True, stop=True).then_inc(rwb_ready, 1)

            def add_pair(a, p):
                pe.wait_ge(mixed_ready, a * PAIRS + p + 1)
                for i in range(NT):
                    last = t_.matmul(out_ps[:, i, :], mixed[:, p % 2, i * P:(i + 1) * P], eo[:, p, :],
                                     start=False, stop=(p == PAIRS - 1 and i == NT - 1),
                                     skip_group_check=True)
                last.then_inc(pair_added, 1)

            def output_pair(a, p, alone=False):
                add_pair(a, p)
                ahead = len(pair_banks[alone])
                if p + ahead < PAIRS:
                    spread_weights(a, p + ahead, alone)

            xn_transpose(0)
            pe.wait_ge(sim_ready, 1)
            gate_logits(0)
            pe.wait_ge(lin_ready, 1)

            def body(b, attn, norm):
                projections(b)
                if isinstance(b, int) and b == 1:
                    pe.wait_ge(const_ready, 1)
                    pe.wait_ge(const_step, 19)
                y_pairs(b, 0, 2)
                if attn and (not isinstance(b, int) or b > 1):
                    output_pair(b - 2, 6)
                if attn:
                    qk_transpose(b - 1)
                y_pairs(b, 2, 4)
                k_to_tokens(b)
                if attn and (not isinstance(b, int) or b > 1):
                    output_pair(b - 2, 7)
                y_pairs(b, 4, 6)
                if attn:
                    soft_scores(b - 1, 0)
                    soft_scores(b - 1, 1)
                y_pairs(b, 6, 8)
                if attn:
                    soft_scores(b - 1, 2)
                y_pairs(b, 8, 10)
                score(b, 0)
                score(b, 1)
                if attn:
                    soft_scores(b - 1, 3)
                y_pairs(b, 10, 12)
                score(b, 2)
                if attn:
                    probs_transpose(b - 1, 0)
                y_pairs(b, 12, 14)
                score(b, 3)
                if attn:
                    start_output(b - 1)
                    probs_transpose(b - 1, 1)
                    probs_transpose(b - 1, 2)
                y_pairs(b, 14, 16)
                if attn:
                    probs_transpose(b - 1, 3)
                if attn:
                    chunk_states(b, 0)
                    chunk_states(b, 1)
                y_pairs(b, 16, 18)
                if not attn:
                    chunk_states(b, 0)
                    chunk_states(b, 1)
                chunk_states(b, 2)
                chunk_states(b, 3)
                if attn:
                    attend(b - 1)
                    weights_transpose(b - 1)
                chunk_states(b, 4)
                y_pairs(b, 18, 20)
                if norm:
                    xn_transpose(b + 1)
                if attn:
                    spread_weights(b - 1, 0)
                    spread_weights(b - 1, 1)
                y_pairs(b, 20, 22)
                la_tile(b, 0, norm)
                if attn:
                    output_pair(b - 1, 0)
                if norm:
                    gate_logits(b + 1)
                la_tile(b, 1, norm)
                y_pairs(b, 22, 24)
                la_tile(b, 2, norm)
                if attn:
                    output_pair(b - 1, 1)
                y_pairs(b, 24, 26)
                la_tile(b, 3, norm)
                if attn:
                    output_pair(b - 1, 2)
                y_pairs(b, 26, 28)
                if attn:
                    output_pair(b - 1, 3)
                y_pairs(b, 28, 30)
                if attn:
                    output_pair(b - 1, 4)
                val_transpose(b, norm)
                y_pairs(b, 30, 32)
                if attn:
                    output_pair(b - 1, 5)

            passes(body)(pe)
            a = B - 1
            output_pair(a - 1, 6)
            output_pair(a - 1, 7)
            qk_transpose(a)
            start_output(a)
            for i in range(NT):
                soft_scores(a, i, alone=True)
            for i in range(NT):
                probs_transpose(a, i, alone=True)
            weights_transpose(a)
            attend(a, alone=True)
            for p in range(len(pair_banks[True])):
                spread_weights(a, p, alone=True)
            for p in range(PAIRS):
                output_pair(a, p, alone=True)


_INS = ["L0_attn_x", "L0_attn_Wq", "L0_attn_bq", "L0_attn_Wk", "L0_attn_bk", "L0_attn_Wv", "L0_attn_bv",
        "L0_attn_Wo", "L0_attn_bo", "L0_ffn_sim_matrix", "L0_ffn_gates", "L0_ffn_q_proj", "L0_ffn_k_proj",
        "L0_ffn_v_proj", "L0_ffn_o_proj"]


def kernel(**inputs):
    import numpy as _np
    import concourse.bacc as _bacc
    from concourse import mybir as _mybir
    from concourse.bass_utils import run_bass_kernel_spmd as _run

    nc = _bacc.Bacc("TRN2", target_bir_lowering=False, num_devices=1)
    arrays, args = {}, []
    for name in _INS:
        a = _np.ascontiguousarray(inputs[name])
        arrays[name] = a
        args.append(nc.dram_tensor(name, a.shape, _mybir.dt.from_np(a.dtype), kind="ExternalInput").ap())
    shape = inputs["L0_attn_x"].shape
    args.append(nc.dram_tensor("out", shape, _mybir.dt.float32, kind="ExternalOutput").ap())
    build(nc, *args)
    r = _run(nc, [arrays], core_ids=[0])
    return r.results[0]["out"]
```
